# Optimizing a Trainium2 kernel written in Bass

```python
import numpy as np
import jax
import jax.numpy as jnp

def _softmax(x, axis=-1):
    return jax.nn.softmax(x, axis=axis)

def _gelu(x):
    return jax.nn.gelu(x, approximate=True)

def _silu(x):
    return jax.nn.silu(x)

def _sigmoid(x):
    return jax.nn.sigmoid(x)

def _layernorm(x, axis=-1, eps=1e-05):
    m = jnp.mean(x, axis=axis, keepdims=True)
    v = jnp.var(x, axis=axis, keepdims=True)
    return (x - m) / jnp.sqrt(v + eps)

def _scatter_add(tgt, idx, src, axis=0):
    return tgt.at[idx].add(src)

def _segment_sum(src, seg, n):
    return jax.ops.segment_sum(src, seg, n)
kernel_name = 'mk_cond_resid_d4_seqx_r8_10d49c'

def setup_inputs(seed: int=0):
    np.random.seed(seed)
    _w = jnp.asarray

    def _rec_inputs():
        import jax
        import jax.numpy as jnp
        _rk = jax.random.key(seed)
        x = 7.22e-05 + 1 * jax.random.normal(jax.random.fold_in(_rk, 1), (128, 32, 128), jnp.float32)
        _lenS = 32 - jax.random.randint(jax.random.fold_in(_rk, 7), (128,), 0, max(1, 32 // 4) + 1, jnp.int32)
        _lenS2 = 32 - jax.random.randint(jax.random.fold_in(_rk, 8), (128,), 0, max(1, 32 // 4) + 1, jnp.int32)
        cond_8 = -0.104238 + 1.01173 * jax.random.normal(jax.random.fold_in(_rk, 11), (128, 8), jnp.float32)
        return (x, cond_8)
    x, cond_8 = _rec_inputs()

    def _L0_cond_setup():
        import jax, jax.numpy as jnp
        import numpy as np
        TOP_K = 2
        NUM_MOE_LAYERS = 12

        def _gemma_mlp(x, gate_w, up_w, down_w):
            g = jnp.einsum('bsh,hi->bsi', x, gate_w)
            u = jnp.einsum('bsh,hi->bsi', x, up_w)
            return jnp.einsum('bsi,ih->bsh', jax.nn.gelu(g, approximate=True) * u, down_w)
        key = jax.random.key(seed)
        ks = jax.random.split(key, 8)
        B, S, H, I, E = (32, 32, 128, 512, 8)
        std = 0.02
        return {'x': jax.random.normal(ks[0], (B, S, H), jnp.float32), 'router_logits': jax.random.normal(ks[1], (B, E), jnp.float32), 'skill_gate': jax.random.normal(ks[2], (E, H, I), jnp.float32) * std, 'skill_up': jax.random.normal(ks[3], (E, H, I), jnp.float32) * std, 'skill_down': jax.random.normal(ks[4], (E, I, H), jnp.float32) * std, 'shared_gate': jax.random.normal(ks[5], (H, I), jnp.float32) * std, 'shared_up': jax.random.normal(ks[6], (H, I), jnp.float32) * std, 'shared_down': jax.random.normal(ks[7], (I, H), jnp.float32) * std}
    _L0_cond_all = _L0_cond_setup()
    _L0_cond_in = {k: v for k, v in _L0_cond_all.items() if k in ('skill_gate', 'skill_up', 'skill_down', 'shared_gate', 'shared_up', 'shared_down')}
    del _L0_cond_all

    def _L1_cond_setup():
        import jax, jax.numpy as jnp
        import numpy as np
        R = 16
        ALPHA = 32.0
        SCALING = ALPHA / R
        key = jax.random.key(seed)
        ks = jax.random.split(key, 6)
        B, T, C, O, E = (16, 1500, 128, 128, 8)
        x = jax.random.normal(ks[0], (B, T, C), dtype=jnp.float32)
        w = jax.random.uniform(ks[1], (B, E), dtype=jnp.float32)
        W_base = jax.random.normal(ks[2], (O, C), dtype=jnp.float32) * 0.02
        b_base = jax.random.normal(ks[3], (O,), dtype=jnp.float32) * 0.02
        As = jax.random.normal(ks[4], (E, R, C), dtype=jnp.float32) * 0.02
        Bs = jax.random.normal(ks[5], (E, O, R), dtype=jnp.float32) * 0.02
        return {'x': x, 'w': w, 'W_base': W_base, 'b_base': b_base, 'As': As, 'Bs': Bs}
    _L1_cond_all = _L1_cond_setup()
    _L1_cond_in = {k: v for k, v in _L1_cond_all.items() if k in ('W_base', 'b_base', 'As', 'Bs')}
    del _L1_cond_all

    def _L2_cond_setup():
        import jax, jax.numpy as jnp
        import numpy as np
        key = jax.random.key(seed)
        k1, k2, k3, k4, k5 = jax.random.split(key, 5)
        B, N, T, O, G = (32, 32, 128, 128, 8)
        x = jax.random.normal(k1, (B, N, T), dtype=jnp.float32)
        y = jax.random.uniform(k2, (B, G), dtype=jnp.float32)
        weight = jax.random.normal(k3, (G, O, T), dtype=jnp.float32) * (1.0 / np.sqrt(T))
        mask = jax.random.uniform(k4, (O, T), dtype=jnp.float32)
        bias = jax.random.normal(k5, (O,), dtype=jnp.float32)
        return {'x': x, 'y': y, 'weight': weight, 'mask': mask, 'bias': bias}
    _L2_cond_all = _L2_cond_setup()
    _L2_cond_in = {k: v for k, v in _L2_cond_all.items() if k in ('weight', 'mask', 'bias')}
    del _L2_cond_all

    def _L3_cond_setup():
        import jax, jax.numpy as jnp
        import numpy as np
        B, S, D = (16, 256, 128)
        E, H = (8, 256)
        key = jax.random.key(seed)
        ks = jax.random.split(key, 8)
        scale = 0.02
        x = jax.random.normal(ks[0], (B, S, D), dtype=jnp.float32)
        opcode_onehot = jax.random.uniform(ks[1], (B, E), dtype=jnp.float32)
        W_up = jax.random.normal(ks[2], (E, H, D), dtype=jnp.float32) * scale
        b_up = jnp.zeros((E, H), dtype=jnp.float32)
        W_gate = jax.random.normal(ks[3], (E, H, D), dtype=jnp.float32) * scale
        b_gate = jnp.zeros((E, H), dtype=jnp.float32)
        W_down = jax.random.normal(ks[4], (E, D, H), dtype=jnp.float32) * scale
        b_down = jnp.zeros((E, D), dtype=jnp.float32)
        return {'x': x, 'opcode_onehot': opcode_onehot, 'W_up': W_up, 'b_up': b_up, 'W_gate': W_gate, 'b_gate': b_gate, 'W_down': W_down, 'b_down': b_down}
    _L3_cond_all = _L3_cond_setup()
    _L3_cond_in = {k: v for k, v in _L3_cond_all.items() if k in ('W_up', 'b_up', 'W_gate', 'b_gate', 'W_down', 'b_down')}
    del _L3_cond_all
    return {'x': x, 'cond_8': cond_8, 'L0_cond_skill_gate': _L0_cond_in['skill_gate'], 'L0_cond_skill_up': _L0_cond_in['skill_up'], 'L0_cond_skill_down': _L0_cond_in['skill_down'], 'L0_cond_shared_gate': _L0_cond_in['shared_gate'], 'L0_cond_shared_up': _L0_cond_in['shared_up'], 'L0_cond_shared_down': _L0_cond_in['shared_down'], 'L1_cond_W_base': _L1_cond_in['W_base'], 'L1_cond_b_base': _L1_cond_in['b_base'], 'L1_cond_As': _L1_cond_in['As'], 'L1_cond_Bs': _L1_cond_in['Bs'], 'L2_cond_weight': _L2_cond_in['weight'], 'L2_cond_mask': _L2_cond_in['mask'], 'L2_cond_bias': _L2_cond_in['bias'], 'L3_cond_W_up': _L3_cond_in['W_up'], 'L3_cond_b_up': _L3_cond_in['b_up'], 'L3_cond_W_gate': _L3_cond_in['W_gate'], 'L3_cond_b_gate': _L3_cond_in['b_gate'], 'L3_cond_W_down': _L3_cond_in['W_down'], 'L3_cond_b_down': _L3_cond_in['b_down']}

def reference(x, cond_8, L0_cond_skill_gate, L0_cond_skill_up, L0_cond_skill_down, L0_cond_shared_gate, L0_cond_shared_up, L0_cond_shared_down, L1_cond_W_base, L1_cond_b_base, L1_cond_As, L1_cond_Bs, L2_cond_weight, L2_cond_mask, L2_cond_bias, L3_cond_W_up, L3_cond_b_up, L3_cond_W_gate, L3_cond_b_gate, L3_cond_W_down, L3_cond_b_down):
    import jax
    import jax.numpy as jnp

    def _L0_cond_ref(x, router_logits, skill_gate, skill_up, skill_down, shared_gate, shared_up, shared_down):
        import jax, jax.numpy as jnp
        import numpy as np
        TOP_K = 2
        NUM_MOE_LAYERS = 12

        def _gemma_mlp(x, gate_w, up_w, down_w):
            g = jnp.einsum('bsh,hi->bsi', x, gate_w)
            u = jnp.einsum('bsh,hi->bsi', x, up_w)
            return jnp.einsum('bsi,ih->bsh', jax.nn.gelu(g, approximate=True) * u, down_w)
        B = x.shape[0]
        E = skill_gate.shape[0]
        rw = jax.nn.softmax(router_logits.astype(jnp.float32), axis=-1)
        w, sel = jax.lax.top_k(rw, TOP_K)
        w = w / w.sum(axis=-1, keepdims=True)
        w = w.astype(x.dtype)
        scale = 1.0 / NUM_MOE_LAYERS
        w = scale * w + (1.0 - scale) * jax.lax.stop_gradient(w)
        dense_w = jnp.zeros((B, E), x.dtype).at[jnp.arange(B)[:, None], sel].add(w)

        def step(acc, params):
            g, u, d, we = params
            return (acc + we[:, None, None] * _gemma_mlp(x, g, u, d), None)
        out, _ = jax.lax.scan(step, jnp.zeros_like(x), (skill_gate, skill_up, skill_down, dense_w.T))
        out = out + _gemma_mlp(x, shared_gate, shared_up, shared_down)
        return out

    def _L1_cond_ref(x, w, W_base, b_base, As, Bs):
        import jax, jax.numpy as jnp
        import numpy as np
        R = 16
        ALPHA = 32.0
        SCALING = ALPHA / R
        out = jnp.einsum('btc,oc->bto', x, W_base) + b_base
        h = jnp.einsum('btc,erc->bter', x, As)
        lora = jnp.einsum('bter,eor,be->bto', h, Bs, w)
        return out + lora * SCALING

    def _L2_cond_ref(x, y, weight, mask, bias):
        import jax, jax.numpy as jnp
        import numpy as np
        masked_w = weight * mask[None, :, :]
        w_bot = jnp.einsum('bg,got->bot', y, masked_w)
        return jnp.einsum('bnt,bot->bno', x, w_bot) + bias

    def _L3_cond_ref(x, opcode_onehot, W_up, b_up, W_gate, b_gate, W_down, b_down):
        import jax, jax.numpy as jnp
        import numpy as np
        B, S, D = (16, 256, 128)
        E, H = (8, 256)
        expert = jnp.argmax(opcode_onehot, axis=-1)
        wu, bu = (W_up[expert], b_up[expert])
        wg, bg = (W_gate[expert], b_gate[expert])
        wd, bd = (W_down[expert], b_down[expert])
        up = jnp.einsum('bsd,bhd->bsh', x, wu) + bu[:, None, :]
        gate = jnp.einsum('bsd,bhd->bsh', x, wg) + bg[:, None, :]
        hidden = jax.nn.silu(up) * gate
        out = jnp.einsum('bsh,bdh->bsd', hidden, wd) + bd[:, None, :]
        return out
    x = x + _L0_cond_ref(x, cond_8, L0_cond_skill_gate, L0_cond_skill_up, L0_cond_skill_down, L0_cond_shared_gate, L0_cond_shared_up, L0_cond_shared_down)
    x = x + _L1_cond_ref(x, cond_8, L1_cond_W_base, L1_cond_b_base, L1_cond_As, L1_cond_Bs)
    x = x + _L2_cond_ref(x, cond_8, L2_cond_weight, L2_cond_mask, L2_cond_bias)
    x = x + _L3_cond_ref(x, cond_8, L3_cond_W_up, L3_cond_b_up, L3_cond_W_gate, L3_cond_b_gate, L3_cond_W_down, L3_cond_b_down)
    return x

_drawn_inputs = setup_inputs


def setup_inputs(seed=0):
    import zlib

    import numpy as np

    out = dict(_drawn_inputs(seed))
    spreads = {'L3_cond_b_up': (0.0, 0.8), 'L3_cond_b_gate': (0.0, 0.8), 'L3_cond_b_down': (0.0, 2.0)}
    factors = {'L0_cond_skill_gate': 7.062,
     'L0_cond_skill_up': 7.011,
     'L0_cond_skill_down': 6.989,
     'L0_cond_shared_gate': 5.311,
     'L0_cond_shared_up': 5.221,
     'L0_cond_shared_down': 5.211,
     'L1_cond_b_base': 10.36,
     'L3_cond_W_up': 2.813,
     'L3_cond_W_gate': 2.747,
     'L3_cond_W_down': 2.717}
    for name, (base, spread) in spreads.items():
        noise = np.random.default_rng([zlib.crc32(name.encode()), seed]).standard_normal(out[name].shape)
        drawn = base * np.exp(spread * noise) if base else spread * noise
        out[name] = jnp.asarray(drawn.astype(out[name].dtype))
    for name, factor in factors.items():
        out[name] = (out[name] * factor).astype(out[name].dtype)
    return out
```

```python
from contextlib import ExitStack

import numpy as np

import concourse.bass as bass
from concourse import mybir

ALU = mybir.AluOpType
ACT = mybir.ActivationFunctionType
AX_X = mybir.AxisListType.X
F32 = mybir.dt.float32
F32R = mybir.dt.float32r
BF16 = mybir.dt.bfloat16
I32 = mybir.dt.int32
POOL = (mybir.EngineType.Pool,)
PE = (mybir.EngineType.PE,)
SP = (mybir.EngineType.SP,)

P = 128
B, S, F = 128, 32, 128
E, I0, I3, R = 8, 512, 256, 16
TOPK, LAYERS = 2, 12
TB = P // S
TB_SHIFT = TB.bit_length() - 1
T0 = (B * TOPK + E * (TB - 1)) // TB
T3 = (B + E * (TB - 1)) // TB
N0, N3 = T0 * TB, T3 * TB
G = 16
NG = B // G
W0 = 3 * I0
W3 = 3 * I3
B3 = 2 * I3 + F
ZC = 4
SC = S // ZC
LOADC = 4
CREDIT = 2

C_ID, C_U, C_ONE, C_B = 0, 128, 256, 384
C_DESC = 385
C_IOTA = C_DESC + E
C_T4 = C_IOTA + N0
C_ZC = C_T4 + 72
C_HI, C_LO = C_ZC + ZC, C_ZC + ZC + 1
C_END = C_LO + 1


def finished(n):
    return n + 1 + CREDIT


def reusable(n):
    return n + 1


def constants():
    c = np.zeros((P, C_END), np.float32)
    p = np.arange(P)
    c[:, C_ID:C_ID + P] = np.eye(P)
    c[:, C_U:C_U + P] = p[:, None] < p[None, :]
    c[:, C_ONE:C_ONE + P] = 1
    c[:, C_B] = p
    c[:, C_DESC:C_DESC + E] = E - np.arange(E)
    c[:, C_IOTA:C_IOTA + N0] = np.arange(N0)
    c[:, C_T4:C_T4 + 72] = TB * np.arange(72)
    c[:, C_ZC:C_ZC + ZC] = np.arange(ZC)
    c[:, C_LO] = (p % 32) // 8 == 2
    c[:, C_HI] = 1 - c[:, C_LO]
    return c


def build(nc, consts_d, cond_d, xt_d, xn_d, w0_d, w1_d, cond_er_d, b1_d, w2_d, mask_d, condt_d, b2_d, w3_d, b3_d, out_d):
    z_d = nc.dram_tensor("layer0_slots", (N0 * S, F), F32, kind="Internal").ap()

    w2_split = nc.dram_tensor("layer2_weights_split", (2, P, E, F), F32, kind="Internal").ap()
    b3_split = nc.dram_tensor("layer3_bias_split", (2, P, E * B3 // P), F32, kind="Internal").ap()

    with ExitStack() as ctx:
        def sb(name, shape, dt=F32):
            return ctx.enter_context(nc.sbuf_tensor(name, shape, dt))

        def sem(name):
            return ctx.enter_context(nc.semaphore(name))

        SIZE_A, SIZE_B, SIZE_C, SIZE_D, SIZE_W = 98304, 32768, 16384, 24576, 24576
        SIZE_ALL = SIZE_A + SIZE_B + SIZE_C + SIZE_D + SIZE_W
        sb("arena", [P, SIZE_ALL // 4])
        A = nc.sbuf_base - SIZE_ALL
        RB = A + SIZE_A
        RC = RB + SIZE_B
        RD = RC + SIZE_C
        RW = RD + SIZE_D

        def at(name, offset, shape, dt=F32):
            return nc.alloc_sbuf_tensor_at(name, shape, dt, offset=offset)

        wx = at("expert_weights", A, [P, E, 2, W0], F32R)
        xt = at("x_hi_lo", RB, [P, B, 2, S], F32R)
        xraw = at("x_raw", RC, [P, B, S])
        res = at("residual", RC, [P, B, S])
        ws = at("shared_weights", RD, [P, 2, W0], F32R)
        stage = at("weight_stage", RD + 12288, [P, 2, W0])
        gt = at("gelu_out", RW, [P, 2, 512])
        h = at("hidden", RW + 4096, [P, 2, 512])
        hh = at("hidden_hi", RW + 8192, [P, 2, 512], F32R)
        hl = at("hidden_lo", RW + 12288, [P, 2, 512], F32R)
        xs = at("tile_x", RW + 16384, [P, 2, 2, TB, S], F32R)
        ysb = at("tile_out", RW + 18432, [P, 2, 2, F])
        cmp_t = at("tile_compare", RW + 20480, [P, E, 72])
        sel0 = at("slot_onehot0", RW + 22784, [P, N0], BF16)
        sel3 = at("slot_onehot3", RW + 23360, [P, N3], BF16)
        before3 = at("slot_before3", RW + 23680, [P, N3], BF16)
        wstk = at("w2_stack", A, [P, S, F], F32R)
        wbot = [at("w_bot0", A + 16384, [P, B // 2, F]), at("w_bot1", RB, [P, B // 2, F])]
        gath = at("gathered", RB, [P, 2, 2, SC * F])
        xn = at("x_batch", RB + 16384, [P, 2, SC * F])
        w2raw = at("w2_raw", RD, [P, E, F])
        w2h = at("w2_hi", RD + 4096, [P, E, F], F32R)
        w2l = at("w2_lo", RD + 8192, [P, E, F], F32R)
        mask = at("mask", RD + 12288, [P, F])
        w1raw = at("w1_raw", RD + 12800, [P, 3 * F])
        er_raw = at("cond_er_raw", RD + 14336, [P, B])
        yraw = at("cond_t_raw", RD + 14848, [P, B])
        yh = at("cond_t_hi", RD + 15360, [P, B], F32R)
        yl = at("cond_t_lo", RD + 15872, [P, B], F32R)
        ysel = at("cond_t_sel", RD + 16384, [P, B])
        b3raw = at("b3_raw", RD + 16896, [P, E * B3 // P])
        b3h = at("b3_hi", RD + 17408, [P, E * B3 // P], F32R)
        b3l = at("b3_lo", RD + 17920, [P, E * B3 // P], F32R)
        x1 = at("x1", RW, [P, 3, 512])
        x1h = at("x1_hi", RW + 6144, [P, 3, 512], F32R)
        x1l = at("x1_lo", RW + 12288, [P, 3, 512], F32R)
        hsh = at("adapter_hi", RW + 18432, [P, 2, 512], F32R)
        hsl = at("adapter_lo", RD + 18432, [P, 2, 512], F32R)
        w3raw = at("w3_raw", RB + 24576, [P, 2, W3])
        hs = at("adapter_h", RB + 30720, [P, 512])
        w3 = at("w3_hi_lo", A + 49152, [P, E, 2, W3], F32R)
        x3t = at("x3_hi_lo", A, [P, B, 2, S], F32R)
        b3 = at("b3_rows", RD, [2, E, B3], F32R)
        st = at("silu_out", RW, [P, 2, I3])
        h3 = at("hidden3", RW + 2048, [P, 2, I3])
        h3h = at("hidden3_hi", RW + 4096, [P, 2, I3], F32R)
        h3l = at("hidden3_lo", RW + 6144, [P, 2, I3], F32R)
        xs3 = at("tile_x3", RW + 8192, [P, 2, 2, TB, S], F32R)
        osb = at("tile_out3", RW + 10240, [P, 2, 2, F])

        kc = sb("constants", [P, C_END])
        kb = sb("constants_bf16", [P, 257], BF16)
        ident = kc[:, C_ID:C_ID + P]
        before = kb[:, 0:P]
        ones = kb[:, P:2 * P]
        batch = kb[:, 2 * P:2 * P + 1]
        ident_r = sb("identity_r", [P, P], F32R)
        ones_r = sb("ones_r", [2, P], F32R)
        cond = sb("cond", [P, E])
        rt = sb("route_scratch", [P, 24, E])
        oh = sb("onehots", [P, 2, E])
        pair = sb("pairs_bf16", [P, 2 * E], BF16)
        rc = sb("rank_count", [P, 4 * E])
        scan = sb("scan", [P, 2, 2, 2 * E])
        up4 = sb("rounded_up", [P, 2, E], I32)
        slot = sb("slot", [P, 2, E])
        prod = sb("prod", [P, 3, E])
        pos = sb("pos", [P, 3])
        idx = sb("gather_rows", [P, ZC, 2], I32)
        rw = sb("rw", [P, 2])
        wt = sb("top_weights", [P, 2])
        sc = sb("scalars", [P, 8])
        batch0 = sb("slot_batch0", [1, N0], I32)
        batch3 = sb("slot_batch3", [1, N3], I32)
        expert0 = sb("tile_expert0", [1, 72], I32)
        expert3 = sb("tile_expert3", [1, 40], I32)
        row3 = sb("slot_row3", [1, N3], I32)
        tmp3 = sb("slot_tmp3", [1, 2, N3])
        w1 = sb("w1_hi_lo", [P, 2, 3 * F], F32R)
        er = sb("cond_er", [P, B])
        ystk = sb("cond_stack", [P, B], F32R)
        b1 = sb("b1", [P, 1])
        b2 = sb("b2", [P, 1])

        ps = ctx.enter_context(nc.psum_tensor("ps", [P, 8, 512], F32))

        def bank(n, width=512):
            return ps[:, n, 0:width]

        def dbank(n):
            return ps[:, bass.ds(n, 1), 0:F].rearrange("p a n -> p (a n)")

        ld_c = sem("ld_constants")
        ld_x = [sem(f"ld_x{i}") for i in range(LOADC)]
        ld_w = [sem(f"ld_stage{i}") for i in range(2)]
        stage_free = sem("stage_free")
        ld_late = sem("ld_late")
        ld_xn = [sem(f"ld_xn{i}") for i in range(2)]
        ld_g = [sem(f"ld_gather{i}") for i in range(2)]
        ld_w3 = [sem(f"ld_w3{i}") for i in range(2)]
        route = sem("route_step")
        exp_done = sem("exp_done")
        max_done = sem("max_done")
        pair_done = sem("pair_done")
        rank_done = sem("rank_done")
        sel_done = sem("sel_done")
        slots_done = sem("slots_done")
        tables = sem("tables_done")
        consts_done = sem("consts_done")
        x_hi = sem("x_hi")
        x_lo = sem("x_lo")
        ws_hi = sem("ws_hi")
        ws_lo = sem("ws_lo")
        wx_hi = sem("wx_hi")
        wx_lo = sem("wx_lo")
        sh_gate, sh_up, sh_gelu, sh_mul, sh_hi, sh_lo, sh_down, sh_out = (
            sem("sh_" + n) for n in ("gate", "up", "gelu", "mul", "hi", "lo", "down", "out"))
        (m_xs, m_gate, m_up, m_gelu, m_mul, m_turn, m_hi, m_lo, m_down, m_out) = (
            sem("moe_" + n) for n in ("xs", "gate", "up", "gelu", "mul", "turn", "hi", "lo", "down", "out"))
        z_done = sem("z_stored")
        z_free = sem("z_free")
        w2_masked, w2_hi, w2_lo, w2_split_done, w2_stack = (sem("w2_" + n) for n in ("masked", "hi", "lo", "split", "stack"))
        w1_hi, w1_lo = sem("w1_hi"), sem("w1_lo")
        y_hi, y_lo, y_sel, y_stk = (sem("y_" + n) for n in ("hi", "lo", "sel", "stack"))
        gen_mm, gen_act, gen_dve = sem("gen_mm"), sem("gen_act"), sem("gen_dve")
        mix1, mix2 = sem("mix1"), sem("mix2")
        (l_turn, l_x1, l_x1h, l_x1l, l_a, l_hs, l_hsh, l_hsl, l_o, l_x2) = (
            sem("l1_" + n) for n in ("turn", "x1", "x1h", "x1l", "a", "hs", "hsh", "hsl", "o", "x2"))
        b3_hi, b3_lo, b3_rows = sem("b3_hi"), sem("b3_lo"), sem("b3_rows")
        w3_hi, w3_lo = sem("w3_hi"), sem("w3_lo")
        q_mm, q_x3, q_hi, q_lo = (sem("l2_" + n) for n in ("mm", "x3", "hi", "lo"))
        (e_xs, e_in, e_silu, e_mul, e_turn, e_hi, e_lo, e_down, e_out) = (
            sem("l3_" + n) for n in ("xs", "in", "silu", "mul", "turn", "hi", "lo", "down", "out"))
        out_pair = [sem(f"out_pair{i}") for i in range(2)]
        out_free = sem("out_free")

        block = ctx.enter_context(nc.Block())

        @block.sync
        def _(sp):
            sp.sem_inc(z_free, CREDIT)
            sp.sem_inc(out_free, CREDIT)
            sp.dma_start(kc[:, :], consts_d).then_inc(ld_c, 16)
            sp.dma_start(cond[:, :], cond_d).then_inc(ld_c, 16)
            sp.dma_start(b1[:, :], b1_d).then_inc(ld_c, 16)
            sp.dma_start(b2[:, :], b2_d).then_inc(ld_c, 16)
            nb = B // LOADC
            sp.dma_start(xraw[:, 0:nb, :], xt_d[:, 0:nb, :]).then_inc(ld_x[0], 16)
            sp.dma_start(stage[:, 0, :], w0_d[E]).then_inc(ld_w[0], 16)
            for i in range(1, LOADC):
                sp.dma_start(xraw[:, i * nb:(i + 1) * nb, :], xt_d[:, i * nb:(i + 1) * nb, :]).then_inc(ld_x[i], 16)
            with sp.Fori(0, E // 2) as i:
                for half in range(2):
                    e = 2 * i + half
                    sp.wait_ge(stage_free, e)
                    if half == 1:
                        sp.wait_ge(ws_lo, 1)
                    sp.dma_start(stage[:, 1 - half, :], w0_d[bass.ds(e, 1)].rearrange("a p n -> p (a n)")).then_inc(
                        ld_w[1 - half], 16)
            sp.wait_ge(wx_lo, E)
            sp.wait_ge(sh_down, finished(NG * 4 - 1))
            for dst, src in ((w2raw[:, :, :], w2_d), (mask[:, :], mask_d), (w1raw[:, :], w1_d), (er_raw[:, :], cond_er_d),
                             (yraw[:, :], condt_d), (b3raw[:, :], b3_d)):
                sp.dma_start(dst, src).then_inc(ld_late, 16)
            with sp.Fori(0, T0 // 2) as i:
                sp.wait_ge(m_out, finished(2 * i + 1))
                for half in range(2):
                    sp.dma_start(z_d[bass.ds(2 * P * i + P * half, P), :],
                                 ysb[:, bass.ds(i % 2, 1), half, :].rearrange("p a n -> p (a n)")).then_inc(z_done, 16)
                sp.wait_ge(z_done, 16 * 2 * (i + 1))
                sp.sem_inc(z_free, 1)
            sp.wait_ge(w2_hi, 1)
            sp.dma_start(w2_split[0], w2h[:, :, :].bitcast(F32)).then_inc(w2_split_done, 16)
            sp.wait_ge(w2_lo, 1)
            sp.dma_start(w2_split[1], w2l[:, :, :].bitcast(F32)).then_inc(w2_split_done, 16)
            sp.wait_ge(w2_split_done, 32)
            sp.wait_ge(m_down, finished(T0 - 1))
            for q in range(4):
                for part, k in enumerate((0, 1, 0)):
                    row = 32 * q + E * part
                    sp.dma_start(wstk[row:row + E, :, :].bitcast(F32),
                                 w2_split[k, 32 * q:32 * q + 32].rearrange("o g t -> g o t")).then_inc(w2_stack, 16)
            for c in range(ZC):
                if c >= 2:
                    sp.wait_ge(l_turn, 2 * (c - 1))
                sp.dma_start(xn[:, c % 2, :], xn_d[:, c, :]).then_inc(ld_xn[c % 2], 16)
            for e in range(E):
                if e >= 2:
                    sp.wait_ge(w3_lo, e - 1)
                elif e == 0:
                    sp.wait_ge(m_down, finished(T0 - 1))
                sp.dma_start(w3raw[:, e % 2, :], w3_d[e]).then_inc(ld_w3[e % 2], 16)
            sp.wait_ge(b3_lo, 1)
            sp.wait_ge(b3_hi, 1)
            sp.wait_ge(y_stk, 1)
            sp.wait_ge(w1_lo, 1)
            sp.wait_ge(w2_stack, 16 * 12)
            sp.wait_ge(l_o, NG)
            sp.dma_start(b3_split[0], b3h[:, :].bitcast(F32)).then_inc(b3_rows, 16)
            sp.dma_start(b3_split[1], b3l[:, :].bitcast(F32)).then_inc(b3_rows, 16)
            sp.wait_ge(b3_rows, 32)
            sp.dma_start(b3[:, :, :].rearrange("p a b -> p (a b)").bitcast(F32),
                         b3_split.rearrange("k p n -> k (p n)")).then_inc(b3_rows, 16)

            def store(i, parity, count):
                sp.wait_ge(e_out, finished(2 * i + 1))
                _, rows = nc.values_load_multi_w_load_instructions(
                    row3[0:1, bass.ds(2 * TB * i, 2 * TB)], engines=SP, min_val=0, max_val=N3 - 1,
                    skip_runtime_bounds_check_because="the table holds a permutation of the rows")
                for half in range(2):
                    for q in range(TB):
                        sp.dma_start(out_d[bass.ds(rows[TB * half + q], 1)].rearrange("a s f -> (a s) f"),
                                     osb[q * S:(q + 1) * S, parity, half, :]).then_inc(out_pair[parity], 16)

            per = 16 * 2 * TB
            with sp.Fori(0, T3 // 4) as i:
                for parity in range(2):
                    store(2 * i + parity, parity, i)
                    sp.wait_ge(out_pair[parity], per * (i + 1))
                    sp.sem_inc(out_free, 1)
            for n in range(T3 // 4 * 2, T3 // 2):
                store(n, n % 2, n // 2)
                sp.wait_ge(out_pair[n % 2], per * (n // 2 + 1))

        @block.gpsimd
        def _(pool):
            pool.wait_ge(ld_w[0], 16)
            pool.tensor_copy(ws[:, 0, :], stage[:, 0, :]).then_inc(ws_hi, 1)
            pool.sem_inc(m_up, CREDIT)
            with pool.Fori(0, E // 2) as i:
                for half in range(2):
                    e = 2 * i + half
                    buf = 1 - half
                    pool.wait_ge(ld_w[buf], 16 * (i + 1 if half == 0 else i + 2))
                    raw = stage[:, buf, :]
                    hi = wx[:, bass.ds(e, 1), 0, :].rearrange("p a n -> p (a n)")
                    lo = wx[:, bass.ds(e, 1), 1, :].rearrange("p a n -> p (a n)")
                    pool.tensor_copy(hi, raw).then_inc(wx_hi, 1)
                    pool.wait_ge(wx_hi, e + 1)
                    pool.tensor_tensor(lo, raw, hi.bitcast(F32), ALU.subtract).then_inc(wx_lo, 1)
                    pool.wait_ge(wx_lo, e + 1)
                    pool.sem_inc(stage_free, 1)
            pool.wait_ge(tables, 2)
            pool.wait_ge(x_lo, NG)

            def bring(dst, src, table, i, used, ready):
                _, rows = nc.values_load_multi_w_load_instructions(
                    table[0:1, bass.ds(2 * TB * i, 2 * TB)], engines=POOL, min_val=0, max_val=B - 1,
                    skip_runtime_bounds_check_because="the table holds batches")
                for half in range(2):
                    pool.wait_ge(used, reusable(2 * i + half))
                    for q in range(TB):
                        last = pool.tensor_copy(dst[:, half, :, q, :],
                                                src[:, bass.ds(rows[TB * half + q], 1), :, :].rearrange("p a k s -> p (a k) s"))
                    last.then_inc(ready, 1)

            with pool.Fori(0, T0 // 2) as i:
                bring(xs, xt, batch0, i, m_up, m_xs)

            pool.wait_ge(z_done, 16 * T0)
            z_rows = z_d.rearrange("(n s) f -> n (s f)", s=SC)
            for c in range(ZC):
                if c >= 2:
                    pool.wait_ge(mix2, c - 1)
                for k in range(TOPK):
                    pool.indirect_dma_start(gath[:, c % 2, k, :], None, z_rows,
                                            bass.IndirectOffsetOnAxis(ap=idx[:, c, k:k + 1], axis=0)).then_inc(ld_g[c % 2], 16)

            def split_w3(e):
                pool.wait_ge(ld_w3[e % 2], 16 * (e // 2 + 1))
                pool.tensor_copy(w3[:, e, 0, :], w3raw[:, e % 2, :]).then_inc(w3_hi, 1)
                pool.wait_ge(w3_hi, e + 1)
                pool.tensor_tensor(w3[:, e, 1, :], w3raw[:, e % 2, :], w3[:, e, 0, :].bitcast(F32), ALU.subtract).then_inc(w3_lo, 1)

            for g in range(-2, NG):
                if g + 2 < NG:
                    n = g + 2
                    pool.wait_ge(l_x1h, n + 1)
                    pool.tensor_tensor(x1l[:, n % 3, :], x1[:, n % 3, :], x1h[:, n % 3, :].bitcast(F32), ALU.subtract).then_inc(l_x1l, 1)
                if 0 <= g + 1 < NG:
                    n = g + 1
                    pool.wait_ge(l_hsh, n + 1)
                    pool.tensor_tensor(hsl[:, n % 2, :], hs[:, :], hsh[:, n % 2, :].bitcast(F32), ALU.subtract).then_inc(l_hsl, 1)
                if g >= 0:
                    split_w3(g)
            for n in range(NG):
                pool.wait_ge(q_hi, n + 1)
                pool.tensor_tensor(x3t[:, n * G:(n + 1) * G, 1, :], x1[:, n % 2, :].rearrange("p (b s) -> p b s", s=S),
                                   x3t[:, n * G:(n + 1) * G, 0, :].bitcast(F32), ALU.subtract).then_inc(q_lo, 1)
            pool.sem_inc(e_in, CREDIT)
            pool.wait_ge(q_lo, NG)
            with pool.Fori(0, T3 // 2) as i:
                bring(xs3, x3t, batch3, i, e_in, e_xs)

        @block.scalar
        def _(act):
            for s in (sh_out, m_out, e_out, sh_gelu):
                act.sem_inc(s, CREDIT)
            act.wait_ge(max_done, 1)
            act.activation(rt[:, 0, :], cond[:, :], ACT.Exp, bias=sc[:, 1:2]).then_inc(exp_done, 1)
            act.activation(sc[:, 7:8], kc[:, 0:1], ACT.Gelu_apprx_tanh)
            for g in range(NG):
                act.wait_ge(ld_x[g * LOADC // NG], 16)
                act.copy(xt[:, g * G:(g + 1) * G, 0, :], xraw[:, g * G:(g + 1) * G, :]).then_inc(x_hi, 1)

            def sh_gelu_chunk(n, c):
                act.wait_ge(sh_gate, n + 1)
                act.wait_ge(sh_mul, reusable(n))
                act.activation(gt[:, c % 2, :], bank(2 * (c % 2)), ACT.Gelu_apprx_tanh).then_inc(sh_gelu, 1)

            def sh_hi_chunk(n, c):
                act.wait_ge(sh_mul, finished(n))
                act.wait_ge(sh_down, reusable(n))
                act.copy(hh[:, c % 2, :], h[:, c % 2, :]).then_inc(sh_hi, 1)

            def sh_result(g, par):
                act.wait_ge(sh_down, finished(4 * g + 3))
                act.copy(res[:, bass.ds(g * G, G), :].rearrange("p b s -> p (b s)"), bank(4 + par)).then_inc(sh_out, 1)

            def sh_act(g, par, first, last):
                for c in range(4):
                    if not (last and c == 3):
                        sh_gelu_chunk(4 * g + c + 1, (c + 1) % 4)
                    sh_hi_chunk(4 * g + c, c)
                    if c == 2 and not first:
                        sh_result(g - 1, 1 - par)

            sh_gelu_chunk(0, 0)
            sh_act(0, 0, True, False)
            with act.Fori(0, (NG - 2) // 2) as i:
                sh_act(2 * i + 1, 1, False, False)
                sh_act(2 * i + 2, 0, False, False)
            sh_act(NG - 1, 1, False, True)
            sh_result(NG - 1, 1)

            def gelu(t, par):
                act.wait_ge(m_gate, t + 1)
                act.wait_ge(m_mul, reusable(t))
                act.activation(gt[:, par, :], bank(2 * par), ACT.Gelu_apprx_tanh).then_inc(m_gelu, 1)

            def hi(t, par):
                act.wait_ge(m_turn, finished(t))
                act.wait_ge(m_down, reusable(t))
                act.copy(hh[:, par, :], bank(4 + par)).then_inc(m_hi, 1)

            def result(i, par):
                act.wait_ge(m_down, finished(2 * i + par))
                act.copy(ysb[:, bass.ds(i % 2, 1), par, :].rearrange("p a n -> p (a n)"), bank(6 + par, F)).then_inc(m_out, 1)

            gelu(0, 0)
            gelu(1, 1)
            hi(0, 0)
            with act.Fori(0, T0 // 2 - 1) as i:
                act.wait_ge(z_free, reusable(i))
                for par in range(2):
                    gelu(2 * i + 2 + par, par)
                    hi(2 * i + 1 + par, 1 - par)
                    result(i, par)
            hi(T0 - 1, 1)
            act.wait_ge(z_free, reusable(T0 // 2 - 1))
            result(T0 // 2 - 1, 0)
            result(T0 // 2 - 1, 1)

            act.wait_ge(ld_late, 16 * 6)
            act.copy(w1[:, 0, :], w1raw[:, :]).then_inc(w1_hi, 1)
            act.copy(yh[:, :], yraw[:, :]).then_inc(y_hi, 1)
            act.copy(b3h[:, :], b3raw[:, :]).then_inc(b3_hi, 1)
            act.wait_ge(w2_masked, 1)
            act.copy(w2h[:, :, :], w2raw[:, :, :]).then_inc(w2_hi, 1)

            def gen(half):
                for r in range(4):
                    n = 4 * half + r
                    act.wait_ge(gen_mm, n + 1)
                    for q in range(2):
                        o = 32 * q + 8 * r
                        last = act.copy(wbot[half][:, :, o:o + 8].rearrange("p b o -> p o b"),
                                        bank(4 * (r % 2) + q).rearrange("p (o b) -> p o b", o=8))
                    last.then_inc(gen_act, 1)

            act.wait_ge(m_down, finished(T0 - 1))
            gen(0)
            for g in range(-2, NG - 1):
                if g + 2 < NG:
                    n = g + 2
                    act.wait_ge(l_x1, n + 1)
                    if n >= 3:
                        act.wait_ge(l_o, n - 2)
                    act.copy(x1h[:, n % 3, :], x1[:, n % 3, :]).then_inc(l_x1h, 1)
                if 0 <= g + 1 < NG:
                    n = g + 1
                    act.wait_ge(l_hs, n + 1)
                    if n >= 2:
                        act.wait_ge(l_o, n - 1)
                    act.copy(hsh[:, n % 2, :], hs[:, :]).then_inc(l_hsh, 1)
            act.activation(sc[:, 7:8], kc[:, 0:1], ACT.Silu)
            act.wait_ge(l_hsl, NG)
            act.wait_ge(w3_lo, E)
            gen(1)
            for n in range(NG):
                act.wait_ge(q_x3, n + 1)
                act.copy(x3t[:, n * G:(n + 1) * G, 0, :], x1[:, n % 2, :].rearrange("p (b s) -> p b s", s=S)).then_inc(q_hi, 1)

            def silu(t, par):
                act.wait_ge(e_in, finished(t))
                act.wait_ge(e_mul, reusable(t))
                act.activation(st[:, par, :], bank(par, I3), ACT.Silu).then_inc(e_silu, 1)

            def hi3(t, par):
                act.wait_ge(e_turn, finished(t))
                act.wait_ge(e_down, reusable(t))
                act.copy(h3h[:, par, :], bank(2 + par, I3)).then_inc(e_hi, 1)

            def result3(i, par):
                act.wait_ge(e_down, finished(2 * i + par))
                act.copy(osb[:, bass.ds(i % 2, 1), par, :].rearrange("p a n -> p (a n)"),
                         dbank(2 * (i % 2) + par + 4)).then_inc(e_out, 1)

            silu(0, 0)
            silu(1, 1)
            hi3(0, 0)
            with act.Fori(0, T3 // 2 - 1) as i:
                act.wait_ge(out_free, reusable(i))
                for par in range(2):
                    silu(2 * i + 2 + par, par)
                    hi3(2 * i + 1 + par, 1 - par)
                    result3(i, par)
            hi3(T3 - 1, 1)
            act.wait_ge(out_free, reusable(T3 // 2 - 1))
            result3(T3 // 2 - 1, 0)
            result3(T3 // 2 - 1, 1)

        @block.vector
        def _(dve):
            for s in (sh_mul, m_mul, sh_lo, m_lo, e_mul, e_lo):
                dve.sem_inc(s, CREDIT)
            steps = [0]

            def step(ins):
                steps[0] += 1
                ins.then_inc(route, 1)
                dve.wait_ge(route, steps[0])

            dve.wait_ge(ld_c, 16 * 4)
            desc = kc[:, C_DESC:C_DESC + E]
            iota = kc[:, C_IOTA:C_IOTA + N0]
            step(dve.tensor_reduce(sc[:, 0:1], cond[:, :], AX_X, ALU.max))
            dve.tensor_scalar(sc[:, 1:2], sc[:, 0:1], -1.0, None, ALU.mult).then_inc(max_done, 1)
            dve.tensor_copy(ident_r[:, :], ident).then_inc(consts_done, 1)
            dve.tensor_copy(ones_r[:, :], kc[0:2, C_ONE:C_ONE + P]).then_inc(consts_done, 1)
            step(dve.tensor_copy(kb[:, :], kc[:, C_U:C_U + 257]))
            step(dve.tensor_scalar(rt[:, 1, :], cond[:, :], sc[:, 0:1], None, ALU.is_equal))
            step(dve.tensor_tensor(rt[:, 2, :], rt[:, 1, :], desc, ALU.mult))
            step(dve.tensor_reduce(sc[:, 2:3], rt[:, 2, :], AX_X, ALU.max))
            step(dve.tensor_scalar(oh[:, 0, :], desc, sc[:, 2:3], None, ALU.is_equal))
            step(dve.scalar_tensor_tensor(out=rt[:, 3, :], in0=oh[:, 0, :], scalar=-3.0e38, in1=cond[:, :],
                                          op0=ALU.mult, op1=ALU.add))
            step(dve.tensor_reduce(sc[:, 3:4], rt[:, 3, :], AX_X, ALU.max))
            step(dve.tensor_scalar(rt[:, 4, :], rt[:, 3, :], sc[:, 3:4], None, ALU.is_equal))
            step(dve.tensor_tensor(rt[:, 5, :], rt[:, 4, :], desc, ALU.mult))
            step(dve.tensor_reduce(sc[:, 4:5], rt[:, 5, :], AX_X, ALU.max))
            step(dve.tensor_scalar(oh[:, 1, :], desc, sc[:, 4:5], None, ALU.is_equal))
            dve.tensor_tensor(pair[:, 0:E], oh[:, 0, :], oh[:, 1, :], ALU.add).then_inc(pair_done, 1)
            dve.tensor_copy(pair[:, E:2 * E], oh[:, 0, :]).then_inc(pair_done, 1)
            dve.memset(scan[:, :, :, 0:E], 0.0).then_inc(pair_done, 1)
            dve.wait_ge(rank_done, 1)
            step(dve.tensor_copy(rc[:, :], bank(7, 4 * E)))
            count = rc[:, 2 * E:4 * E].rearrange("p (l e) -> p l e", l=2)
            rank = rc[:, 0:2 * E].rearrange("p (l e) -> p l e", l=2)
            full = rt[:, 8:10, :]
            step(dve.tensor_scalar(up4[:, :, :], count, float(TB - 1), None, ALU.add))
            step(dve.tensor_scalar(up4[:, :, :], up4[:, :, :], TB_SHIFT, TB_SHIFT, ALU.logical_shift_right, ALU.logical_shift_left))
            step(dve.tensor_copy(full, up4[:, :, :]))
            a, b = scan[:, 0, :, :], scan[:, 1, :, :]
            dve.wait_ge(pair_done, 3)
            step(dve.tensor_copy(a[:, :, E:], full))
            step(dve.tensor_tensor(b[:, :, E:], a[:, :, E:], a[:, :, E - 1:2 * E - 1], ALU.add))
            step(dve.tensor_tensor(a[:, :, E:], b[:, :, E:], b[:, :, E - 2:2 * E - 2], ALU.add))
            step(dve.tensor_tensor(b[:, :, E:], a[:, :, E:], a[:, :, E - 4:2 * E - 4], ALU.add))
            end = b[:, :, E:]
            step(dve.tensor_tensor(slot[:, :, :], end, full, ALU.subtract))
            step(dve.tensor_tensor(rt[:, 10:12, :], slot[:, :, :], rank, ALU.add))
            step(dve.tensor_tensor(prod[:, 0, :], rt[:, 10, :], oh[:, 0, :], ALU.mult))
            step(dve.tensor_tensor(prod[:, 1, :], rt[:, 10, :], oh[:, 1, :], ALU.mult))
            step(dve.tensor_tensor(prod[:, 2, :], rt[:, 11, :], oh[:, 0, :], ALU.mult))
            step(dve.tensor_reduce(pos[:, :], prod[:, :, :], AX_X, ALU.add))
            step(dve.tensor_scalar(sel0[:, :], iota, pos[:, 0:1], None, ALU.is_equal))
            dve.scalar_tensor_tensor(out=sel0[:, :], in0=iota, scalar=pos[:, 1:2], in1=sel0[:, :],
                                     op0=ALU.is_equal, op1=ALU.add).then_inc(sel_done, 1)
            dve.tensor_scalar(sel3[:, :], iota[:, 0:N3], pos[:, 2:3], None, ALU.is_equal).then_inc(sel_done, 1)
            dve.tensor_scalar(before3[:, :], iota[:, 0:N3], pos[:, 2:3], None, ALU.is_gt).then_inc(sel_done, 1)
            t4 = kc[0:1, C_T4:C_T4 + 72]
            for l, (n, table) in enumerate(((72, expert0), (40, expert3))):
                step(dve.tensor_tensor(cmp_t[0:1, :, 0:n], t4[:, None, 0:n].to_broadcast([1, E, n]),
                                       end[0:1, l, :].unsqueeze(2).to_broadcast([1, E, n]), ALU.is_ge))
                step(dve.tensor_reduce(tmp3[0:1, 0, 0:n], cmp_t[0:1, :, 0:n].rearrange("p e t -> p t e"), AX_X, ALU.add))
                step(dve.tensor_scalar(table[:, :], tmp3[0:1, 0, 0:n], float(E - 1), None, ALU.min))
            dve.wait_ge(slots_done, 1)
            step(dve.tensor_copy(batch0[:, :], ps[0:1, 7, 0:N0]))
            step(dve.tensor_copy(batch3[:, :], ps[0:1, 6, 0:N3]))
            step(dve.scalar_tensor_tensor(out=tmp3[:, 0, :], in0=kc[0:1, C_IOTA:C_IOTA + N3], scalar=float(B),
                                          in1=ps[0:1, 6, 2 * N3:3 * N3], op0=ALU.add, op1=ALU.subtract))
            step(dve.tensor_scalar(tmp3[:, 1, :], ps[0:1, 6, N3:2 * N3], -1.0, 1.0, ALU.mult, ALU.add))
            step(dve.tensor_tensor(tmp3[:, 0, :], tmp3[:, 0, :], tmp3[:, 1, :], ALU.mult))
            step(dve.tensor_tensor(row3[:, :], tmp3[:, 0, :], ps[0:1, 6, 0:N3], ALU.add))
            for k in range(TOPK):
                dve.scalar_tensor_tensor(out=idx[:, :, k], in0=pos[:, k:k + 1].to_broadcast([P, ZC]), scalar=float(ZC),
                                         in1=kc[:, C_ZC:C_ZC + ZC], op0=ALU.mult, op1=ALU.add).then_inc(tables, 1)

            dve.wait_ge(ws_hi, 1)
            dve.tensor_tensor(ws[:, 1, :], stage[:, 0, :], ws[:, 0, :].bitcast(F32), ALU.subtract).then_inc(ws_lo, 1)
            for g in range(NG):
                dve.wait_ge(x_hi, g + 1)
                dve.tensor_tensor(xt[:, g * G:(g + 1) * G, 1, :], xraw[:, g * G:(g + 1) * G, :],
                                  xt[:, g * G:(g + 1) * G, 0, :].bitcast(F32), ALU.subtract).then_inc(x_lo, 1)

            def sh_mul_chunk(n, c):
                dve.wait_ge(sh_up, n + 1)
                dve.wait_ge(sh_gelu, finished(n))
                dve.wait_ge(sh_lo, reusable(n))
                dve.tensor_tensor(h[:, c % 2, :], gt[:, c % 2, :], bank(2 * (c % 2) + 1), ALU.mult).then_inc(sh_mul, 1)

            def sh_lo_chunk(n, c):
                dve.wait_ge(sh_hi, n + 1)
                dve.tensor_tensor(hl[:, c % 2, :], h[:, c % 2, :], hh[:, c % 2, :].bitcast(F32), ALU.subtract).then_inc(sh_lo, 1)

            def sh_dve(g, last):
                for c in range(4):
                    if not (last and c == 3):
                        sh_mul_chunk(4 * g + c + 1, (c + 1) % 4)
                    sh_lo_chunk(4 * g + c, c)

            sh_mul_chunk(0, 0)
            with dve.Fori(0, NG - 1) as g:
                sh_dve(g, False)
            sh_dve(NG - 1, True)

            dve.wait_ge(exp_done, 1)
            step(dve.tensor_reduce(sc[:, 5:6], rt[:, 0, :], AX_X, ALU.add))
            step(dve.reciprocal(sc[:, 6:7], sc[:, 5:6]))
            step(dve.tensor_scalar(rt[:, 12, :], rt[:, 0, :], sc[:, 6:7], None, ALU.mult))
            step(dve.tensor_tensor(prod[:, 0, :], rt[:, 12, :], oh[:, 0, :], ALU.mult))
            step(dve.tensor_tensor(prod[:, 1, :], rt[:, 12, :], oh[:, 1, :], ALU.mult))
            step(dve.tensor_reduce(rw[:, :], prod[:, 0:2, :], AX_X, ALU.add))
            step(dve.tensor_tensor(sc[:, 5:6], rw[:, 0:1], rw[:, 1:2], ALU.add))
            step(dve.reciprocal(sc[:, 6:7], sc[:, 5:6]))
            step(dve.tensor_scalar(rw[:, :], rw[:, :], sc[:, 6:7], None, ALU.mult))
            step(dve.tensor_scalar(rt[:, 13, 0:2], rw[:, :], 1.0 / LAYERS, None, ALU.mult))
            step(dve.scalar_tensor_tensor(out=wt[:, :], in0=rw[:, :], scalar=1.0 - 1.0 / LAYERS, in1=rt[:, 13, 0:2],
                                          op0=ALU.mult, op1=ALU.add))

            def mul(t, par):
                dve.wait_ge(m_up, finished(t))
                dve.wait_ge(m_gelu, t + 1)
                dve.wait_ge(m_turn, reusable(t))
                dve.tensor_tensor(h[:, par, :], gt[:, par, :], bank(2 * par + 1), ALU.mult).then_inc(m_mul, 1)

            def lo(t, par):
                dve.wait_ge(m_hi, t + 1)
                dve.tensor_tensor(hl[:, par, :], bank(4 + par), hh[:, par, :].bitcast(F32), ALU.subtract).then_inc(m_lo, 1)

            mul(0, 0)
            mul(1, 1)
            lo(0, 0)
            with dve.Fori(0, T0 // 2 - 1) as i:
                for par in range(2):
                    mul(2 * i + 2 + par, par)
                    lo(2 * i + 1 + par, 1 - par)
            lo(T0 - 1, 1)

            dve.wait_ge(ld_late, 16 * 6)
            dve.tensor_tensor(w2raw[:, :, :], w2raw[:, :, :], mask[:, None, :].to_broadcast([P, E, F]), ALU.mult).then_inc(w2_masked, 1)
            dve.wait_ge(w1_hi, 1)
            dve.tensor_tensor(w1[:, 1, :], w1raw[:, :], w1[:, 0, :].bitcast(F32), ALU.subtract).then_inc(w1_lo, 1)
            dve.wait_ge(y_hi, 1)
            dve.tensor_tensor(yl[:, :], yraw[:, :], yh[:, :].bitcast(F32), ALU.subtract).then_inc(y_lo, 1)
            dve.tensor_scalar(ysel[:, :], yh[:, :].bitcast(F32), kc[:, C_HI:C_HI + 1], None, ALU.mult).then_inc(y_sel, 1)
            dve.wait_ge(y_lo, 1)
            dve.wait_ge(y_sel, 1)
            dve.scalar_tensor_tensor(out=ystk[:, :], in0=yl[:, :].bitcast(F32), scalar=kc[:, C_LO:C_LO + 1], in1=ysel[:, :],
                                     op0=ALU.mult, op1=ALU.add).then_inc(y_stk, 1)
            dve.wait_ge(b3_hi, 1)
            dve.tensor_tensor(b3l[:, :], b3raw[:, :], b3h[:, :].bitcast(F32), ALU.subtract).then_inc(b3_lo, 1)
            dve.tensor_scalar(er[:, :], er_raw[:, :], 2.0, None, ALU.mult).then_inc(y_sel, 1)
            dve.wait_ge(w2_hi, 1)
            dve.tensor_tensor(w2l[:, :, :], w2raw[:, :, :], w2h[:, :, :].bitcast(F32), ALU.subtract).then_inc(w2_lo, 1)

            def gen(half):
                for r in range(4):
                    n = 4 * half + r
                    dve.wait_ge(gen_mm, n + 1)
                    for q in range(2, 4):
                        o = 32 * q + 8 * r
                        last = dve.tensor_copy(wbot[half][:, :, o:o + 8].rearrange("p b o -> p o b"),
                                               bank(4 * (r % 2) + q).rearrange("p (o b) -> p o b", o=8))
                    last.then_inc(gen_dve, 1)

            dve.wait_ge(m_down, finished(T0 - 1))
            gen(0)

            def mix(c):
                dve.wait_ge(ld_g[c % 2], 32 * (c // 2 + 1))
                dve.wait_ge(ld_xn[c % 2], 16 * (c // 2 + 1))
                dve.scalar_tensor_tensor(out=xn[:, c % 2, :], in0=gath[:, c % 2, 0, :], scalar=wt[:, 0:1], in1=xn[:, c % 2, :],
                                         op0=ALU.mult, op1=ALU.add).then_inc(mix1, 1)
                dve.wait_ge(mix1, c + 1)
                dve.scalar_tensor_tensor(out=xn[:, c % 2, :], in0=gath[:, c % 2, 1, :], scalar=wt[:, 1:2], in1=xn[:, c % 2, :],
                                         op0=ALU.mult, op1=ALU.add).then_inc(mix2, 1)

            def cols(g):
                return res[:, :, 4 * g:4 * g + 4].rearrange("p b s -> p s b")

            def grp(ap):
                return ap.rearrange("p (s b) -> p s b", s=4)

            for g in range(-3, NG):
                if g + 3 < NG and (g + 3) % 2 == 0:
                    mix((g + 3) // 2)
                if 0 <= g + 2 < NG:
                    n = g + 2
                    dve.wait_ge(l_turn, n + 1)
                    if n >= 3:
                        dve.wait_ge(l_x1l, n - 2)
                        dve.wait_ge(l_x2, n - 2)
                    dve.tensor_tensor(grp(x1[:, n % 3, :]), grp(bank(n % 2)), cols(n), ALU.add).then_inc(l_x1, 1)
                if 0 <= g + 1 < NG:
                    n = g + 1
                    dve.wait_ge(l_a, n + 1)
                    dve.wait_ge(y_sel, 2)
                    if n >= 1:
                        dve.wait_ge(l_hsl, n)
                    dve.tensor_tensor(grp(hs[:, :]), grp(bank(2 + n % 2)), er[:, None, :].to_broadcast([P, 4, B]), ALU.mult).then_inc(l_hs, 1)
                if g >= 0:
                    dve.wait_ge(l_o, g + 1)
                    dve.scalar_tensor_tensor(out=cols(g), in0=grp(bank(4 + g % 2)), scalar=b1[:, 0:1], in1=grp(x1[:, g % 3, :]),
                                             op0=ALU.add, op1=ALU.add).then_inc(l_x2, 1)
            dve.wait_ge(l_hsl, NG)
            dve.wait_ge(w3_lo, E)
            gen(1)
            dve.wait_ge(l_x2, NG)
            for n in range(NG):
                dve.wait_ge(q_mm, n + 1)
                if n >= 2:
                    dve.wait_ge(q_lo, n - 1)
                dve.scalar_tensor_tensor(out=x1[:, n % 2, :], in0=bank(n % 4), scalar=b2[:, 0:1],
                                         in1=res[:, n * G:(n + 1) * G, :].rearrange("p b s -> p (b s)"),
                                         op0=ALU.add, op1=ALU.add).then_inc(q_x3, 1)

            def mul3(t, par):
                dve.wait_ge(e_silu, t + 1)
                dve.wait_ge(e_turn, reusable(t))
                dve.tensor_tensor(h3[:, par, :], st[:, par, :], ps[:, par, I3:2 * I3], ALU.mult).then_inc(e_mul, 1)

            def lo3(t, par):
                dve.wait_ge(e_hi, t + 1)
                dve.tensor_tensor(h3l[:, par, :], bank(2 + par, I3), h3h[:, par, :].bitcast(F32), ALU.subtract).then_inc(e_lo, 1)

            mul3(0, 0)
            mul3(1, 1)
            lo3(0, 0)
            with dve.Fori(0, T3 // 2 - 1) as i:
                for par in range(2):
                    mul3(2 * i + 2 + par, par)
                    lo3(2 * i + 1 + par, 1 - par)
            lo3(T3 - 1, 1)

        @block.tensor
        def _(pe):
            for s in (sh_down, m_turn, m_down, e_turn, e_down):
                pe.sem_inc(s, CREDIT)

            def split_product(out, w, m, start=True, stop=True):
                for n, (a, b) in enumerate(((0, 0), (0, 1), (1, 0))):
                    last = pe.matmul(out, w[a], m[b], start=start and n == 0, stop=stop and n == 2)
                return last

            pe.wait_ge(pair_done, 2)
            pe.wait_ge(route, 1)
            pe.matmul(ps[:, 7, 0:2 * E], before, pair[:, :], start=True, stop=True)
            pe.matmul(ps[:, 7, 2 * E:4 * E], ones, pair[:, :], start=True, stop=True).then_inc(rank_done, 1)
            pe.wait_ge(sel_done, 3)
            pe.matmul(ps[0:1, 7, 0:N0], batch, sel0[:, :], start=True, stop=True)
            pe.matmul(ps[0:1, 6, 0:N3], batch, sel3[:, :], start=True, stop=True)
            pe.matmul(ps[0:1, 6, N3:2 * N3], ones[:, 0:1], sel3[:, :], start=True, stop=True)
            pe.matmul(ps[0:1, 6, 2 * N3:3 * N3], ones[:, 0:1], before3[:, :], start=True, stop=True).then_inc(slots_done, 1)

            def sh_in(g, n, c):
                if c == 0:
                    pe.wait_ge(x_lo, g + 1)
                pe.wait_ge(sh_mul, reusable(n))
                m = [xt[:, bass.ds(g * G, G), k, :] for k in range(2)]
                for what, sem_ in ((0, sh_gate), (1, sh_up)):
                    w = [ws[:, k, what * I0 + c * P:what * I0 + (c + 1) * P] for k in range(2)]
                    out = bank(2 * (c % 2) + what).rearrange("p (b s) -> p b s", s=S)
                    split_product(out, w, m).then_inc(sem_, 1)

            def sh_down_(g, par, n, c):
                if c == 0:
                    pe.wait_ge(sh_out, reusable(g))
                pe.wait_ge(sh_lo, finished(n))
                w = [ws[:, k, 2 * I0 + c * P:2 * I0 + (c + 1) * P] for k in range(2)]
                split_product(bank(4 + par), w, (hh[:, c % 2, :], hl[:, c % 2, :]), start=c == 0, stop=c == 3).then_inc(sh_down, 1)

            def sh_pe(g, par, last):
                for c in range(4):
                    if c < 2:
                        sh_in(g, 4 * g + c + 2, c + 2)
                    elif not last:
                        sh_in(g + 1, 4 * g + c + 2, c - 2)
                    sh_down_(g, par, 4 * g + c, c)

            pe.wait_ge(ws_lo, 1)
            sh_in(0, 0, 0)
            sh_in(0, 1, 1)
            sh_pe(0, 0, False)
            with pe.Fori(0, (NG - 2) // 2) as i:
                sh_pe(2 * i + 1, 1, False)
                sh_pe(2 * i + 2, 0, False)
            sh_pe(NG - 1, 1, True)

            def experts(table, start, count):
                _, e = nc.values_load_multi_w_load_instructions(
                    table[0:1, bass.ds(start, count)], engines=PE, min_val=0, max_val=E - 1,
                    skip_runtime_bounds_check_because="the table holds experts")
                return e

            def weights(w, e, k, a, b):
                return w[:, bass.ds(e, 1), k, a:b].rearrange("p a n -> p (a n)")

            def gate_up(t, par, e):
                pe.wait_ge(m_xs, t + 1)
                pe.wait_ge(m_mul, reusable(t))
                x = [xs[:, par, k, :, :].rearrange("p q s -> p (q s)") for k in range(2)]
                for what, sem_ in ((0, m_gate), (1, m_up)):
                    w = [weights(wx, e, k, what * I0, (what + 1) * I0) for k in range(2)]
                    split_product(bank(2 * par + what), x, w).then_inc(sem_, 1)

            def turn(t, par):
                pe.wait_ge(m_mul, finished(t))
                pe.wait_ge(m_lo, reusable(t))
                for c in range(4):
                    last = pe.transpose(bank(4 + par)[:, c * P:(c + 1) * P], h[:, par, c * P:(c + 1) * P], ident)
                last.then_inc(m_turn, 1)

            def down(t, par, e):
                pe.wait_ge(m_lo, finished(t))
                pe.wait_ge(m_out, reusable(t))
                for c in range(4):
                    x = [v[:, par, c * P:(c + 1) * P] for v in (hh, hl)]
                    w = [weights(wx, e, k, 2 * I0 + c * P, 2 * I0 + (c + 1) * P) for k in range(2)]
                    last = split_product(bank(6 + par, F), x, w, start=c == 0, stop=c == 3)
                last.then_inc(m_down, 1)

            pe.wait_ge(sh_out, finished(NG - 1))
            pe.wait_ge(tables, 2)
            pe.wait_ge(wx_lo, E)
            e0, e1 = experts(expert0, 0, 2)
            gate_up(0, 0, e0)
            gate_up(1, 1, e1)
            turn(0, 0)
            with pe.Fori(0, T0 // 2 - 1) as i:
                e = experts(expert0, 2 * i, 4)
                for par in range(2):
                    gate_up(2 * i + 2 + par, par, e[2 + par])
                    turn(2 * i + 1 + par, 1 - par)
                    down(2 * i + par, par, e[par])
            e0, e1 = experts(expert0, T0 - 2, 2)
            turn(T0 - 1, 1)
            down(T0 - 2, 0, e0)
            down(T0 - 1, 1, e1)

            def gen(half):
                for r in range(4):
                    n = 4 * half + r
                    if r >= 2:
                        pe.wait_ge(gen_act, n - 1)
                        pe.wait_ge(gen_dve, n - 1)
                    for k in range(8):
                        for q in range(4):
                            last = pe.matmul(ps[:, 4 * (r % 2) + q, 64 * k:64 * k + 64],
                                             wstk[32 * q:32 * q + 3 * E, 8 * r + k, :],
                                             ystk[32 * q:32 * q + 3 * E, 64 * half:64 * half + 64], start=True, stop=True)
                    last.then_inc(gen_mm, 1)

            pe.wait_ge(w2_stack, 16 * 12)
            pe.wait_ge(y_stk, 1)
            pe.wait_ge(m_out, finished(T0 - 1))
            gen(0)

            pe.wait_ge(gen_act, 4)
            pe.wait_ge(gen_dve, 4)
            pe.wait_ge(w1_lo, 1)
            A_, WB, BB = ([w1[:, k, n * F:(n + 1) * F] for k in range(2)] for n in range(3))
            for g in range(-2, NG):
                if g + 2 < NG:
                    n = g + 2
                    pe.wait_ge(mix2, n // 2 + 1)
                    if n >= 2:
                        pe.wait_ge(l_x1, n - 1)
                    for s in range(4):
                        col = (4 * (n % 2) + s) * F
                        last = pe.transpose(bank(n % 2)[:, s * P:(s + 1) * P], xn[:, n // 2 % 2, col:col + F], ident)
                    last.then_inc(l_turn, 1)
                if 0 <= g + 1 < NG:
                    n = g + 1
                    pe.wait_ge(l_x1l, n + 1)
                    if n >= 2:
                        pe.wait_ge(l_hs, n - 1)
                    split_product(bank(2 + n % 2), A_, (x1h[:, n % 3, :], x1l[:, n % 3, :])).then_inc(l_a, 1)
                if g >= 0:
                    if g >= 2:
                        pe.wait_ge(l_x2, g - 1)
                    split_product(bank(4 + g % 2), WB, (x1h[:, g % 3, :], x1l[:, g % 3, :]), stop=False)
                    pe.wait_ge(l_hsl, g + 1)
                    split_product(bank(4 + g % 2), BB, (hsh[:, g % 2, :], hsl[:, g % 2, :]), start=False).then_inc(l_o, 1)

            pe.wait_ge(l_x2, NG)
            gen(1)
            pe.wait_ge(gen_act, 8)
            pe.wait_ge(gen_dve, 8)
            for n in range(NG):
                if n >= 4:
                    pe.wait_ge(q_x3, n - 3)
                for k in range(G):
                    b = n * G + k
                    last = pe.matmul(ps[:, n % 4, k * S:(k + 1) * S], wbot[b // 64][:, b % 64, :], res[:, b, :], start=True, stop=True)
                last.then_inc(q_mm, 1)

            def gate_up3(t, par, ybank, e):
                pe.wait_ge(e_xs, t + 1)
                pe.wait_ge(e_mul, reusable(t))
                x = [xs3[:, par, k, :, :].rearrange("p q s -> p (q s)") for k in range(2)]
                for k in range(2):
                    pe.matmul(dbank(ybank), x[k], ident_r[:, :], start=k == 0, stop=False, skip_group_check=True)
                w = [weights(w3, e, k, 0, 2 * I3) for k in range(2)]
                split_product(bank(par), x, w, stop=False)
                pe.matmul(bank(par), ones_r[:, :], b3[:, bass.ds(e, 1), 0:2 * I3].rearrange("p a n -> p (a n)"),
                          start=False, stop=True).then_inc(e_in, 1)

            def turn3(t, par):
                pe.wait_ge(e_mul, finished(t))
                pe.wait_ge(e_lo, reusable(t))
                for c in range(2):
                    last = pe.transpose(bank(2 + par)[:, c * P:(c + 1) * P], h3[:, par, c * P:(c + 1) * P], ident)
                last.then_inc(e_turn, 1)

            def down3(t, par, ybank, e):
                pe.wait_ge(e_lo, finished(t))
                for c in range(2):
                    x = [v[:, par, c * P:(c + 1) * P] for v in (h3h, h3l)]
                    w = [weights(w3, e, k, 2 * I3 + c * P, 2 * I3 + (c + 1) * P) for k in range(2)]
                    for a, b in ((0, 0), (0, 1), (1, 0)):
                        pe.matmul(dbank(ybank), x[a], w[b], start=False, stop=False, skip_group_check=True)
                pe.matmul(dbank(ybank), ones_r[:, :], b3[:, bass.ds(e, 1), 2 * I3:B3].rearrange("p a n -> p (a n)"),
                          start=False, stop=True, skip_group_check=True).then_inc(e_down, 1)

            pe.wait_ge(q_x3, NG)
            pe.wait_ge(w3_lo, E)
            pe.wait_ge(b3_rows, 48)
            pe.wait_ge(consts_done, 2)
            e0, e1 = experts(expert3, 0, 2)
            gate_up3(0, 0, 4, e0)
            gate_up3(1, 1, 5, e1)
            turn3(0, 0)
            with pe.Fori(0, T3 // 2 - 1) as i:
                e = experts(expert3, 2 * i, 4)
                for par in range(2):
                    pe.wait_ge(e_out, reusable(2 * i + par))
                    gate_up3(2 * i + 2 + par, par, 2 * ((i + 1) % 2) + par + 4, e[2 + par])
                    turn3(2 * i + 1 + par, 1 - par)
                    down3(2 * i + par, par, 2 * (i % 2) + par + 4, e[par])
            e0, e1 = experts(expert3, T3 - 2, 2)
            turn3(T3 - 1, 1)
            last_pair = T3 // 2 - 1
            down3(T3 - 2, 0, 4 + 2 * (last_pair % 2), e0)
            down3(T3 - 1, 1, 5 + 2 * (last_pair % 2), e1)


def kernel(**inputs):
    import numpy as _np
    import concourse.bacc as _bacc
    from concourse import mybir as _mybir
    from concourse.bass_utils import run_bass_kernel_spmd as _run

    v = {k: _np.asarray(a) for k, a in inputs.items()}
    x, cond = v["x"], v["cond_8"]

    def mlp(gate, up, down, inner):
        return _np.concatenate([gate, up, down.reshape(inner // P, P, F).transpose(1, 0, 2).reshape(P, inner)], axis=1)

    w0 = _np.stack([mlp(g, u, d, I0) for g, u, d in zip(v["L0_cond_skill_gate"], v["L0_cond_skill_up"], v["L0_cond_skill_down"])]
                   + [mlp(v["L0_cond_shared_gate"], v["L0_cond_shared_up"], v["L0_cond_shared_down"], I0)])
    w3 = _np.stack([mlp(u.T, g.T, d.T, I3) for u, g, d in zip(v["L3_cond_W_up"], v["L3_cond_W_gate"], v["L3_cond_W_down"])])
    w1 = _np.concatenate([v["L1_cond_As"].reshape(P, F).T, v["L1_cond_W_base"].T,
                          v["L1_cond_Bs"].transpose(0, 2, 1).reshape(P, F)], axis=1)
    rows = _np.zeros((4, 32, B), cond.dtype)
    rows[:, 0:3 * E] = _np.tile(cond.T, (3, 1))
    arrays = {
        "constants": constants(),
        "cond": cond,
        "x_feature": x.transpose(2, 0, 1),
        "x_batch": x.reshape(B, ZC, SC * F),
        "w_layer0": w0,
        "w_layer1": w1,
        "cond_er": _np.repeat(cond.T, R, axis=0),
        "b_layer1": v["L1_cond_b_base"].reshape(F, 1),
        "w_layer2": v["L2_cond_weight"].transpose(1, 0, 2),
        "mask": v["L2_cond_mask"],
        "cond_rows": rows.reshape(P, B),
        "b_layer2": v["L2_cond_bias"].reshape(F, 1),
        "w_layer3": w3,
        "b_layer3": _np.concatenate([v["L3_cond_b_up"], v["L3_cond_b_gate"], v["L3_cond_b_down"]], axis=1).reshape(P, E * B3 // P),
    }
    nc = _bacc.Bacc("TRN2", target_bir_lowering=False, num_devices=1)
    arrays = {"in_" + k: _np.ascontiguousarray(a) for k, a in arrays.items()}
    args = [nc.dram_tensor(k, a.shape, _mybir.dt.from_np(a.dtype), kind="ExternalInput").ap() for k, a in arrays.items()]
    args.append(nc.dram_tensor("out", (N3, S, F), _mybir.dt.float32, kind="ExternalOutput").ap())
    build(nc, *args)
    r = _run(nc, [arrays], core_ids=[0])
    return r.results[0]["out"][0:B]
```

```python
from contextlib import ExitStack

import numpy as np

import concourse.bass as bass
from concourse import mybir

ALU = mybir.AluOpType
ACT = mybir.ActivationFunctionType
AX_X = mybir.AxisListType.X
F32 = mybir.dt.float32
F32R = mybir.dt.float32r
BF16 = mybir.dt.bfloat16
I32 = mybir.dt.int32
POOL = (mybir.EngineType.Pool,)
PE = (mybir.EngineType.PE,)
SP = (mybir.EngineType.SP,)

P = 128
B, S, F = 128, 32, 128
E, I0, I3, R = 8, 512, 256, 16
TOPK, LAYERS = 2, 12
TB = P // S
TB_SHIFT = TB.bit_length() - 1
T0 = (B * TOPK + E * (TB - 1)) // TB
T3 = (B + E * (TB - 1)) // TB
N0, N3 = T0 * TB, T3 * TB
G = 16
NG = B // G
W0 = 3 * I0
W3 = 3 * I3
B3 = 2 * I3 + F
ZC = 4
SC = S // ZC
LOADC = 4
CREDIT = 2

C_ID, C_U, C_ONE, C_B = 0, 128, 256, 384
C_DESC = 385
C_IOTA = C_DESC + E
C_T4 = C_IOTA + N0
C_ZC = C_T4 + 72
C_Y = C_ZC + ZC
C_END = C_Y + 3
W_PART = (0, 0, 1, 1, 0, 2)
Y_PART = (0, 1, 0, 1, 2, 0)
KY = E * len(W_PART)


def finished(n):
    return n + 1 + CREDIT


def reusable(n):
    return n + 1


def constants():
    c = np.zeros((P, C_END), np.float32)
    p = np.arange(P)
    c[:, C_ID:C_ID + P] = np.eye(P)
    c[:, C_U:C_U + P] = p[:, None] < p[None, :]
    c[:, C_ONE:C_ONE + P] = 1
    c[:, C_B] = p
    c[:, C_DESC:C_DESC + E] = E - np.arange(E)
    c[:, C_IOTA:C_IOTA + N0] = np.arange(N0)
    c[:, C_T4:C_T4 + 72] = TB * np.arange(72)
    c[:, C_ZC:C_ZC + ZC] = np.arange(ZC)
    for row in range(KY):
        for half in (0, 64):
            c[half + row, C_Y + Y_PART[row // E]] = 1
    return c


def build(nc, consts_d, cond_d, xt_d, w0_d, w1_d, cond_er_d, b1_d, w2_d, mask_d, condt_d, b2_d, w3_d, b3_d, out_d):
    z_d = nc.dram_tensor("layer0_slots", (N0 * S, F), F32, kind="Internal").ap()

    w2_split = nc.dram_tensor("layer2_weight_parts", (3, E, P, F), BF16, kind="Internal").ap()
    b3_split = nc.dram_tensor("layer3_bias_split", (2, P, E * B3 // P), F32, kind="Internal").ap()

    with ExitStack() as ctx:
        def sb(name, shape, dt=F32):
            return ctx.enter_context(nc.sbuf_tensor(name, shape, dt))

        def sem(name):
            return ctx.enter_context(nc.semaphore(name))

        SIZE_A, SIZE_B, SIZE_C, SIZE_D, SIZE_W = 98304, 32768, 16384, 24576, 24576
        SIZE_ALL = SIZE_A + SIZE_B + SIZE_C + SIZE_D + SIZE_W
        sb("arena", [P, SIZE_ALL // 4])
        A = nc.sbuf_base - SIZE_ALL
        RB = A + SIZE_A
        RC = RB + SIZE_B
        RD = RC + SIZE_C
        RW = RD + SIZE_D

        def at(name, offset, shape, dt=F32):
            return nc.alloc_sbuf_tensor_at(name, shape, dt, offset=offset)

        wx = at("expert_weights", A, [P, E, 2, W0], F32R)
        xt = at("x_hi_lo", RB, [P, B, 2, S], F32R)
        xraw = at("x_raw", RC, [P, B, S])
        res = at("residual", RC, [P, B, S])
        ws = at("shared_weights", RD, [P, 2, W0], F32R)
        stage = at("weight_stage", RD + 12288, [P, 2, W0])
        gt = at("gelu_out", RW, [P, 2, 512])
        h = at("hidden", RW + 4096, [P, 2, 512])
        hh = at("hidden_hi", RW + 8192, [P, 2, 512], F32R)
        hl = at("hidden_lo", RW + 12288, [P, 2, 512], F32R)
        xs = at("tile_x", RW + 16384, [P, 2, 2, TB, S], F32R)
        ysb = at("tile_out", RW + 18432, [P, 2, 2, F])
        cmp_t = at("tile_compare", RW + 20480, [P, E, 72])
        sel0 = at("slot_onehot0", RW + 22784, [P, N0], BF16)
        sel3 = at("slot_onehot3", RW + 23360, [P, N3], BF16)
        before3 = at("slot_before3", RW + 23680, [P, N3], BF16)
        wstk = at("w2_stack", A + 49152, [64 + KY, F // 2, F], BF16)
        wbot = at("w_bot", A + 65536, [P, B, F])
        gath = at("gathered", RB, [P, ZC, TOPK, SC * F])
        w2raw = at("w2_raw", RD, [P, E, F])
        w2p = at("w2_parts", RD + 4096, [P, 3, E, F], BF16)
        mask = at("mask", RD + 12288, [P, F])
        w1raw = at("w1_raw", RD + 12800, [P, 3 * F])
        er_raw = at("cond_er_raw", RD + 14336, [P, B])
        yraw = at("cond_t_raw", RD + 14848, [P, B])
        yp = at("cond_t_parts", RD + 15360, [P, 3, B], BF16)
        ysum = at("cond_t_sum", RD + 16128, [P, B])
        b3raw = at("b3_raw", RD + 16896, [P, E * B3 // P])
        b3h = at("b3_hi", RD + 17408, [P, E * B3 // P], F32R)
        b3l = at("b3_lo", RD + 17920, [P, E * B3 // P], F32R)
        x1 = at("x1", RW, [P, 3, 512])
        x1h = at("x1_hi", RW + 6144, [P, 3, 512], F32R)
        x1l = at("x1_lo", RW + 12288, [P, 3, 512], F32R)
        hsh = at("adapter_hi", RW + 18432, [P, 2, 512], F32R)
        hsl = at("adapter_lo", RD + 18432, [P, 2, 512], F32R)
        w3raw = at("w3_raw", RW + 18432, [P, 2, W3])
        hs = at("adapter_h", A, [P, 512])
        w3 = at("w3_hi_lo", A, [P, E, 2, W3], F32R)
        x3t = at("x3_hi_lo", A + 49152, [P, B, 2, S], F32R)
        b3 = at("b3_rows", RD, [2, E, B3], F32R)
        st = at("silu_out", RW, [P, 2, I3])
        h3 = at("hidden3", RW + 2048, [P, 2, I3])
        h3h = at("hidden3_hi", RW + 4096, [P, 2, I3], F32R)
        h3l = at("hidden3_lo", RW + 6144, [P, 2, I3], F32R)
        xs3 = at("tile_x3", RW + 8192, [P, 2, 2, TB, S], F32R)
        osb = at("tile_out3", RW + 10240, [P, 2, 2, F])
        yres3 = at("tile_rest3", RW + 12288, [P, 2, F])

        kc = sb("constants", [P, C_END])
        kb = sb("constants_bf16", [P, 257], BF16)
        ident = kc[:, C_ID:C_ID + P]
        before = kb[:, 0:P]
        ones = kb[:, P:2 * P]
        batch = kb[:, 2 * P:2 * P + 1]
        ident_r = sb("identity_zero_identity", [P, 3 * P], F32R)
        ones_r = sb("ones_r", [2, P], F32R)
        cond = sb("cond", [P, E])
        rt = sb("route_scratch", [P, 24, E])
        oh = sb("onehots", [P, 2, E])
        pair = sb("pairs_bf16", [P, 2 * E], BF16)
        rc = sb("rank_count", [P, 4 * E])
        scan = sb("scan", [P, 2, 2, 2 * E])
        up4 = sb("rounded_up", [P, 2, E], I32)
        slot = sb("slot", [P, 2, E])
        prod = sb("prod", [P, 3, E])
        pos = sb("pos", [P, 3])
        idx = sb("gather_rows", [P, ZC, 2], I32)
        rw = sb("rw", [P, 2])
        wt = sb("top_weights", [P, 2])
        sc = sb("scalars", [P, 8])
        batch0 = sb("slot_batch0", [1, N0], I32)
        batch3 = sb("slot_batch3", [1, N3], I32)
        expert0 = sb("tile_expert0", [1, 72], I32)
        expert3 = sb("tile_expert3", [1, 40], I32)
        row3 = sb("slot_row3", [1, N3], I32)
        tmp3 = sb("slot_tmp3", [1, 2, N3])
        w1 = sb("w1_hi_lo", [P, 2, 3 * F], F32R)
        er = sb("cond_er", [P, B])
        ystk = sb("cond_stack", [P, B], BF16)
        yres = sb("tile_rest", [P, 2, F])
        b1 = sb("b1", [P, 1])
        b2 = sb("b2", [P, 1])

        ps = ctx.enter_context(nc.psum_tensor("ps", [P, 8, 512], F32))

        def bank(n, width=512):
            return ps[:, n, 0:width]

        def dbank(n, start=0, end=F):
            return ps[:, bass.ds(n, 1), start:end].rearrange("p a n -> p (a n)")

        def gen_out(n):
            return F // 2 * (n % 2) + 4 * (n // 2)

        ld_c = sem("ld_constants")
        ld_x = [sem(f"ld_x{i}") for i in range(LOADC)]
        ld_w = [sem(f"ld_stage{i}") for i in range(2)]
        stage_free = sem("stage_free")
        ld_late = sem("ld_late")
        ld_g = [sem(f"ld_gather{i}") for i in range(ZC)]
        ld_w3 = [sem(f"ld_w3{i}") for i in range(2)]
        route = sem("route_step")
        late = sem("late_step")
        exp_done = sem("exp_done")
        max_done = sem("max_done")
        pair_done = sem("pair_done")
        rank_done = sem("rank_done")
        sel_done = sem("sel_done")
        slots_done = sem("slots_done")
        tables = sem("tables_done")
        consts_done = sem("consts_done")
        x_hi = sem("x_hi")
        x_lo = sem("x_lo")
        ws_hi = sem("ws_hi")
        ws_lo = sem("ws_lo")
        wx_hi = sem("wx_hi")
        wx_lo = sem("wx_lo")
        sh_gate, sh_up, sh_gelu, sh_mul, sh_hi, sh_lo, sh_down, sh_out = (
            sem("sh_" + n) for n in ("gate", "up", "gelu", "mul", "hi", "lo", "down", "out"))
        (m_xs, m_gate, m_up, m_gelu, m_mul, m_turn, m_hi, m_lo, m_down, m_rest, m_out) = (
            sem("moe_" + n) for n in ("xs", "gate", "up", "gelu", "mul", "turn", "hi", "lo", "down", "rest", "out"))
        z_done = sem("z_stored")
        z_free = sem("z_free")
        w2_parts, w2_split_done, w2_stack = (sem("w2_" + n) for n in ("parts", "split", "stack"))
        w1_hi, w1_lo = sem("w1_hi"), sem("w1_lo")
        y_stk, er_done = sem("y_stack"), sem("er_done")
        gen_mm, gen_act, gen_dve = sem("gen_mm"), sem("gen_act"), sem("gen_dve")
        mix1, mix2, wt_done = sem("mix1"), sem("mix2"), sem("wt_done")
        (l_turn, l_x1, l_x1h, l_x1l, l_a, l_hs, l_hsh, l_hsl, l_o, l_x2) = (
            sem("l1_" + n) for n in ("turn", "x1", "x1h", "x1l", "a", "hs", "hsh", "hsl", "o", "x2"))
        b3_hi, b3_lo, b3_rows = sem("b3_hi"), sem("b3_lo"), sem("b3_rows")
        w3_hi, w3_lo = sem("w3_hi"), sem("w3_lo")
        q_mm, q_x3, q_hi, q_lo = (sem("l2_" + n) for n in ("mm", "x3", "hi", "lo"))
        (e_xs, e_in, e_silu, e_mul, e_turn, e_hi, e_lo, e_down, e_rest, e_out) = (
            sem("l3_" + n) for n in ("xs", "in", "silu", "mul", "turn", "hi", "lo", "down", "rest", "out"))
        out_pair = [sem(f"out_pair{i}") for i in range(2)]
        out_free = sem("out_free")

        block = ctx.enter_context(nc.Block())

        @block.sync
        def _(sp):
            sp.sem_inc(z_free, CREDIT)
            sp.sem_inc(out_free, CREDIT)
            sp.dma_start(kc[:, :], consts_d).then_inc(ld_c, 16)
            sp.dma_start(cond[:, :], cond_d).then_inc(ld_c, 16)
            sp.dma_start(b1[:, :], b1_d).then_inc(ld_c, 16)
            sp.dma_start(b2[:, :], b2_d).then_inc(ld_c, 16)
            nb = B // LOADC
            sp.dma_start(xraw[:, 0:nb, :], xt_d[:, 0:nb, :]).then_inc(ld_x[0], 16)
            sp.dma_start(stage[:, 0, :], w0_d[E]).then_inc(ld_w[0], 16)
            for i in range(1, LOADC):
                sp.dma_start(xraw[:, i * nb:(i + 1) * nb, :], xt_d[:, i * nb:(i + 1) * nb, :]).then_inc(ld_x[i], 16)
            with sp.Fori(0, E // 2) as i:
                for half in range(2):
                    e = 2 * i + half
                    sp.wait_ge(stage_free, e + 1)
                    if half == 1:
                        sp.wait_ge(ws_lo, 1)
                    sp.dma_start(stage[:, 1 - half, :], w0_d[bass.ds(e, 1)].rearrange("a p n -> p (a n)")).then_inc(
                        ld_w[1 - half], 16)
            sp.wait_ge(wx_lo, E)
            sp.wait_ge(sh_down, finished(NG * 4 - 1))
            for dst, src in ((w2raw[:, :, :], w2_d), (mask[:, :], mask_d), (w1raw[:, :], w1_d), (er_raw[:, :], cond_er_d),
                             (yraw[:, :], condt_d), (b3raw[:, :], b3_d)):
                sp.dma_start(dst, src).then_inc(ld_late, 16)
            with sp.Fori(0, T0 // 2) as i:
                sp.wait_ge(m_out, finished(2 * i + 1))
                for half in range(2):
                    sp.dma_start(z_d[bass.ds(2 * P * i + P * half, P), :],
                                 ysb[:, bass.ds(i % 2, 1), half, :].rearrange("p a n -> p (a n)")).then_inc(z_done, 16)
                sp.wait_ge(z_done, 16 * 2 * (i + 1))
                sp.sem_inc(z_free, 1)
            sp.wait_ge(w2_parts, 3)
            for k in range(3):
                sp.dma_start(w2_split[k].rearrange("g o t -> o g t"), w2p[:, k, :, :]).then_inc(w2_split_done, 16)
            sp.wait_ge(w2_split_done, 48)
            sp.wait_ge(m_down, finished(T0 - 1))
            for half in range(2):
                for n, k in enumerate(W_PART):
                    row = 64 * half + E * n
                    sp.dma_start(wstk[row:row + E, :, :], w2_split[k, :, 64 * half:64 * half + 64]).then_inc(w2_stack, 16)
            sp.wait_ge(l_o, NG)
            for e in range(E):
                if e >= 2:
                    sp.wait_ge(w3_lo, e - 1)
                sp.dma_start(w3raw[:, e % 2, :], w3_d[e]).then_inc(ld_w3[e % 2], 16)
            sp.wait_ge(b3_lo, 1)
            sp.wait_ge(b3_hi, 1)
            sp.wait_ge(y_stk, 1)
            sp.wait_ge(w1_lo, 1)
            sp.wait_ge(er_done, 1)
            sp.dma_start(b3_split[0], b3h[:, :].bitcast(F32)).then_inc(b3_rows, 16)
            sp.dma_start(b3_split[1], b3l[:, :].bitcast(F32)).then_inc(b3_rows, 16)
            sp.wait_ge(b3_rows, 32)
            sp.dma_start(b3[:, :, :].rearrange("p a b -> p (a b)").bitcast(F32),
                         b3_split.rearrange("k p n -> k (p n)")).then_inc(b3_rows, 16)

            def store(i, parity, count):
                sp.wait_ge(e_out, finished(2 * i + 1))
                _, rows = nc.values_load_multi_w_load_instructions(
                    row3[0:1, bass.ds(2 * TB * i, 2 * TB)], engines=SP, min_val=0, max_val=N3 - 1,
                    skip_runtime_bounds_check_because="the table holds a permutation of the rows")
                for half in range(2):
                    for q in range(TB):
                        sp.dma_start(out_d[bass.ds(rows[TB * half + q], 1)].rearrange("a s f -> (a s) f"),
                                     osb[q * S:(q + 1) * S, parity, half, :]).then_inc(out_pair[parity], 16)

            per = 16 * 2 * TB
            with sp.Fori(0, T3 // 4) as i:
                for parity in range(2):
                    store(2 * i + parity, parity, i)
                    sp.wait_ge(out_pair[parity], per * (i + 1))
                    sp.sem_inc(out_free, 1)
            for n in range(T3 // 4 * 2, T3 // 2):
                store(n, n % 2, n // 2)
                sp.wait_ge(out_pair[n % 2], per * (n // 2 + 1))

        @block.gpsimd
        def _(pool):
            pool.sem_inc(m_up, CREDIT)
            pool.sem_inc(stage_free, 1)
            for g in range(2, NG):
                pool.wait_ge(x_hi, g + 1)
                pool.wait_ge(x_lo, g)
                pool.tensor_tensor(xt[:, g * G:(g + 1) * G, 1, :], xraw[:, g * G:(g + 1) * G, :],
                                   xt[:, g * G:(g + 1) * G, 0, :].bitcast(F32), ALU.subtract).then_inc(x_lo, 1)
            with pool.Fori(0, E // 2) as i:
                for half in range(2):
                    e = 2 * i + half
                    pool.wait_ge(wx_hi, e + 1)
                    pool.tensor_tensor(wx[:, bass.ds(e, 1), 1, :].rearrange("p a n -> p (a n)"), stage[:, 1 - half, :],
                                       wx[:, bass.ds(e, 1), 0, :].rearrange("p a n -> p (a n)").bitcast(F32),
                                       ALU.subtract).then_inc(wx_lo, 1)
                    pool.wait_ge(wx_lo, e + 1)
                    pool.sem_inc(stage_free, 1)
            pool.wait_ge(tables, 2)
            pool.wait_ge(x_lo, NG)

            def bring(dst, src, table, i, used, ready):
                _, rows = nc.values_load_multi_w_load_instructions(
                    table[0:1, bass.ds(2 * TB * i, 2 * TB)], engines=POOL, min_val=0, max_val=B - 1,
                    skip_runtime_bounds_check_because="the table holds batches")
                for half in range(2):
                    pool.wait_ge(used, reusable(2 * i + half))
                    for q in range(TB):
                        last = pool.tensor_copy(dst[:, half, :, q, :],
                                                src[:, bass.ds(rows[TB * half + q], 1), :, :].rearrange("p a k s -> p (a k) s"))
                    last.then_inc(ready, 1)

            with pool.Fori(0, T0 // 2) as i:
                bring(xs, xt, batch0, i, m_up, m_xs)

            pool.wait_ge(z_done, 16 * T0)
            z_rows = z_d.rearrange("(n s) f -> n (s f)", s=SC)
            for c in range(ZC):
                for k in range(TOPK):
                    pool.indirect_dma_start(gath[:, c, k, :], None, z_rows,
                                            bass.IndirectOffsetOnAxis(ap=idx[:, c, k:k + 1], axis=0)).then_inc(ld_g[c], 16)

            for g in range(-2, NG):
                if g + 2 < NG:
                    n = g + 2
                    pool.wait_ge(l_x1h, n + 1)
                    pool.tensor_tensor(x1l[:, n % 3, :], x1[:, n % 3, :], x1h[:, n % 3, :].bitcast(F32), ALU.subtract).then_inc(l_x1l, 1)
                if 0 <= g + 1 < NG:
                    n = g + 1
                    pool.wait_ge(l_hsh, n + 1)
                    pool.tensor_tensor(hsl[:, n % 2, :], hs[:, :], hsh[:, n % 2, :].bitcast(F32), ALU.subtract).then_inc(l_hsl, 1)
            for n in range(NG):
                pool.wait_ge(q_hi, n + 1)
                pool.tensor_tensor(x3t[:, n * G:(n + 1) * G, 1, :], x1[:, n % 2, :].rearrange("p (b s) -> p b s", s=S),
                                   x3t[:, n * G:(n + 1) * G, 0, :].bitcast(F32), ALU.subtract).then_inc(q_lo, 1)
                pool.wait_ge(w3_hi, n + 1)
                pool.tensor_tensor(w3[:, n, 1, :], w3raw[:, n % 2, :], w3[:, n, 0, :].bitcast(F32), ALU.subtract).then_inc(w3_lo, 1)
            pool.sem_inc(e_in, CREDIT)
            pool.wait_ge(q_lo, NG)
            with pool.Fori(0, T3 // 2) as i:
                bring(xs3, x3t, batch3, i, e_in, e_xs)

        @block.scalar
        def _(act):
            for s in (sh_gelu, m_rest, e_rest):
                act.sem_inc(s, CREDIT)
            act.wait_ge(max_done, 1)
            act.activation(rt[:, 0, :], cond[:, :], ACT.Exp, bias=sc[:, 1:2]).then_inc(exp_done, 1)
            act.activation(sc[:, 7:8], kc[:, 0:1], ACT.Gelu_apprx_tanh)
            for g in range(NG):
                if g == 2:
                    act.wait_ge(ld_w[0], 16)
                    act.copy(ws[:, 0, :], stage[:, 0, :]).then_inc(ws_hi, 1)
                act.wait_ge(ld_x[g * LOADC // NG], 16)
                act.copy(xt[:, g * G:(g + 1) * G, 0, :], xraw[:, g * G:(g + 1) * G, :]).then_inc(x_hi, 1)

            def sh_gelu_chunk(n, c):
                act.wait_ge(sh_gate, n + 1)
                act.wait_ge(sh_mul, reusable(n))
                act.activation(gt[:, c % 2, :], bank(2 * (c % 2)), ACT.Gelu_apprx_tanh).then_inc(sh_gelu, 1)

            def sh_hi_chunk(n, c):
                act.wait_ge(sh_mul, finished(n))
                act.wait_ge(sh_down, reusable(n))
                act.copy(hh[:, c % 2, :], h[:, c % 2, :]).then_inc(sh_hi, 1)

            def expert_hi(e, buf, count):
                act.wait_ge(ld_w[buf], 16 * count)
                act.copy(wx[:, bass.ds(e, 1), 0, :].rearrange("p a n -> p (a n)"), stage[:, buf, :]).then_inc(wx_hi, 1)

            def sh_act(g, last, e, buf, count):
                for c in range(4):
                    if not (last and c == 3):
                        sh_gelu_chunk(4 * g + c + 1, (c + 1) % 4)
                    sh_hi_chunk(4 * g + c, c)
                    if c == 1 and e is not None:
                        expert_hi(e, buf, count)

            sh_gelu_chunk(0, 0)
            sh_act(0, False, 0, 1, 1)
            expert_hi(1, 0, 2)
            with act.Fori(0, (NG - 2) // 2) as i:
                sh_act(2 * i + 1, False, 2 * i + 2, 1, i + 2)
                sh_act(2 * i + 2, False, 2 * i + 3, 0, i + 3)
            sh_act(NG - 1, True, None, 0, 0)

            def gelu(t, par):
                act.wait_ge(m_gate, t + 1)
                act.wait_ge(m_mul, reusable(t))
                act.activation(gt[:, par, :], bank(2 * par), ACT.Gelu_apprx_tanh).then_inc(m_gelu, 1)

            def hi(t, par):
                act.wait_ge(m_turn, finished(t))
                act.wait_ge(m_down, reusable(t))
                act.copy(hh[:, par, :], bank(4 + par)).then_inc(m_hi, 1)

            def rest(t, par):
                act.wait_ge(m_down, finished(t))
                act.wait_ge(m_out, reusable(t))
                act.copy(yres[:, par, :], ps[:, 6 + par, F:2 * F]).then_inc(m_rest, 1)

            gelu(0, 0)
            gelu(1, 1)
            hi(0, 0)
            with act.Fori(0, T0 // 2 - 1) as i:
                for par in range(2):
                    gelu(2 * i + 2 + par, par)
                    hi(2 * i + 1 + par, 1 - par)
                    rest(2 * i + par, par)
            hi(T0 - 1, 1)
            rest(T0 - 2, 0)
            rest(T0 - 1, 1)

            act.wait_ge(ld_late, 16 * 6)
            act.copy(w1[:, 0, :], w1raw[:, :]).then_inc(w1_hi, 1)
            act.copy(b3h[:, :], b3raw[:, :]).then_inc(b3_hi, 1)

            def mix_first(c):
                act.wait_ge(ld_g[c], 16 * TOPK)
                act.activation(gath[:, c, 0, :], gath[:, c, 0, :], ACT.Copy, scale=wt[:, 0:1]).then_inc(mix1, 1)

            act.wait_ge(wt_done, 1)
            for g in range(-3, NG - 1):
                if g + 3 < NG and (g + 3) % 2 == 0:
                    mix_first((g + 3) // 2)
                if 0 <= g + 2 < NG:
                    n = g + 2
                    act.wait_ge(l_x1, n + 1)
                    if n >= 3:
                        act.wait_ge(l_o, n - 2)
                    act.copy(x1h[:, n % 3, :], x1[:, n % 3, :]).then_inc(l_x1h, 1)
                if 0 <= g + 1 < NG:
                    n = g + 1
                    act.wait_ge(l_hs, n + 1)
                    if n >= 2:
                        act.wait_ge(l_o, n - 1)
                    act.copy(hsh[:, n % 2, :], hs[:, :]).then_inc(l_hsh, 1)
            act.activation(sc[:, 7:8], kc[:, 0:1], ACT.Silu)
            act.wait_ge(l_hsl, NG)
            for n in range(0, F // 4, 2):
                act.wait_ge(gen_mm, n + 1)
                act.copy(wbot[:, :, gen_out(n):gen_out(n) + 4].rearrange("p b o -> p o b"),
                         bank(n % 8).rearrange("p (o b) -> p o b", o=4)).then_inc(gen_act, 1)
            for n in range(NG):
                act.wait_ge(q_x3, n + 1)
                act.copy(x3t[:, n * G:(n + 1) * G, 0, :], x1[:, n % 2, :].rearrange("p (b s) -> p b s", s=S)).then_inc(q_hi, 1)
                act.wait_ge(ld_w3[n % 2], 16 * (n // 2 + 1))
                act.copy(w3[:, n, 0, :], w3raw[:, n % 2, :]).then_inc(w3_hi, 1)

            def silu(t, par):
                act.wait_ge(e_in, finished(t))
                act.wait_ge(e_mul, reusable(t))
                act.activation(st[:, par, :], bank(par, I3), ACT.Silu).then_inc(e_silu, 1)

            def hi3(t, par):
                act.wait_ge(e_turn, finished(t))
                act.wait_ge(e_down, reusable(t))
                act.copy(h3h[:, par, :], bank(2 + par, I3)).then_inc(e_hi, 1)

            def rest3(i, par):
                t = 2 * i + par
                act.wait_ge(e_down, finished(t))
                act.wait_ge(e_out, reusable(t))
                act.copy(yres3[:, par, :], dbank(2 * (i % 2) + par + 4, F, 2 * F)).then_inc(e_rest, 1)

            silu(0, 0)
            silu(1, 1)
            hi3(0, 0)
            with act.Fori(0, T3 // 2 - 1) as i:
                for par in range(2):
                    silu(2 * i + 2 + par, par)
                    hi3(2 * i + 1 + par, 1 - par)
                    rest3(i, par)
            hi3(T3 - 1, 1)
            rest3(T3 // 2 - 1, 0)
            rest3(T3 // 2 - 1, 1)

        @block.vector
        def _(dve):
            for s in (sh_mul, m_mul, sh_lo, m_lo, e_mul, e_lo, sh_out, m_out, e_out):
                dve.sem_inc(s, CREDIT)
            steps = [0]

            def step(ins):
                steps[0] += 1
                ins.then_inc(route, 1)
                dve.wait_ge(route, steps[0])

            dve.wait_ge(ld_c, 16 * 4)
            desc = kc[:, C_DESC:C_DESC + E]
            iota = kc[:, C_IOTA:C_IOTA + N0]
            step(dve.tensor_reduce(sc[:, 0:1], cond[:, :], AX_X, ALU.max))
            dve.tensor_scalar(sc[:, 1:2], sc[:, 0:1], -1.0, None, ALU.mult).then_inc(max_done, 1)
            dve.tensor_copy(ident_r[:, 0:P], ident).then_inc(consts_done, 1)
            dve.tensor_scalar(ident_r[:, P:2 * P], ident, 0.0, None, ALU.mult).then_inc(consts_done, 1)
            dve.tensor_copy(ident_r[:, 2 * P:3 * P], ident).then_inc(consts_done, 1)
            dve.tensor_copy(ones_r[:, :], kc[0:2, C_ONE:C_ONE + P]).then_inc(consts_done, 1)
            step(dve.tensor_copy(kb[:, :], kc[:, C_U:C_U + 257]))
            step(dve.tensor_scalar(rt[:, 1, :], cond[:, :], sc[:, 0:1], None, ALU.is_equal))
            step(dve.tensor_tensor(rt[:, 2, :], rt[:, 1, :], desc, ALU.mult))
            step(dve.tensor_reduce(sc[:, 2:3], rt[:, 2, :], AX_X, ALU.max))
            step(dve.tensor_scalar(oh[:, 0, :], desc, sc[:, 2:3], None, ALU.is_equal))
            step(dve.scalar_tensor_tensor(out=rt[:, 3, :], in0=oh[:, 0, :], scalar=-3.0e38, in1=cond[:, :],
                                          op0=ALU.mult, op1=ALU.add))
            step(dve.tensor_reduce(sc[:, 3:4], rt[:, 3, :], AX_X, ALU.max))
            step(dve.tensor_scalar(rt[:, 4, :], rt[:, 3, :], sc[:, 3:4], None, ALU.is_equal))
            step(dve.tensor_tensor(rt[:, 5, :], rt[:, 4, :], desc, ALU.mult))
            step(dve.tensor_reduce(sc[:, 4:5], rt[:, 5, :], AX_X, ALU.max))
            step(dve.tensor_scalar(oh[:, 1, :], desc, sc[:, 4:5], None, ALU.is_equal))
            dve.tensor_tensor(pair[:, 0:E], oh[:, 0, :], oh[:, 1, :], ALU.add).then_inc(pair_done, 1)
            dve.tensor_copy(pair[:, E:2 * E], oh[:, 0, :]).then_inc(pair_done, 1)
            dve.memset(scan[:, :, :, 0:E], 0.0).then_inc(pair_done, 1)
            dve.wait_ge(ws_hi, 1)
            dve.tensor_tensor(ws[:, 1, :], stage[:, 0, :], ws[:, 0, :].bitcast(F32), ALU.subtract).then_inc(ws_lo, 1)
            for g in range(2):
                dve.wait_ge(x_hi, g + 1)
                dve.tensor_tensor(xt[:, g * G:(g + 1) * G, 1, :], xraw[:, g * G:(g + 1) * G, :],
                                  xt[:, g * G:(g + 1) * G, 0, :].bitcast(F32), ALU.subtract).then_inc(x_lo, 1)

            count = rc[:, 2 * E:4 * E].rearrange("p (l e) -> p l e", l=2)
            rank = rc[:, 0:2 * E].rearrange("p (l e) -> p l e", l=2)
            full = rt[:, 8:10, :]
            end = scan[:, 1, :, E:]

            def route_counts():
                dve.wait_ge(rank_done, 1)
                step(dve.tensor_copy(rc[:, :], bank(7, 4 * E)))
                step(dve.tensor_scalar(up4[:, :, :], count, float(TB - 1), None, ALU.add))
                step(dve.tensor_scalar(up4[:, :, :], up4[:, :, :], TB_SHIFT, TB_SHIFT, ALU.logical_shift_right, ALU.logical_shift_left))
                step(dve.tensor_copy(full, up4[:, :, :]))

            def route_ends():
                a, b = scan[:, 0, :, :], scan[:, 1, :, :]
                dve.wait_ge(pair_done, 3)
                step(dve.tensor_copy(a[:, :, E:], full))
                step(dve.tensor_tensor(b[:, :, E:], a[:, :, E:], a[:, :, E - 1:2 * E - 1], ALU.add))
                step(dve.tensor_tensor(a[:, :, E:], b[:, :, E:], b[:, :, E - 2:2 * E - 2], ALU.add))
                step(dve.tensor_tensor(b[:, :, E:], a[:, :, E:], a[:, :, E - 4:2 * E - 4], ALU.add))
                step(dve.tensor_tensor(slot[:, :, :], end, full, ALU.subtract))
                step(dve.tensor_tensor(rt[:, 10:12, :], slot[:, :, :], rank, ALU.add))

            def route_slots():
                step(dve.tensor_tensor(prod[:, 0, :], rt[:, 10, :], oh[:, 0, :], ALU.mult))
                step(dve.tensor_tensor(prod[:, 1, :], rt[:, 10, :], oh[:, 1, :], ALU.mult))
                step(dve.tensor_tensor(prod[:, 2, :], rt[:, 11, :], oh[:, 0, :], ALU.mult))
                step(dve.tensor_reduce(pos[:, :], prod[:, :, :], AX_X, ALU.add))
                step(dve.tensor_scalar(sel0[:, :], iota, pos[:, 0:1], None, ALU.is_equal))
                dve.scalar_tensor_tensor(out=sel0[:, :], in0=iota, scalar=pos[:, 1:2], in1=sel0[:, :],
                                         op0=ALU.is_equal, op1=ALU.add).then_inc(sel_done, 1)
                dve.tensor_scalar(sel3[:, :], iota[:, 0:N3], pos[:, 2:3], None, ALU.is_equal).then_inc(sel_done, 1)
                dve.tensor_scalar(before3[:, :], iota[:, 0:N3], pos[:, 2:3], None, ALU.is_gt).then_inc(sel_done, 1)

            def route_experts():
                t4 = kc[0:1, C_T4:C_T4 + 72]
                for l, (n, table) in enumerate(((72, expert0), (40, expert3))):
                    step(dve.tensor_tensor(cmp_t[0:1, :, 0:n], t4[:, None, 0:n].to_broadcast([1, E, n]),
                                           end[0:1, l, :].unsqueeze(2).to_broadcast([1, E, n]), ALU.is_ge))
                    step(dve.tensor_reduce(tmp3[0:1, 0, 0:n], cmp_t[0:1, :, 0:n].rearrange("p e t -> p t e"), AX_X, ALU.add))
                    step(dve.tensor_scalar(table[:, :], tmp3[0:1, 0, 0:n], float(E - 1), None, ALU.min))

            def route_tables():
                dve.wait_ge(slots_done, 1)
                step(dve.tensor_copy(batch0[:, :], ps[0:1, 7, 0:N0]))
                step(dve.tensor_copy(batch3[:, :], ps[0:1, 6, 0:N3]))
                step(dve.scalar_tensor_tensor(out=tmp3[:, 0, :], in0=kc[0:1, C_IOTA:C_IOTA + N3], scalar=float(B),
                                              in1=ps[0:1, 6, 2 * N3:3 * N3], op0=ALU.add, op1=ALU.subtract))
                step(dve.tensor_scalar(tmp3[:, 1, :], ps[0:1, 6, N3:2 * N3], -1.0, 1.0, ALU.mult, ALU.add))
                step(dve.tensor_tensor(tmp3[:, 0, :], tmp3[:, 0, :], tmp3[:, 1, :], ALU.mult))
                step(dve.tensor_tensor(row3[:, :], tmp3[:, 0, :], ps[0:1, 6, 0:N3], ALU.add))
                for k in range(TOPK):
                    dve.scalar_tensor_tensor(out=idx[:, :, k], in0=pos[:, k:k + 1].to_broadcast([P, ZC]), scalar=float(ZC),
                                             in1=kc[:, C_ZC:C_ZC + ZC], op0=ALU.mult, op1=ALU.add).then_inc(tables, 1)

            def sh_mul_chunk(n, c):
                dve.wait_ge(sh_up, n + 1)
                dve.wait_ge(sh_gelu, finished(n))
                dve.wait_ge(sh_lo, reusable(n))
                dve.tensor_tensor(h[:, c % 2, :], gt[:, c % 2, :], bank(2 * (c % 2) + 1), ALU.mult).then_inc(sh_mul, 1)

            def sh_lo_chunk(n, c):
                dve.wait_ge(sh_hi, n + 1)
                dve.tensor_tensor(hl[:, c % 2, :], h[:, c % 2, :], hh[:, c % 2, :].bitcast(F32), ALU.subtract).then_inc(sh_lo, 1)

            def sh_result(g):
                dve.wait_ge(sh_down, finished(4 * g + 3))
                cols = res[:, g * G:(g + 1) * G, :].rearrange("p b s -> p (b s)")
                dve.tensor_tensor(cols, bank(4 + g % 2), xraw[:, g * G:(g + 1) * G, :].rearrange("p b s -> p (b s)"),
                                  ALU.add).then_inc(sh_out, 1)

            sh_mul_chunk(0, 0)
            for g in range(NG):
                for c in range(4):
                    if not (g == NG - 1 and c == 3):
                        sh_mul_chunk(4 * g + c + 1, (c + 1) % 4)
                    sh_lo_chunk(4 * g + c, c)
                    if c == 2 and g >= 1:
                        sh_result(g - 1)
                if g < 4:
                    (route_counts, route_ends, route_slots, route_experts)[g]()
                if g == NG - 2:
                    route_tables()
            sh_result(NG - 1)

            dve.wait_ge(exp_done, 1)
            step(dve.tensor_reduce(sc[:, 5:6], rt[:, 0, :], AX_X, ALU.add))
            step(dve.reciprocal(sc[:, 6:7], sc[:, 5:6]))
            step(dve.tensor_scalar(rt[:, 12, :], rt[:, 0, :], sc[:, 6:7], None, ALU.mult))
            step(dve.tensor_tensor(prod[:, 0, :], rt[:, 12, :], oh[:, 0, :], ALU.mult))
            step(dve.tensor_tensor(prod[:, 1, :], rt[:, 12, :], oh[:, 1, :], ALU.mult))
            step(dve.tensor_reduce(rw[:, :], prod[:, 0:2, :], AX_X, ALU.add))
            step(dve.tensor_tensor(sc[:, 5:6], rw[:, 0:1], rw[:, 1:2], ALU.add))
            step(dve.reciprocal(sc[:, 6:7], sc[:, 5:6]))
            step(dve.tensor_scalar(rw[:, :], rw[:, :], sc[:, 6:7], None, ALU.mult))
            step(dve.tensor_scalar(rt[:, 13, 0:2], rw[:, :], 1.0 / LAYERS, None, ALU.mult))
            dve.scalar_tensor_tensor(out=wt[:, :], in0=rw[:, :], scalar=1.0 - 1.0 / LAYERS, in1=rt[:, 13, 0:2],
                                     op0=ALU.mult, op1=ALU.add).then_inc(wt_done, 1)

            def mul(t, par):
                dve.wait_ge(m_up, finished(t))
                dve.wait_ge(m_gelu, t + 1)
                dve.wait_ge(m_turn, reusable(t))
                dve.tensor_tensor(h[:, par, :], gt[:, par, :], bank(2 * par + 1), ALU.mult).then_inc(m_mul, 1)

            def lo(t, par):
                dve.wait_ge(m_hi, t + 1)
                dve.tensor_tensor(hl[:, par, :], bank(4 + par), hh[:, par, :].bitcast(F32), ALU.subtract).then_inc(m_lo, 1)

            def result(i, par):
                t = 2 * i + par
                dve.wait_ge(m_rest, finished(t))
                dve.tensor_tensor(ysb[:, bass.ds(i % 2, 1), par, :].rearrange("p a n -> p (a n)"), yres[:, par, :],
                                  bank(6 + par, F), ALU.add).then_inc(m_out, 1)

            mul(0, 0)
            mul(1, 1)
            lo(0, 0)
            with dve.Fori(0, T0 // 2 - 1) as i:
                dve.wait_ge(z_free, reusable(i))
                for par in range(2):
                    mul(2 * i + 2 + par, par)
                    lo(2 * i + 1 + par, 1 - par)
                    result(i, par)
            lo(T0 - 1, 1)
            dve.wait_ge(z_free, reusable(T0 // 2 - 1))
            result(T0 // 2 - 1, 0)
            result(T0 // 2 - 1, 1)

            lates = [0]

            def late_step(ins):
                lates[0] += 1
                ins.then_inc(late, 1)
                dve.wait_ge(late, lates[0])

            dve.wait_ge(ld_late, 16 * 6)
            dve.tensor_scalar(er[:, :], er_raw[:, :], 2.0, None, ALU.mult).then_inc(er_done, 1)
            dve.wait_ge(w1_hi, 1)
            dve.tensor_tensor(w1[:, 1, :], w1raw[:, :], w1[:, 0, :].bitcast(F32), ALU.subtract).then_inc(w1_lo, 1)
            late_step(dve.tensor_tensor(w2raw[:, :, :], w2raw[:, :, :], mask[:, None, :].to_broadcast([P, E, F]), ALU.mult))
            for k in range(3):
                ins = dve.tensor_copy(w2p[:, k, :, :], w2raw[:, :, :])
                if k == 2:
                    ins.then_inc(w2_parts, 3)
                else:
                    late_step(ins)
                    late_step(dve.tensor_tensor(w2raw[:, :, :], w2raw[:, :, :], w2p[:, k, :, :], ALU.subtract))
            for k in range(3):
                late_step(dve.tensor_copy(yp[:, k, :], yraw[:, :]))
                if k < 2:
                    late_step(dve.tensor_tensor(yraw[:, :], yraw[:, :], yp[:, k, :], ALU.subtract))
            late_step(dve.tensor_scalar(ysum[:, :], yp[:, 0, :], kc[:, C_Y:C_Y + 1], None, ALU.mult))
            late_step(dve.scalar_tensor_tensor(out=ysum[:, :], in0=yp[:, 1, :], scalar=kc[:, C_Y + 1:C_Y + 2], in1=ysum[:, :],
                                               op0=ALU.mult, op1=ALU.add))
            dve.scalar_tensor_tensor(out=ystk[:, :], in0=yp[:, 2, :], scalar=kc[:, C_Y + 2:C_Y + 3], in1=ysum[:, :],
                                     op0=ALU.mult, op1=ALU.add).then_inc(y_stk, 1)
            dve.wait_ge(b3_hi, 1)
            dve.tensor_tensor(b3l[:, :], b3raw[:, :], b3h[:, :].bitcast(F32), ALU.subtract).then_inc(b3_lo, 1)

            def mix(c):
                dve.wait_ge(mix1, c + 1)
                dve.scalar_tensor_tensor(out=gath[:, c, 0, :], in0=gath[:, c, 1, :], scalar=wt[:, 1:2],
                                         in1=gath[:, c, 0, :], op0=ALU.mult, op1=ALU.add).then_inc(mix2, 1)

            def cols(g):
                return res[:, :, 4 * g:4 * g + 4].rearrange("p b s -> p s b")

            def grp(ap):
                return ap.rearrange("p (s b) -> p s b", s=4)

            for g in range(-3, NG):
                if g + 3 < NG and (g + 3) % 2 == 0:
                    mix((g + 3) // 2)
                if 0 <= g + 2 < NG:
                    n = g + 2
                    dve.wait_ge(l_turn, n + 1)
                    if n >= 3:
                        dve.wait_ge(l_x1l, n - 2)
                        dve.wait_ge(l_x2, n - 2)
                    dve.tensor_tensor(grp(x1[:, n % 3, :]), grp(bank(n % 2)), cols(n), ALU.add).then_inc(l_x1, 1)
                if 0 <= g + 1 < NG:
                    n = g + 1
                    dve.wait_ge(l_a, n + 1)
                    if n >= 1:
                        dve.wait_ge(l_hsl, n)
                    dve.tensor_tensor(grp(hs[:, :]), grp(bank(2 + n % 2)), er[:, None, :].to_broadcast([P, 4, B]), ALU.mult).then_inc(l_hs, 1)
                if g >= 0:
                    dve.wait_ge(l_o, g + 1)
                    dve.scalar_tensor_tensor(out=cols(g), in0=grp(bank(4 + g % 2)), scalar=b1[:, 0:1], in1=grp(x1[:, g % 3, :]),
                                             op0=ALU.add, op1=ALU.add).then_inc(l_x2, 1)
            dve.wait_ge(l_hsl, NG)
            for n in range(1, F // 4, 2):
                dve.wait_ge(gen_mm, n + 1)
                dve.tensor_copy(wbot[:, :, gen_out(n):gen_out(n) + 4].rearrange("p b o -> p o b"),
                                bank(n % 8).rearrange("p (o b) -> p o b", o=4)).then_inc(gen_dve, 1)
            dve.wait_ge(l_x2, NG)
            for n in range(NG):
                dve.wait_ge(q_mm, n + 1)
                if n >= 2:
                    dve.wait_ge(q_lo, n - 1)
                dve.scalar_tensor_tensor(out=x1[:, n % 2, :], in0=bank(n % 4), scalar=b2[:, 0:1],
                                         in1=res[:, n * G:(n + 1) * G, :].rearrange("p b s -> p (b s)"),
                                         op0=ALU.add, op1=ALU.add).then_inc(q_x3, 1)

            def mul3(t, par):
                dve.wait_ge(e_silu, t + 1)
                dve.wait_ge(e_turn, reusable(t))
                dve.tensor_tensor(h3[:, par, :], st[:, par, :], ps[:, par, I3:2 * I3], ALU.mult).then_inc(e_mul, 1)

            def lo3(t, par):
                dve.wait_ge(e_hi, t + 1)
                dve.tensor_tensor(h3l[:, par, :], bank(2 + par, I3), h3h[:, par, :].bitcast(F32), ALU.subtract).then_inc(e_lo, 1)

            def result3(i, par):
                dve.wait_ge(e_rest, finished(2 * i + par))
                dve.tensor_tensor(osb[:, bass.ds(i % 2, 1), par, :].rearrange("p a n -> p (a n)"), yres3[:, par, :],
                                  dbank(2 * (i % 2) + par + 4), ALU.add).then_inc(e_out, 1)

            mul3(0, 0)
            mul3(1, 1)
            lo3(0, 0)
            with dve.Fori(0, T3 // 2 - 1) as i:
                dve.wait_ge(out_free, reusable(i))
                for par in range(2):
                    mul3(2 * i + 2 + par, par)
                    lo3(2 * i + 1 + par, 1 - par)
                    result3(i, par)
            lo3(T3 - 1, 1)
            dve.wait_ge(out_free, reusable(T3 // 2 - 1))
            result3(T3 // 2 - 1, 0)
            result3(T3 // 2 - 1, 1)

        @block.tensor
        def _(pe):
            for s in (sh_down, m_turn, m_down, e_turn, e_down):
                pe.sem_inc(s, CREDIT)

            def split_product(out, w, m, start=True, stop=True):
                for n, (a, b) in enumerate(((0, 0), (0, 1), (1, 0))):
                    last = pe.matmul(out, w[a], m[b], start=start and n == 0, stop=stop and n == 2)
                return last

            pe.wait_ge(pair_done, 2)
            pe.wait_ge(route, 1)
            pe.matmul(ps[:, 7, 0:2 * E], before, pair[:, :], start=True, stop=True)
            pe.matmul(ps[:, 7, 2 * E:4 * E], ones, pair[:, :], start=True, stop=True).then_inc(rank_done, 1)

            def sh_in(g, n, c):
                if c == 0:
                    pe.wait_ge(x_lo, g + 1)
                pe.wait_ge(sh_mul, reusable(n))
                m = [xt[:, bass.ds(g * G, G), k, :] for k in range(2)]
                for what, sem_ in ((0, sh_gate), (1, sh_up)):
                    w = [ws[:, k, what * I0 + c * P:what * I0 + (c + 1) * P] for k in range(2)]
                    out = bank(2 * (c % 2) + what).rearrange("p (b s) -> p b s", s=S)
                    split_product(out, w, m).then_inc(sem_, 1)

            def sh_down_(g, par, n, c):
                if c == 0:
                    pe.wait_ge(sh_out, reusable(g))
                pe.wait_ge(sh_lo, finished(n))
                w = [ws[:, k, 2 * I0 + c * P:2 * I0 + (c + 1) * P] for k in range(2)]
                split_product(bank(4 + par), w, (hh[:, c % 2, :], hl[:, c % 2, :]), start=c == 0, stop=c == 3).then_inc(sh_down, 1)

            def sh_pe(g, par, last):
                for c in range(4):
                    if c < 2:
                        sh_in(g, 4 * g + c + 2, c + 2)
                    elif not last:
                        sh_in(g + 1, 4 * g + c + 2, c - 2)
                    sh_down_(g, par, 4 * g + c, c)

            pe.wait_ge(ws_lo, 1)
            sh_in(0, 0, 0)
            sh_in(0, 1, 1)
            with pe.Fori(0, NG // 2 - 1) as i:
                sh_pe(2 * i, 0, False)
                sh_pe(2 * i + 1, 1, False)
            pe.wait_ge(sel_done, 3)
            pe.matmul(ps[0:1, 7, 0:N0], batch, sel0[:, :], start=True, stop=True)
            pe.matmul(ps[0:1, 6, 0:N3], batch, sel3[:, :], start=True, stop=True)
            pe.matmul(ps[0:1, 6, N3:2 * N3], ones[:, 0:1], sel3[:, :], start=True, stop=True)
            pe.matmul(ps[0:1, 6, 2 * N3:3 * N3], ones[:, 0:1], before3[:, :], start=True, stop=True).then_inc(slots_done, 1)
            sh_pe(NG - 2, 0, False)
            sh_pe(NG - 1, 1, True)

            def experts(table, start, count):
                _, e = nc.values_load_multi_w_load_instructions(
                    table[0:1, bass.ds(start, count)], engines=PE, min_val=0, max_val=E - 1,
                    skip_runtime_bounds_check_because="the table holds experts")
                return e

            def both_products(out, x, w, e, inner, start, last_stop):
                halves = out.rearrange("p (k n) -> p k n", k=2)
                for c in range(inner // P):
                    down = w[:, bass.ds(e, 1), :, 2 * inner + c * P:2 * inner + (c + 1) * P].rearrange("p a k n -> p (a k) n")
                    for n, v in enumerate(x):
                        last = pe.matmul(halves, v[:, c * P:(c + 1) * P], down, start=start and c == 0 and n == 0,
                                         stop=last_stop and c == inner // P - 1 and n == 1, skip_group_check=True)
                return last

            def weights(w, e, k, a, b):
                return w[:, bass.ds(e, 1), k, a:b].rearrange("p a n -> p (a n)")

            def gate_up(t, par, e):
                pe.wait_ge(m_xs, t + 1)
                pe.wait_ge(m_mul, reusable(t))
                x = [xs[:, par, k, :, :].rearrange("p q s -> p (q s)") for k in range(2)]
                for what, sem_ in ((0, m_gate), (1, m_up)):
                    w = [weights(wx, e, k, what * I0, (what + 1) * I0) for k in range(2)]
                    split_product(bank(2 * par + what), x, w).then_inc(sem_, 1)

            def turn(t, par):
                pe.wait_ge(m_mul, finished(t))
                pe.wait_ge(m_lo, reusable(t))
                for c in range(4):
                    last = pe.transpose(bank(4 + par)[:, c * P:(c + 1) * P], h[:, par, c * P:(c + 1) * P], ident)
                last.then_inc(m_turn, 1)

            def down(t, par, e):
                pe.wait_ge(m_lo, finished(t))
                pe.wait_ge(m_out, reusable(t))
                both_products(bank(6 + par, 2 * F), (hh[:, par, :], hl[:, par, :]), wx, e, I0, True, True).then_inc(m_down, 1)

            pe.wait_ge(sh_out, finished(NG - 1))
            pe.wait_ge(tables, 2)
            pe.wait_ge(wx_lo, E)
            e0, e1 = experts(expert0, 0, 2)
            gate_up(0, 0, e0)
            gate_up(1, 1, e1)
            turn(0, 0)
            with pe.Fori(0, T0 // 2 - 1) as i:
                e = experts(expert0, 2 * i, 4)
                for par in range(2):
                    gate_up(2 * i + 2 + par, par, e[2 + par])
                    turn(2 * i + 1 + par, 1 - par)
                    down(2 * i + par, par, e[par])
            e0, e1 = experts(expert0, T0 - 2, 2)
            turn(T0 - 1, 1)
            down(T0 - 2, 0, e0)
            down(T0 - 1, 1, e1)

            pe.wait_ge(m_out, finished(T0 - 1))
            pe.wait_ge(w1_lo, 1)
            A_, WB, BB = ([w1[:, k, n * F:(n + 1) * F] for k in range(2)] for n in range(3))
            for g in range(-2, NG):
                if g + 2 < NG:
                    n = g + 2
                    pe.wait_ge(mix2, n // 2 + 1)
                    if n >= 2:
                        pe.wait_ge(l_x1, n - 1)
                    for s in range(4):
                        col = (4 * (n % 2) + s) * F
                        last = pe.transpose(bank(n % 2)[:, s * P:(s + 1) * P], gath[:, n // 2, 0, col:col + F], ident)
                    last.then_inc(l_turn, 1)
                if 0 <= g + 1 < NG:
                    n = g + 1
                    pe.wait_ge(l_x1l, n + 1)
                    if n >= 2:
                        pe.wait_ge(l_hs, n - 1)
                    split_product(bank(2 + n % 2), A_, (x1h[:, n % 3, :], x1l[:, n % 3, :])).then_inc(l_a, 1)
                if g >= 0:
                    if g >= 2:
                        pe.wait_ge(l_x2, g - 1)
                    split_product(bank(4 + g % 2), WB, (x1h[:, g % 3, :], x1l[:, g % 3, :]), stop=False)
                    pe.wait_ge(l_hsl, g + 1)
                    split_product(bank(4 + g % 2), BB, (hsh[:, g % 2, :], hsl[:, g % 2, :]), start=False).then_inc(l_o, 1)

            pe.wait_ge(w2_stack, 16 * 2 * len(W_PART))
            pe.wait_ge(y_stk, 1)
            pe.wait_ge(l_x2, NG)
            for n in range(0, F // 4, 2):
                if n >= 8:
                    pe.wait_ge(gen_act, n // 2 - 3)
                    pe.wait_ge(gen_dve, n // 2 - 3)
                for k in range(4):
                    for half in range(2):
                        row = 64 * half
                        last = pe.matmul(ps[:, (n + half) % 8, k * B:(k + 1) * B], wstk[row:row + KY, 2 * n + k, :],
                                         ystk[row:row + KY, :], start=True, stop=True)
                last.then_inc(gen_mm, 2)
            pe.wait_ge(gen_act, F // 8)
            pe.wait_ge(gen_dve, F // 8)
            for n in range(NG):
                if n >= 4:
                    pe.wait_ge(q_x3, n - 3)
                for k in range(G):
                    b = n * G + k
                    last = pe.matmul(ps[:, n % 4, k * S:(k + 1) * S], wbot[:, b, :], res[:, b, :], start=True, stop=True)
                last.then_inc(q_mm, 1)

            def gate_up3(t, par, ybank, e):
                pe.wait_ge(e_xs, t + 1)
                pe.wait_ge(e_mul, reusable(t))
                x = [xs3[:, par, k, :, :].rearrange("p q s -> p (q s)") for k in range(2)]
                for k in range(2):
                    pe.matmul(dbank(ybank, 0, 2 * F), x[k], ident_r[:, k * P:(k + 2) * P], start=k == 0, stop=False,
                              skip_group_check=True)
                w = [weights(w3, e, k, 0, 2 * I3) for k in range(2)]
                split_product(bank(par), x, w, stop=False)
                pe.matmul(bank(par), ones_r[:, :], b3[:, bass.ds(e, 1), 0:2 * I3].rearrange("p a n -> p (a n)"),
                          start=False, stop=True).then_inc(e_in, 1)

            def turn3(t, par):
                pe.wait_ge(e_mul, finished(t))
                pe.wait_ge(e_lo, reusable(t))
                for c in range(2):
                    last = pe.transpose(bank(2 + par)[:, c * P:(c + 1) * P], h3[:, par, c * P:(c + 1) * P], ident)
                last.then_inc(e_turn, 1)

            def down3(t, par, ybank, e):
                pe.wait_ge(e_lo, finished(t))
                both_products(dbank(ybank, 0, 2 * F), (h3h[:, par, :], h3l[:, par, :]), w3, e, I3, False, False)
                pe.matmul(dbank(ybank), ones_r[:, :], b3[:, bass.ds(e, 1), 2 * I3:B3].rearrange("p a n -> p (a n)"),
                          start=False, stop=True, skip_group_check=True).then_inc(e_down, 1)

            pe.wait_ge(q_x3, NG)
            pe.wait_ge(w3_lo, E)
            pe.wait_ge(b3_rows, 48)
            pe.wait_ge(consts_done, 4)
            e0, e1 = experts(expert3, 0, 2)
            gate_up3(0, 0, 4, e0)
            gate_up3(1, 1, 5, e1)
            turn3(0, 0)
            with pe.Fori(0, T3 // 2 - 1) as i:
                e = experts(expert3, 2 * i, 4)
                for par in range(2):
                    pe.wait_ge(e_out, reusable(2 * i + par))
                    gate_up3(2 * i + 2 + par, par, 2 * ((i + 1) % 2) + par + 4, e[2 + par])
                    turn3(2 * i + 1 + par, 1 - par)
                    down3(2 * i + par, par, 2 * (i % 2) + par + 4, e[par])
            e0, e1 = experts(expert3, T3 - 2, 2)
            turn3(T3 - 1, 1)
            last_pair = T3 // 2 - 1
            down3(T3 - 2, 0, 4 + 2 * (last_pair % 2), e0)
            down3(T3 - 1, 1, 5 + 2 * (last_pair % 2), e1)


def kernel(**inputs):
    import numpy as _np
    import concourse.bacc as _bacc
    from concourse import mybir as _mybir
    from concourse.bass_utils import run_bass_kernel_spmd as _run

    v = {k: _np.asarray(a) for k, a in inputs.items()}
    x, cond = v["x"], v["cond_8"]

    def mlp(gate, up, down, inner):
        return _np.concatenate([gate, up, down.reshape(inner // P, P, F).transpose(1, 0, 2).reshape(P, inner)], axis=1)

    w0 = _np.stack([mlp(g, u, d, I0) for g, u, d in zip(v["L0_cond_skill_gate"], v["L0_cond_skill_up"], v["L0_cond_skill_down"])]
                   + [mlp(v["L0_cond_shared_gate"], v["L0_cond_shared_up"], v["L0_cond_shared_down"], I0)])
    w3 = _np.stack([mlp(u.T, g.T, d.T, I3) for u, g, d in zip(v["L3_cond_W_up"], v["L3_cond_W_gate"], v["L3_cond_W_down"])])
    w1 = _np.concatenate([v["L1_cond_As"].reshape(P, F).T, v["L1_cond_W_base"].T,
                          v["L1_cond_Bs"].transpose(0, 2, 1).reshape(P, F)], axis=1)
    rows = _np.zeros((2, 64, B), cond.dtype)
    rows[:, 0:KY] = _np.tile(cond.T, (KY // E, 1))
    arrays = {
        "constants": constants(),
        "cond": cond,
        "x_feature": x.transpose(2, 0, 1),
        "w_layer0": w0,
        "w_layer1": w1,
        "cond_er": _np.repeat(cond.T, R, axis=0),
        "b_layer1": v["L1_cond_b_base"].reshape(F, 1),
        "w_layer2": v["L2_cond_weight"].transpose(1, 0, 2),
        "mask": v["L2_cond_mask"],
        "cond_rows": rows.reshape(P, B),
        "b_layer2": v["L2_cond_bias"].reshape(F, 1),
        "w_layer3": w3,
        "b_layer3": _np.concatenate([v["L3_cond_b_up"], v["L3_cond_b_gate"], v["L3_cond_b_down"]], axis=1).reshape(P, E * B3 // P),
    }
    nc = _bacc.Bacc("TRN2", target_bir_lowering=False, num_devices=1)
    arrays = {"in_" + k: _np.ascontiguousarray(a) for k, a in arrays.items()}
    args = [nc.dram_tensor(k, a.shape, _mybir.dt.from_np(a.dtype), kind="ExternalInput").ap() for k, a in arrays.items()]
    args.append(nc.dram_tensor("out", (N3, S, F), _mybir.dt.float32, kind="ExternalOutput").ap())
    build(nc, *args)
    r = _run(nc, [arrays], core_ids=[0])
    return r.results[0]["out"][0:B]
```

```python
from contextlib import ExitStack

import numpy as np

import concourse.bass as bass
from concourse import mybir

ALU = mybir.AluOpType
ACT = mybir.ActivationFunctionType
AX_X = mybir.AxisListType.X
F32 = mybir.dt.float32
F32R = mybir.dt.float32r
BF16 = mybir.dt.bfloat16
I32 = mybir.dt.int32
POOL = (mybir.EngineType.Pool,)
PE = (mybir.EngineType.PE,)
ACTE = (mybir.EngineType.Activation,)
DVE = (mybir.EngineType.DVE,)

P = 128
B, S, F = 128, 32, 128
E, I0, I3, R = 8, 512, 256, 16
TOPK, LAYERS = 2, 12
TB = P // S
TB_SHIFT = TB.bit_length() - 1
T0 = (B * TOPK + E * (TB - 1)) // TB
T3 = (B + E * (TB - 1)) // TB
N0, N3 = T0 * TB, T3 * TB
G = 16
NG = B // G
W0 = 3 * I0
W3 = 3 * I3
B3 = 2 * I3 + F
ZC = P // G
SC = S // ZC
LOADC = 4
CREDIT = 2

C_ID, C_U, C_ONE, C_B = 0, 128, 256, 384
C_DESC = 512
C_IOTA = C_DESC + E
C_T4 = C_IOTA + N0
C_ZC = C_T4 + 72
C_Y = C_ZC + 1
C_Q = C_Y + 3
C_S = C_Q + TB
C_REP = C_S + 1
C_G = C_REP + P
C_END = C_G + NG
W_PART = (0, 1, 2, 0, 1, 0)
Y_PART = (0, 0, 0, 1, 1, 2)
KY = E * len(W_PART)
OB = 512 // B
FILLS = F // OB


PREP_FIRST, PREPARED = 24, 29


def finished(n):
    return n + 1 + CREDIT


def reusable(n):
    return n + 1


def constants():
    c = np.zeros((P, C_END), np.float32)
    p = np.arange(P)
    c[:, C_ID:C_ID + P] = np.eye(P)
    c[:, C_U:C_U + P] = p[:, None] < p[None, :]
    c[:, C_ONE:C_ONE + P] = 1
    c[:, C_B:C_B + P] = p[:, None]
    c[:, C_Q:C_Q + TB] = p[:, None] // S == np.arange(TB)
    c[:, C_S] = p % S
    c[:, C_DESC:C_DESC + E] = E - np.arange(E)
    c[:, C_IOTA:C_IOTA + N0] = np.arange(N0)
    c[:, C_T4:C_T4 + 72] = TB * np.arange(72)
    c[:, C_ZC] = p % ZC
    c[:, C_REP:C_REP + P] = p[:, None] % G == p[None, :] // ZC
    c[:, C_G:C_G + NG] = p[:, None] // G == np.arange(NG)
    for row in range(KY):
        for half in (0, 64):
            c[half + row, C_Y + Y_PART[row // E]] = 1
    return c


def build(nc, consts_d, cond_d, xt_d, w0_d, w1_d, cond_er_d, b1_d, w2_d, mask_d, condt_d, b2_d, w3_d, b3_d, out_d):
    z_d = nc.dram_tensor("layer0_slots", (N0 * S, F), F32, kind="Internal").ap()

    w2_split = nc.dram_tensor("layer2_weight_parts", (3, E, P, F), BF16, kind="Internal").ap()
    b3_split = nc.dram_tensor("layer3_bias_split", (2, P, E * B3 // P), F32, kind="Internal").ap()

    with ExitStack() as ctx:
        def sb(name, shape, dt=F32):
            return ctx.enter_context(nc.sbuf_tensor(name, shape, dt))

        def sem(name):
            return ctx.enter_context(nc.semaphore(name))

        SIZE_A, SIZE_B, SIZE_C, SIZE_D, SIZE_W = 98304, 32768, 16384, 24576, 24576
        SIZE_ALL = SIZE_A + SIZE_B + SIZE_C + SIZE_D + SIZE_W
        sb("arena", [P, SIZE_ALL // 4])
        A = nc.sbuf_base - SIZE_ALL
        RB = A + SIZE_A
        RC = RB + SIZE_B
        RD = RC + SIZE_C
        RW = RD + SIZE_D

        def at(name, offset, shape, dt=F32):
            return nc.alloc_sbuf_tensor_at(name, shape, dt, offset=offset)

        wx = at("expert_weights", A, [P, E, 2, W0], F32R)
        xt = at("x_hi_lo", RB, [P, B, 2, S], F32R)
        xraw = at("x_raw", RC, [P, B, S])
        res = at("residual", RC, [P, B, S])
        ws = at("shared_weights", RD, [P, 2, W0], F32R)
        stage = at("weight_stage", RD + 12288, [P, 2, W0])
        gt = at("gelu_out", RW, [P, 2, 512])
        h = at("hidden", RW + 4096, [P, 2, 512])
        hh = at("hidden_hi", RW + 8192, [P, 2, 512], F32R)
        hl = at("hidden_lo", RW + 12288, [P, 2, 512], F32R)
        xs = at("tile_x", RW + 16384, [P, 2, 2, TB, S], F32R)
        ysb = at("tile_out", RW + 18432, [P, 2, 2, F])
        yres = at("tile_rest", RW + 20480, [P, 2, F])
        cmp_t = at("tile_compare", RW + 20480, [P, E, 72])
        tmp3 = at("slot_tmp3", RW + 16384, [P, 2, N3])
        sel0 = at("slot_onehot0", RW + 22784, [P, N0], BF16)
        sel3 = at("slot_onehot3", RW + 23360, [P, N3], BF16)
        before3 = at("slot_before3", RW + 23680, [P, N3], BF16)
        w2raw = at("w2_raw", RD, [P, E, F])
        w2p = at("w2_parts", RD + 4096, [P, 3, E, F], BF16)
        mask = at("mask", RD + 12288, [P, F])
        w1raw = at("w1_raw", RD + 12800, [P, 3 * F])
        er_raw = at("cond_er_raw", RD + 14336, [P, B])
        yraw = at("cond_t_raw", RD + 14848, [P, B])
        yp = at("cond_t_parts", RD + 15360, [P, 3, B], BF16)
        ysum = at("cond_t_sum", RD + 16128, [P, B])
        b3raw = at("b3_raw", RD + 16896, [P, E * B3 // P])
        b3h = at("b3_hi", RD + 17408, [P, E * B3 // P], F32R)
        b3l = at("b3_lo", RD + 17920, [P, E * B3 // P], F32R)
        wbot = at("w_bot", A, [P, B, F])
        wstk = at("w2_stack", RD, [64 + KY, F // 2, F], BF16)
        gath = at("gathered", A + 90112, [P, 3, TOPK, SC * F])
        hs = at("adapter_h", A + 102400, [P, 512])
        hsl = at("adapter_lo", A + 104448, [P, 2, 512], F32R)
        x1 = at("x1", A + 108544, [P, 3, 512])
        x1h = at("x1_hi", A + 114688, [P, 3, 512], F32R)
        x1l = at("x1_lo", A + 120832, [P, 3, 512], F32R)
        hsh = at("adapter_hi", A + 126976, [P, 2, 512], F32R)
        tok = at("layer2_tokens", RW + 20480, [P, 2, 4, P])
        x3s = at("x3_slots", RW, [P, N3 + 2 * TB, S])
        x3g = at("x3_group", RD + 16384, [P, 3, G, S])
        w3 = at("w3_hi_lo", A + 65536, [P, E, 2, W3], F32R)
        b3 = at("b3_up_gate", A, [2, E, 2 * I3], F32R)
        b3d = at("b3_down", A + 114688, [2, E, F], F32R)
        w3raw = at("w3_raw", RD, [P, 2, W3])
        RH = A + 32768
        st = at("silu_out", RH, [P, 2, I3])
        h3 = at("hidden3", RH + 2048, [P, 2, I3])
        h3h = at("hidden3_hi", RH + 4096, [P, 2, I3], F32R)
        h3l = at("hidden3_lo", RH + 6144, [P, 2, I3], F32R)
        xs3 = at("tile_x3", RH + 8192, [P, 4, 2, P], F32R)
        osb = at("tile_out3", RH + 12288, [P, 4, F])
        yres3 = at("tile_rest3", RH + 14336, [P, 2, F])

        kc = sb("constants", [P, C_END])
        kb = sb("constants_bf16", [P, 4 * P], BF16)
        ident = kc[:, C_ID:C_ID + P]
        ident_b, before, ones, batch = (kb[:, n * P:(n + 1) * P] for n in range(4))
        ident_r = sb("identity_zero_identity", [P, 3 * P], F32R)
        ones_r = sb("ones_r", [2, P], F32R)
        cond = sb("cond", [P, E])
        rt = sb("route_scratch", [P, 24, E])
        oh = sb("onehots", [P, 2, E])
        pair = sb("pairs_bf16", [P, 2 * E], BF16)
        rc = sb("rank_count", [P, 4 * E])
        scan = sb("scan", [P, 2, 2, 2 * E])
        up4 = sb("rounded_up", [P, 2, E], I32)
        slot = sb("slot", [P, 2, E])
        prod = sb("prod", [P, 3, E])
        pos = sb("pos", [P, 3])
        vals = sb("pos_and_weight_by_group", [P, 2, NG, TOPK])
        idx = sb("gather_rows", [P, NG, TOPK], I32)
        wtx = sb("gather_weights", [P, NG, TOPK])
        rw = sb("rw", [P, 2])
        wt = sb("top_weights", [P, 2])
        sc = sb("scalars", [P, 8])
        batch0 = sb("slot_batch0", [1, N0], I32)
        slot3 = sb("batch_slot3", [1, B], I32)
        pos3 = sb("slot3_bf16", [P, 1], BF16)
        expert0 = sb("tile_expert0", [1, 72], I32)
        expert3 = sb("tile_expert3", [1, 40], I32)
        row3 = sb("out_rows3", [P, T3], I32)
        row_now = sb("out_row_of_store", [P, 4], I32)
        w1 = sb("w1_hi_lo", [P, 2, 3 * F], F32R)
        er = sb("cond_er", [P, B])
        ystk = sb("cond_stack", [P, B], BF16)
        b1 = sb("b1", [P, 1])
        b2 = sb("b2", [P, 1])

        ps = ctx.enter_context(nc.psum_tensor("ps", [P, 8, 512], F32))

        def bank(n, width=512):
            return ps[:, n, 0:width]

        def gen_out(n):
            return F // 2 * (n % 2) + OB * (n // 2)

        W3_STEP = {1: (0,), 2: (1,), 3: (2,), 4: (3,), NG - 2: (4,), NG - 1: (5,), NG: (6, 7)}

        W3_LO_ODD = {4: 1, 5: 3, NG - 1: 5, NG: 7}

        def w3_raw(e):
            return w3[:, e, 1, :].bitcast(F32) if e < E - 2 else w3raw[:, e - (E - 2), :]

        GEN_STEP = {-3: range(0, 22, 2), -2: range(22, 26, 2), -1: range(26, 28, 2), 0: range(28, 32, 2)}

        def gen_bank(n):
            return 2 + n % 6 if n < 30 else 4 + n % 2

        ld_c = sem("ld_constants")
        ld_gu = sem("ld_shared_gate_up")
        ld_x = [sem(f"ld_x{i}") for i in range(LOADC)]
        ld_w = [sem(f"ld_stage{i}") for i in range(2)]
        stage_free = sem("stage_free")
        ld_late = sem("ld_late")
        ld_g = [sem(f"ld_gather{i}") for i in range(3)]
        ld_w3 = [sem(f"ld_w3_{i}") for i in range(E)]
        route = sem("route_step")
        late = sem("late_step")
        exp_done = sem("exp_done")
        max_done = sem("max_done")
        pair_done = sem("pair_done")
        rank_done = sem("rank_done")
        sel_done = sem("sel_done")
        slots_done = sem("slots_done")
        vals_done = sem("vals_done")
        tables = sem("tables_done")
        consts_done = sem("consts_done")
        x_hi = sem("x_hi")
        x_lo = sem("x_lo")
        ws_hi = sem("ws_hi")
        ws_lo = sem("ws_lo")
        wx_hi = sem("wx_hi")
        wx_lo = sem("wx_lo")
        sh_gate, sh_up, sh_gelu, sh_mul, sh_hi, sh_lo, sh_down, sh_out = (
            sem("sh_" + n) for n in ("gate", "up", "gelu", "mul", "hi", "lo", "down", "out"))
        (m_xs, m_gate, m_up, m_gelu, m_mul, m_turn, m_hi, m_lo, m_down, m_rest, m_out) = (
            sem("moe_" + n) for n in ("xs", "gate", "up", "gelu", "mul", "turn", "hi", "lo", "down", "rest", "out"))
        z_done = sem("z_stored")
        z_free = sem("z_free")
        w2_parts, w2_split_done, w2_stack = (sem("w2_" + n) for n in ("parts", "split", "stack"))
        w1_hi, w1_lo = sem("w1_hi"), sem("w1_lo")
        y_stk, er_done = sem("y_stack"), sem("er_done")
        gen_mm, gen_act, gen_dve = sem("gen_mm"), sem("gen_act"), sem("gen_dve")
        x3_clear = sem("x3_slots_cleared")
        mix1, mix2 = sem("mix1"), sem("mix2")
        (l_turn, l_x1, l_x1h, l_x1l, l_a, l_hs, l_hsh, l_hsl, l_o, l_x2) = (
            sem("l1_" + n) for n in ("turn", "x1", "x1h", "x1l", "a", "hs", "hsh", "hsl", "o", "x2"))
        b3_hi, b3_lo, b3_rows = sem("b3_hi"), sem("b3_lo"), sem("b3_rows")
        w3_hi, w3_lo = [sem("w3_hi_act"), sem("w3_hi_dve")], [sem("w3_lo_even"), sem("w3_lo_odd")]
        q_mm, q_tok, q_turn, q_x3g, q_x3 = (sem("l2_" + n) for n in ("mm", "tok", "turn", "x3_group", "x3"))
        (e_xhi, e_xlo, e_in, e_silu, e_mul, e_turn, e_hi, e_lo, e_down, e_rest, e_out) = (
            sem("l3_" + n) for n in ("x_hi", "x_lo", "in", "silu", "mul", "turn", "hi", "lo", "down", "rest", "out"))
        out_free = sem("out_free")
        last_placed = sem("l2_last_placed")
        row_set = sem("out_row_set")
        stored = [sem(f"out_stored{i}") for i in range(4)]

        block = ctx.enter_context(nc.Block())

        @block.sync
        def _(sp):
            sp.sem_inc(z_free, CREDIT)
            sp.sem_inc(out_free, 4)
            nb = B // LOADC
            sp.dma_start(stage[:, 0, 0:2 * I0], w0_d[E, :, 0:2 * I0]).then_inc(ld_gu, 16)
            sp.dma_start(xraw[:, 0:nb, :], xt_d[:, 0:nb, :]).then_inc(ld_x[0], 16)
            sp.dma_start(kc[:, :], consts_d).then_inc(ld_c, 16)
            sp.dma_start(cond[:, :], cond_d).then_inc(ld_c, 16)
            sp.dma_start(stage[:, 0, 2 * I0:], w0_d[E, :, 2 * I0:]).then_inc(ld_w[0], 16)
            sp.dma_start(b1[:, :], b1_d).then_inc(ld_c, 16)
            sp.dma_start(b2[:, :], b2_d).then_inc(ld_c, 16)
            for i in range(1, LOADC):
                sp.dma_start(xraw[:, i * nb:(i + 1) * nb, :], xt_d[:, i * nb:(i + 1) * nb, :]).then_inc(ld_x[i], 16)
            with sp.Fori(0, E // 2) as i:
                for half in range(2):
                    e = 2 * i + half
                    sp.wait_ge(stage_free, e + 1)
                    if half == 1:
                        sp.wait_ge(ws_lo, 2)
                    sp.dma_start(stage[:, 1 - half, :], w0_d[bass.ds(e, 1)].rearrange("a p n -> p (a n)")).then_inc(
                        ld_w[1 - half], 16)
            sp.wait_ge(wx_lo, E)
            sp.wait_ge(sh_down, finished(NG * 4 - 1))
            for dst, src in ((w2raw[:, :, :], w2_d), (mask[:, :], mask_d), (w1raw[:, :], w1_d), (er_raw[:, :], cond_er_d),
                             (yraw[:, :], condt_d), (b3raw[:, :], b3_d)):
                sp.dma_start(dst, src).then_inc(ld_late, 16)
            def store_pair(i):
                sp.wait_ge(m_out, finished(2 * i + 1))
                for half in range(2):
                    sp.dma_start(z_d[bass.ds(2 * P * i + P * half, P), :],
                                 ysb[:, bass.ds(i % 2, 1), half, :].rearrange("p a n -> p (a n)")).then_inc(z_done, 16)

            def store_and_free(i):
                store_pair(i)
                sp.wait_ge(z_done, 16 * 2 * (i + 1))
                sp.sem_inc(z_free, 1)

            with sp.Fori(0, PREPARED + 1) as i:
                store_and_free(i)
            sp.wait_ge(w2_parts, 3)
            for k in range(3):
                sp.dma_start(w2_split[k].rearrange("g o t -> o g t"), w2p[:, k, :, :]).then_inc(w2_split_done, 16)
            sp.wait_ge(b3_lo, 1)
            sp.wait_ge(b3_hi, 1)
            sp.dma_start(b3_split[0], b3h[:, :].bitcast(F32)).then_inc(b3_rows, 16)
            sp.dma_start(b3_split[1], b3l[:, :].bitcast(F32)).then_inc(b3_rows, 16)
            store_and_free(PREPARED + 1)
            for done, count in ((w2_split_done, 48), (b3_rows, 32), (y_stk, 1), (er_done, 1), (w1_lo, 1)):
                sp.wait_ge(done, count)
            for half in range(2):
                row = 64 * half
                for parts in (3, 2, 1):
                    sp.dma_start(wstk[row:row + E * parts, :, :],
                                 w2_split[0:parts, :, 64 * half:64 * half + 64].rearrange("k g o t -> (k g) o t")).then_inc(w2_stack, 16)
                    row += E * parts
            with sp.Fori(PREPARED + 2, T0 // 2 - 1) as i:
                store_and_free(i)
            store_pair(T0 // 2 - 1)
            for e in range(E):
                if e == 4:
                    sp.wait_ge(l_turn, NG)
                if e == E - 2:
                    sp.wait_ge(gen_mm, FILLS)
                sp.dma_start(w3_raw(e), w3_d[e]).then_inc(ld_w3[e], 16)
            rows = b3_split.rearrange("k p n -> k (p n)")
            up_gate = E * 2 * I3
            sp.wait_ge(l_x2, NG)
            sp.dma_start(b3d[:, :, :].rearrange("p a b -> p (a b)").bitcast(F32), rows[:, up_gate:]).then_inc(b3_rows, 16)
            sp.wait_ge(q_mm, NG // 4)
            sp.dma_start(b3[:, :, :].rearrange("p a b -> p (a b)").bitcast(F32), rows[:, :up_gate]).then_inc(b3_rows, 16)
            with sp.Fori(0, T3 // 4) as i:
                for k in range(4):
                    sp.wait_ge(stored[k], 16 * (i + 1))
                    sp.sem_inc(out_free, 1)
            for k in range(T3 % 4):
                sp.wait_ge(stored[k], 16 * (T3 // 4 + 1))

        @block.gpsimd
        def _(pool):
            pool.sem_inc(m_up, CREDIT)
            pool.sem_inc(stage_free, CREDIT)
            for g in range(2, NG):
                pool.wait_ge(x_hi, g + 1)
                pool.wait_ge(x_lo, g)
                pool.tensor_tensor(xt[:, g * G:(g + 1) * G, 1, :], xraw[:, g * G:(g + 1) * G, :],
                                   xt[:, g * G:(g + 1) * G, 0, :].bitcast(F32), ALU.subtract).then_inc(x_lo, 1)
            with pool.Fori(0, E // 2) as i:
                for half in range(2):
                    e = 2 * i + half
                    pool.wait_ge(wx_hi, e + 1)
                    pool.tensor_tensor(wx[:, bass.ds(e, 1), 1, :].rearrange("p a n -> p (a n)"), stage[:, 1 - half, :],
                                       wx[:, bass.ds(e, 1), 0, :].rearrange("p a n -> p (a n)").bitcast(F32),
                                       ALU.subtract).then_inc(wx_lo, 1)
                    pool.wait_ge(wx_lo, e + 1)
                    pool.sem_inc(stage_free, 1)
            pool.wait_ge(tables, 4)
            pool.wait_ge(x_lo, NG)

            def bring(dst, src, table, i, used, ready):
                _, rows = nc.values_load_multi_w_load_instructions(
                    table[0:1, bass.ds(2 * TB * i, 2 * TB)], engines=POOL, min_val=0, max_val=B - 1,
                    skip_runtime_bounds_check_because="the table holds batches")
                for half in range(2):
                    pool.wait_ge(used, reusable(2 * i + half))
                    for q in range(TB):
                        last = pool.tensor_copy(dst[:, half, :, q, :],
                                                src[:, bass.ds(rows[TB * half + q], 1), :, :].rearrange("p a k s -> p (a k) s"))
                    last.then_inc(ready, 1)

            with pool.Fori(0, T0 // 2) as i:
                bring(xs, xt, batch0, i, m_up, m_xs)

            z_rows = z_d.rearrange("(n s) f -> n (s f)", s=SC)

            def gather(n):
                if n >= 3:
                    pool.wait_ge(l_turn, n - 2)
                for k in range(TOPK):
                    pool.indirect_dma_start(gath[:, n % 3, k, :], None, z_rows,
                                            bass.IndirectOffsetOnAxis(ap=idx[:, n, k:k + 1], axis=0)).then_inc(ld_g[n % 3], 16)

            def w3_lo_part(e):
                pool.wait_ge(w3_hi[e // (E - 2)], e % (E - 2) + 1)
                pool.tensor_tensor(w3[:, e, 1, :], w3_raw(e), w3[:, e, 0, :].bitcast(F32), ALU.subtract).then_inc(w3_lo[1], 1)

            pool.wait_ge(z_done, 16 * T0)
            for n in range(3):
                gather(n)
            pool.memset(x3s[:, :, :], 0.0).then_inc(x3_clear, 1)
            for g in range(-2, NG + 1):
                if 3 <= g + 4 < NG:
                    gather(g + 4)
                if g + 2 < NG:
                    n = g + 2
                    pool.wait_ge(l_x1h, n + 1)
                    pool.tensor_tensor(x1l[:, n % 3, :], x1[:, n % 3, :], x1h[:, n % 3, :].bitcast(F32), ALU.subtract).then_inc(l_x1l, 1)
                if 0 <= g + 1 < NG:
                    n = g + 1
                    pool.wait_ge(l_hsh, n + 1)
                    pool.tensor_tensor(hsl[:, n % 2, :], hs[:, :], hsh[:, n % 2, :].bitcast(F32), ALU.subtract).then_inc(l_hsl, 1)
                if g in W3_LO_ODD:
                    w3_lo_part(W3_LO_ODD[g])

            def store(i, k, last=False):
                t = 4 * i + k
                pool.wait_ge(e_out, finished(t))
                pool.wait_ge(row_set, t + 1)
                if not last:
                    pool.wait_ge(out_free, t + 2)
                    pool.tensor_copy(row_now[:, (k + 1) % 4:(k + 1) % 4 + 1], row3[:, bass.ds(t + 1, 1)]).then_inc(row_set, 1)
                pool.indirect_dma_start(out_d.rearrange("b s f -> (b s) f"),
                                        bass.IndirectOffsetOnAxis(ap=row_now[:, k:k + 1], axis=0),
                                        osb[:, k, :], None).then_inc(stored[k], 16)

            pool.tensor_copy(row_now[:, 0:1], row3[:, 0:1]).then_inc(row_set, 1)
            with pool.Fori(0, (T3 - 2) // 4) as i:
                for k in range(4):
                    store(i, k)
            store(T3 // 4, 0)
            store(T3 // 4, 1, last=True)

        @block.scalar
        def _(act):
            for s in (sh_gelu, m_rest):
                act.sem_inc(s, CREDIT)
            act.wait_ge(ld_gu, 16)
            act.copy(ws[:, 0, 0:2 * I0], stage[:, 0, 0:2 * I0]).then_inc(ws_hi, 1)

            def x_hi_part(g):
                act.wait_ge(ld_x[g * LOADC // NG], 16)
                act.copy(xt[:, g * G:(g + 1) * G, 0, :], xraw[:, g * G:(g + 1) * G, :]).then_inc(x_hi, 1)

            x_hi_part(0)
            x_hi_part(1)
            act.wait_ge(ld_w[0], 16)
            act.copy(ws[:, 0, 2 * I0:], stage[:, 0, 2 * I0:]).then_inc(ws_hi, 1)
            act.wait_ge(max_done, 1)
            act.activation(rt[:, 0, :], cond[:, :], ACT.Exp, bias=sc[:, 1:2]).then_inc(exp_done, 1)
            act.activation(sc[:, 7:8], kc[:, 0:1], ACT.Gelu_apprx_tanh)

            def sh_gelu_chunk(n, c):
                act.wait_ge(sh_gate, n + 1)
                act.wait_ge(sh_mul, reusable(n))
                act.activation(gt[:, c % 2, :], bank(2 * (c % 2)), ACT.Gelu_apprx_tanh).then_inc(sh_gelu, 1)

            def sh_hi_chunk(n, c):
                act.wait_ge(sh_mul, finished(n))
                act.wait_ge(sh_down, reusable(n))
                act.copy(hh[:, c % 2, :], h[:, c % 2, :]).then_inc(sh_hi, 1)

            def expert_hi(e, half, buf, count):
                act.wait_ge(ld_w[buf], 16 * count)
                ins = act.copy(wx[:, e, 0, half * W0 // 2:(half + 1) * W0 // 2],
                               stage[:, buf, half * W0 // 2:(half + 1) * W0 // 2])
                if half == 1:
                    ins.then_inc(wx_hi, 1)

            sh_gelu_chunk(0, 0)
            x_hi_part(2)
            for n in range(4 * NG):
                if n + 1 < 4 * NG:
                    sh_gelu_chunk(n + 1, (n + 1) % 4)
                sh_hi_chunk(n, n % 4)
                if n + 3 < NG:
                    x_hi_part(n + 3)
                for e in range(E):
                    for half in range(2):
                        if n == 4 + 3 * e + half:
                            expert_hi(e, half, 1 - e % 2, e // 2 + 1 + e % 2)

            def gelu(t, par):
                act.wait_ge(m_gate, t + 1)
                act.wait_ge(m_mul, reusable(t))
                act.activation(gt[:, par, :], bank(2 * par), ACT.Gelu_apprx_tanh).then_inc(m_gelu, 1)

            def hi(t, par):
                act.wait_ge(m_turn, finished(t))
                act.wait_ge(m_down, reusable(t))
                act.copy(hh[:, par, :], bank(4 + par)).then_inc(m_hi, 1)

            def rest(t, par):
                act.wait_ge(m_down, finished(t))
                act.wait_ge(m_out, reusable(t))
                act.copy(yres[:, par, :], ps[:, 6 + par, F:2 * F]).then_inc(m_rest, 1)

            gelu(0, 0)
            gelu(1, 1)
            hi(0, 0)
            with act.Fori(0, T0 // 2 - 1) as i:
                for par in range(2):
                    gelu(2 * i + 2 + par, par)
                    hi(2 * i + 1 + par, 1 - par)
                    rest(2 * i + par, par)
            hi(T0 - 1, 1)
            rest(T0 - 2, 0)
            rest(T0 - 1, 1)

            act.activation(sc[:, 7:8], kc[:, 0:1], ACT.Silu)

            def place(n, slots):
                act.wait_ge(q_x3g, n + 1)
                for j in range(G // 2 if n == NG - 1 else G):
                    last = act.copy(x3s[:, bass.ds(slots[j], 1), :].rearrange("p a s -> p (a s)"), x3g[:, n % 3, j, :])
                last.then_inc(q_x3, 1)

            def slots_of(n):
                _, slots = nc.values_load_multi_w_load_instructions(
                    slot3[0:1, n * G:(n + 1) * G], engines=ACTE, min_val=0, max_val=N3 - 1,
                    skip_runtime_bounds_check_because="the table holds slots")
                return slots

            def w3_hi_part(e):
                act.wait_ge(ld_w3[e], 16)
                act.copy(w3[:, e, 0, :], w3_raw(e)).then_inc(w3_hi[0], 1)

            act.wait_ge(tables, 4)
            def gen_even(fills):
                for n in fills:
                    act.wait_ge(gen_mm, n + 1)
                    act.copy(wbot[:, :, gen_out(n):gen_out(n) + OB].rearrange("p b o -> p o b"),
                             bank(gen_bank(n)).rearrange("p (o b) -> p o b", o=OB)).then_inc(gen_act, 1)

            gen_even(GEN_STEP[-3])
            for g in range(-2, NG + 2):
                if 0 <= g + 2 < NG:
                    n = g + 2
                    act.wait_ge(l_x1, n + 1)
                    if n >= 3:
                        act.wait_ge(l_o, n - 2)
                    act.copy(x1h[:, n % 3, :], x1[:, n % 3, :]).then_inc(l_x1h, 1)
                if 0 <= g + 1 < NG:
                    n = g + 1
                    act.wait_ge(l_hs, n + 1)
                    if n >= 2:
                        act.wait_ge(l_o, n - 1)
                    act.copy(hsh[:, n % 2, :], hs[:, :]).then_inc(l_hsh, 1)
                gen_even(GEN_STEP.get(g, ()))
                for e in W3_STEP.get(g, ()):
                    if e < E - 2:
                        if e >= 4:
                            act.wait_ge(l_turn, NG)
                        w3_hi_part(e)
                if g == 2:
                    act.wait_ge(x3_clear, 1)
                if g >= 2:
                    place(g - 2, slots_of(g - 2))
            def x3_hi_part(t, k):
                act.copy(xs3[:, k, 0, :].rearrange("p (q s) -> p q s", s=S), x3s[:, bass.ds(t * TB, TB), :]).then_inc(e_xhi, 1)

            def silu(t, par):
                act.wait_ge(e_in, t + 1)
                act.wait_ge(e_mul, reusable(t))
                act.activation(st[:, par, :], bank(par, I3), ACT.Silu).then_inc(e_silu, 1)

            def hi3(t, par):
                act.wait_ge(e_turn, finished(t))
                act.wait_ge(e_down, reusable(t))
                act.copy(h3h[:, par, :], bank(2 + par, I3)).then_inc(e_hi, 1)

            def rest3(t, k):
                act.wait_ge(e_down, finished(t))
                act.wait_ge(e_out, reusable(t))
                act.copy(yres3[:, k % 2, :], ps[:, 4 + k, F:2 * F]).then_inc(e_rest, 1)

            act.wait_ge(q_x3, NG)
            act.wait_ge(last_placed, 1)
            for t in range(4):
                x3_hi_part(t, t)
            silu(0, 0)
            silu(1, 1)
            hi3(0, 0)
            with act.Fori(0, (T3 - 2) // 4) as i:
                for k in range(4):
                    silu(4 * i + k + 2, k % 2)
                    hi3(4 * i + k + 1, (k + 1) % 2)
                    x3_hi_part(4 * i + k + 4, k)
                    rest3(4 * i + k, k)
            hi3(T3 - 1, 1)
            rest3(T3 - 2, 0)
            rest3(T3 - 1, 1)

        @block.vector
        def _(dve):
            for s in (sh_mul, m_mul, sh_lo, m_lo, e_mul, e_lo, sh_out, m_out, e_out):
                dve.sem_inc(s, CREDIT)
            steps = [0]

            def step(ins):
                steps[0] += 1
                ins.then_inc(route, 1)
                dve.wait_ge(route, steps[0])

            def shared_lo(n, a, b):
                dve.wait_ge(ws_hi, n + 1)
                dve.tensor_tensor(ws[:, 1, a:b], stage[:, 0, a:b], ws[:, 0, a:b].bitcast(F32), ALU.subtract).then_inc(ws_lo, 1)

            shared_lo(0, 0, 2 * I0)
            for g in range(2):
                dve.wait_ge(x_hi, g + 1)
                dve.tensor_tensor(xt[:, g * G:(g + 1) * G, 1, :], xraw[:, g * G:(g + 1) * G, :],
                                  xt[:, g * G:(g + 1) * G, 0, :].bitcast(F32), ALU.subtract).then_inc(x_lo, 1)

            dve.wait_ge(ld_c, 16 * 4)
            desc = kc[:, C_DESC:C_DESC + E]
            iota = kc[:, C_IOTA:C_IOTA + N0]
            step(dve.tensor_reduce(sc[:, 0:1], cond[:, :], AX_X, ALU.max))
            dve.tensor_scalar(sc[:, 1:2], sc[:, 0:1], -1.0, None, ALU.mult).then_inc(max_done, 1)
            dve.tensor_copy(ident_r[:, 0:P], ident).then_inc(consts_done, 1)
            dve.tensor_scalar(ident_r[:, P:2 * P], ident, 0.0, None, ALU.mult).then_inc(consts_done, 1)
            dve.tensor_copy(ident_r[:, 2 * P:3 * P], ident).then_inc(consts_done, 1)
            dve.tensor_copy(ones_r[:, :], kc[0:2, C_ONE:C_ONE + P]).then_inc(consts_done, 1)
            step(dve.tensor_copy(kb[:, :], kc[:, 0:4 * P]))
            step(dve.tensor_scalar(rt[:, 1, :], cond[:, :], sc[:, 0:1], None, ALU.is_equal))
            step(dve.tensor_tensor(rt[:, 2, :], rt[:, 1, :], desc, ALU.mult))
            step(dve.tensor_reduce(sc[:, 2:3], rt[:, 2, :], AX_X, ALU.max))
            step(dve.tensor_scalar(oh[:, 0, :], desc, sc[:, 2:3], None, ALU.is_equal))
            step(dve.scalar_tensor_tensor(out=rt[:, 3, :], in0=oh[:, 0, :], scalar=-3.0e38, in1=cond[:, :],
                                          op0=ALU.mult, op1=ALU.add))
            step(dve.tensor_reduce(sc[:, 3:4], rt[:, 3, :], AX_X, ALU.max))
            step(dve.tensor_scalar(rt[:, 4, :], rt[:, 3, :], sc[:, 3:4], None, ALU.is_equal))
            step(dve.tensor_tensor(rt[:, 5, :], rt[:, 4, :], desc, ALU.mult))
            step(dve.tensor_reduce(sc[:, 4:5], rt[:, 5, :], AX_X, ALU.max))
            step(dve.tensor_scalar(oh[:, 1, :], desc, sc[:, 4:5], None, ALU.is_equal))
            dve.tensor_tensor(pair[:, 0:E], oh[:, 0, :], oh[:, 1, :], ALU.add).then_inc(pair_done, 1)
            dve.tensor_copy(pair[:, E:2 * E], oh[:, 0, :]).then_inc(pair_done, 1)
            dve.memset(scan[:, :, :, 0:E], 0.0).then_inc(pair_done, 1)
            shared_lo(1, 2 * I0, W0)

            count = rc[:, 2 * E:4 * E].rearrange("p (l e) -> p l e", l=2)
            rank = rc[:, 0:2 * E].rearrange("p (l e) -> p l e", l=2)
            full = rt[:, 8:10, :]
            end = scan[:, 1, :, E:]

            def route_counts():
                dve.wait_ge(rank_done, 1)
                step(dve.tensor_copy(rc[:, :], bank(7, 4 * E)))
                step(dve.tensor_scalar(up4[:, :, :], count, float(TB - 1), None, ALU.add))

            def route_rounded():
                step(dve.tensor_scalar(up4[:, :, :], up4[:, :, :], TB_SHIFT, TB_SHIFT, ALU.logical_shift_right, ALU.logical_shift_left))
                step(dve.tensor_copy(full, up4[:, :, :]))

            def route_ends():
                a, b = scan[:, 0, :, :], scan[:, 1, :, :]
                dve.wait_ge(pair_done, 3)
                step(dve.tensor_copy(a[:, :, E:], full))
                step(dve.tensor_tensor(b[:, :, E:], a[:, :, E:], a[:, :, E - 1:2 * E - 1], ALU.add))

            def route_lists():
                a, b = scan[:, 0, :, :], scan[:, 1, :, :]
                step(dve.tensor_tensor(a[:, :, E:], b[:, :, E:], b[:, :, E - 2:2 * E - 2], ALU.add))
                step(dve.tensor_tensor(b[:, :, E:], a[:, :, E:], a[:, :, E - 4:2 * E - 4], ALU.add))

            def route_ranks():
                step(dve.tensor_tensor(slot[:, :, :], end, full, ALU.subtract))
                step(dve.tensor_tensor(rt[:, 10:12, :], slot[:, :, :], rank, ALU.add))

            def route_slots():
                step(dve.tensor_tensor(prod[:, 0, :], rt[:, 10, :], oh[:, 0, :], ALU.mult))
                step(dve.tensor_tensor(prod[:, 1, :], rt[:, 10, :], oh[:, 1, :], ALU.mult))
                step(dve.tensor_tensor(prod[:, 2, :], rt[:, 11, :], oh[:, 0, :], ALU.mult))

            def route_positions():
                step(dve.tensor_reduce(pos[:, :], prod[:, :, :], AX_X, ALU.add))
                step(dve.tensor_copy(pos3[:, :], pos[:, 2:3]))

            def route_onehots():
                step(dve.tensor_scalar(sel0[:, :], iota, pos[:, 0:1], None, ALU.is_equal))
                dve.scalar_tensor_tensor(out=sel0[:, :], in0=iota, scalar=pos[:, 1:2], in1=sel0[:, :],
                                         op0=ALU.is_equal, op1=ALU.add).then_inc(sel_done, 1)

            def route_onehots3():
                dve.tensor_scalar(sel3[:, :], iota[:, 0:N3], pos[:, 2:3], None, ALU.is_equal).then_inc(sel_done, 1)
                dve.tensor_scalar(before3[:, :], iota[:, 0:N3], pos[:, 2:3], None, ALU.is_gt).then_inc(sel_done, 1)

            def route_weights():
                dve.wait_ge(exp_done, 1)
                step(dve.tensor_reduce(sc[:, 5:6], rt[:, 0, :], AX_X, ALU.add))
                step(dve.reciprocal(sc[:, 6:7], sc[:, 5:6]))
                step(dve.tensor_scalar(rt[:, 12, :], rt[:, 0, :], sc[:, 6:7], None, ALU.mult))

            def route_top():
                step(dve.tensor_tensor(prod[:, 0, :], rt[:, 12, :], oh[:, 0, :], ALU.mult))
                step(dve.tensor_tensor(prod[:, 1, :], rt[:, 12, :], oh[:, 1, :], ALU.mult))
                step(dve.tensor_reduce(rw[:, :], prod[:, 0:2, :], AX_X, ALU.add))

            def route_normalised():
                step(dve.tensor_tensor(sc[:, 5:6], rw[:, 0:1], rw[:, 1:2], ALU.add))
                step(dve.reciprocal(sc[:, 6:7], sc[:, 5:6]))
                step(dve.tensor_scalar(rw[:, :], rw[:, :], sc[:, 6:7], None, ALU.mult))

            def route_scaled():
                step(dve.tensor_scalar(rt[:, 13, 0:2], rw[:, :], 1.0 / LAYERS, None, ALU.mult))
                step(dve.scalar_tensor_tensor(out=wt[:, :], in0=rw[:, :], scalar=1.0 - 1.0 / LAYERS, in1=rt[:, 13, 0:2],
                                         op0=ALU.mult, op1=ALU.add))
                for w, v in enumerate((pos, wt)):
                    dve.tensor_tensor(vals[:, w, :, :], v[:, None, 0:TOPK].to_broadcast([P, NG, TOPK]),
                                      kc[:, C_G:C_G + NG].unsqueeze(2).to_broadcast([P, NG, TOPK]), ALU.mult).then_inc(vals_done, 1)

            def route_expert(l, n, table):
                t4 = kc[0:1, C_T4:C_T4 + 72]
                step(dve.tensor_tensor(cmp_t[0:1, :, 0:n], t4[:, None, 0:n].to_broadcast([1, E, n]),
                                       end[0:1, l, :].unsqueeze(2).to_broadcast([1, E, n]), ALU.is_ge))
                step(dve.tensor_reduce(tmp3[0:1, 0, 0:n], cmp_t[0:1, :, 0:n].rearrange("p e t -> p t e"), AX_X, ALU.add))
                step(dve.tensor_scalar(table[:, :], tmp3[0:1, 0, 0:n], float(E - 1), None, ALU.min))

            def route_tables():
                dve.wait_ge(slots_done, 1)
                step(dve.tensor_copy(batch0[:, :], ps[0:1, 7, 0:N0]))
                step(dve.tensor_copy(slot3[:, :], ps[0:1, 7, N0:N0 + B]))

            def route_rows():
                step(dve.scalar_tensor_tensor(out=tmp3[:, 0, :], in0=kc[:, C_IOTA:C_IOTA + N3], scalar=float(B),
                                              in1=ps[:, 6, 2 * N3:3 * N3], op0=ALU.add, op1=ALU.subtract))
                step(dve.tensor_scalar(tmp3[:, 1, :], ps[:, 6, N3:2 * N3], -1.0, 1.0, ALU.mult, ALU.add))

            def route_rows_of_slots():
                step(dve.tensor_tensor(tmp3[:, 0, :], tmp3[:, 0, :], tmp3[:, 1, :], ALU.mult))
                step(dve.tensor_tensor(tmp3[:, 0, :], tmp3[:, 0, :], ps[:, 6, 0:N3], ALU.add))

            def route_rows_of_tokens():
                by_tile = tmp3[:, :, :].rearrange("p k (t q) -> p k t q", q=TB)
                step(dve.tensor_tensor(by_tile[:, 1], by_tile[:, 0], kc[:, None, C_Q:C_Q + TB].to_broadcast([P, T3, TB]), ALU.mult))
                step(dve.tensor_reduce(tmp3[:, 0, 0:T3], by_tile[:, 1], AX_X, ALU.add))
                step(dve.tensor_scalar(row3[:, :], tmp3[:, 0, 0:T3], float(S), kc[:, C_S:C_S + 1], ALU.mult, ALU.add))

            def route_gathers():
                expanded = ps[:, 7, N0 + B:N0 + B + 2 * NG * TOPK].rearrange("p (w g k) -> p w g k", w=2, k=TOPK)
                dve.tensor_copy(wtx[:, :, :], expanded[:, 1]).then_inc(tables, 1)
                dve.tensor_scalar(idx[:, :, :], expanded[:, 0], float(ZC), kc[:, C_ZC:C_ZC + 1], ALU.mult, ALU.add).then_inc(tables, 3)

            def route_part(n):
                if n == 3:
                    route_counts()
                elif n == 4:
                    route_rounded()
                elif n == 5:
                    route_ends()
                elif n == 6:
                    route_lists()
                elif n == 7:
                    route_ranks()
                elif n == 8:
                    route_slots()
                elif n == 9:
                    route_positions()
                elif n == 10:
                    route_onehots()
                elif n == 11:
                    route_onehots3()
                elif n == 12:
                    route_weights()
                elif n == 13:
                    route_top()
                elif n == 14:
                    route_normalised()
                elif n == 15:
                    route_scaled()
                elif n == 17:
                    route_expert(0, 72, expert0)
                elif n == 19:
                    route_expert(1, 40, expert3)
                elif n == 25:
                    route_tables()
                elif n == 26:
                    route_rows()
                elif n == 27:
                    route_rows_of_slots()
                elif n == 28:
                    route_rows_of_tokens()
                elif n == 29:
                    route_gathers()

            def sh_mul_chunk(n, c):
                dve.wait_ge(sh_up, n + 1)
                dve.wait_ge(sh_gelu, finished(n))
                dve.wait_ge(sh_lo, reusable(n))
                dve.tensor_tensor(h[:, c % 2, :], gt[:, c % 2, :], bank(2 * (c % 2) + 1), ALU.mult).then_inc(sh_mul, 1)

            def sh_lo_chunk(n, c):
                dve.wait_ge(sh_hi, n + 1)
                dve.tensor_tensor(hl[:, c % 2, :], h[:, c % 2, :], hh[:, c % 2, :].bitcast(F32), ALU.subtract).then_inc(sh_lo, 1)

            def sh_result(g):
                dve.wait_ge(sh_down, finished(4 * g + 3))
                cols = res[:, g * G:(g + 1) * G, :].rearrange("p b s -> p (b s)")
                dve.tensor_tensor(cols, bank(4 + g % 2), xraw[:, g * G:(g + 1) * G, :].rearrange("p b s -> p (b s)"),
                                  ALU.add).then_inc(sh_out, 1)

            sh_mul_chunk(0, 0)
            for g in range(NG):
                for c in range(4):
                    if not (g == NG - 1 and c == 3):
                        sh_mul_chunk(4 * g + c + 1, (c + 1) % 4)
                    sh_lo_chunk(4 * g + c, c)
                    route_part(4 * g + c)
                    if c == 2 and g >= 1:
                        sh_result(g - 1)
            sh_result(NG - 1)

            def mul(t, par):
                dve.wait_ge(m_up, finished(t))
                dve.wait_ge(m_gelu, t + 1)
                dve.wait_ge(m_turn, reusable(t))
                dve.tensor_tensor(h[:, par, :], gt[:, par, :], bank(2 * par + 1), ALU.mult).then_inc(m_mul, 1)

            def lo(t, par):
                dve.wait_ge(m_hi, t + 1)
                dve.tensor_tensor(hl[:, par, :], bank(4 + par), hh[:, par, :].bitcast(F32), ALU.subtract).then_inc(m_lo, 1)

            def result(i, par):
                t = 2 * i + par
                dve.wait_ge(m_rest, finished(t))
                dve.tensor_tensor(ysb[:, bass.ds(i % 2, 1), par, :].rearrange("p a n -> p (a n)"), yres[:, par, :],
                                  bank(6 + par, F), ALU.add).then_inc(m_out, 1)

            lates = [0]

            def late_step(ins):
                lates[0] += 1
                ins.then_inc(late, 1)
                dve.wait_ge(late, lates[0])

            def w1_parts():
                dve.wait_ge(ld_late, 16 * 6)
                dve.tensor_scalar(er[:, :], er_raw[:, :], 2.0, None, ALU.mult).then_inc(er_done, 1)
                late_step(dve.tensor_copy(w1[:, 0, :], w1raw[:, :]))
                dve.tensor_tensor(w1[:, 1, :], w1raw[:, :], w1[:, 0, :].bitcast(F32), ALU.subtract).then_inc(w1_lo, 1)

            def w2_masked():
                late_step(dve.tensor_tensor(w2raw[:, :, :], w2raw[:, :, :], mask[:, None, :].to_broadcast([P, E, F]), ALU.mult))

            def w2_part(k):
                ins = dve.tensor_copy(w2p[:, k, :, :], w2raw[:, :, :])
                if k == 2:
                    ins.then_inc(w2_parts, 3)
                else:
                    late_step(ins)

            def w2_rest(k):
                late_step(dve.tensor_tensor(w2raw[:, :, :], w2raw[:, :, :], w2p[:, k, :, :], ALU.subtract))

            def y_parts():
                for k in range(3):
                    late_step(dve.tensor_copy(yp[:, k, :], yraw[:, :]))
                    if k < 2:
                        late_step(dve.tensor_tensor(yraw[:, :], yraw[:, :], yp[:, k, :], ALU.subtract))

            def y_stack():
                late_step(dve.tensor_scalar(ysum[:, :], yp[:, 0, :], kc[:, C_Y:C_Y + 1], None, ALU.mult))
                late_step(dve.scalar_tensor_tensor(out=ysum[:, :], in0=yp[:, 1, :], scalar=kc[:, C_Y + 1:C_Y + 2], in1=ysum[:, :],
                                                   op0=ALU.mult, op1=ALU.add))
                dve.scalar_tensor_tensor(out=ystk[:, :], in0=yp[:, 2, :], scalar=kc[:, C_Y + 2:C_Y + 3], in1=ysum[:, :],
                                         op0=ALU.mult, op1=ALU.add).then_inc(y_stk, 1)
                dve.tensor_copy(b3h[:, :], b3raw[:, :]).then_inc(b3_hi, 1)
                dve.wait_ge(b3_hi, 1)
                dve.tensor_tensor(b3l[:, :], b3raw[:, :], b3h[:, :].bitcast(F32), ALU.subtract).then_inc(b3_lo, 1)

            def prepare(n):
                if n == 0:
                    w1_parts()
                elif n == 1:
                    w2_masked()
                elif n in (2, 4, 6):
                    w2_part(n // 2 - 1)
                elif n in (3, 5):
                    w2_rest(n // 2 - 1)
                elif n == 7:
                    y_parts()
                elif n == 8:
                    y_stack()

            def tile(i, par):
                mul(2 * i + 2 + par, par)
                lo(2 * i + 1 + par, 1 - par)
                result(i, par)

            mul(0, 0)
            mul(1, 1)
            lo(0, 0)
            with dve.Fori(0, PREP_FIRST) as i:
                dve.wait_ge(z_free, reusable(i))
                for par in range(2):
                    tile(i, par)
            for i in range(PREP_FIRST, PREPARED):
                dve.wait_ge(z_free, reusable(i))
                for par in range(2):
                    tile(i, par)
                    prepare(2 * (i - PREP_FIRST) + par)
            with dve.Fori(PREPARED, T0 // 2 - 1) as i:
                dve.wait_ge(z_free, reusable(i))
                for par in range(2):
                    tile(i, par)
            lo(T0 - 1, 1)
            dve.wait_ge(z_free, reusable(T0 // 2 - 1))
            result(T0 // 2 - 1, 0)
            result(T0 // 2 - 1, 1)

            def mix(n):
                dve.wait_ge(ld_g[n % 3], 16 * TOPK * (n // 3 + 1))
                dve.tensor_scalar(gath[:, n % 3, 0, :], gath[:, n % 3, 0, :], wtx[:, n, 0:1], None, ALU.mult).then_inc(mix1, 1)
                dve.wait_ge(mix1, n + 1)
                dve.scalar_tensor_tensor(out=gath[:, n % 3, 0, :], in0=gath[:, n % 3, 1, :], scalar=wtx[:, n, 1:2],
                                         in1=gath[:, n % 3, 0, :], op0=ALU.mult, op1=ALU.add).then_inc(mix2, 1)

            def cols(g):
                return res[:, g * G:(g + 1) * G, :].rearrange("p b s -> p (b s)").rearrange("p (m s) -> p s m", s=SC)

            def grp(ap):
                return ap.rearrange("p (s m) -> p s m", s=SC)

            def by_batch(ap):
                return ap.rearrange("p (s b c) -> p s b c", s=SC, c=ZC)

            def tok_part(n):
                dve.wait_ge(q_mm, n + 1)
                if n >= 2:
                    dve.wait_ge(q_turn, n - 1)
                dve.tensor_copy(tok[:, n % 2, :, :].rearrange("p t o -> p (t o)"), bank(4 + n % 2)).then_inc(q_tok, 1)

            def x3_part(n):
                dve.wait_ge(q_turn, n + 1)
                if n >= 3:
                    dve.wait_ge(q_x3, n - 2)
                dve.scalar_tensor_tensor(out=x3g[:, n % 3, :, :], in0=bank(3).rearrange("p (b s) -> p b s", s=S),
                                         scalar=b2[:, 0:1], in1=res[:, n * G:(n + 1) * G, :],
                                         op0=ALU.add, op1=ALU.add).then_inc(q_x3g, 1)

            def w3_lo_part(e):
                dve.wait_ge(w3_hi[e // (E - 2)], e % (E - 2) + 1)
                dve.tensor_tensor(w3[:, e, 1, :], w3_raw(e), w3[:, e, 0, :].bitcast(F32), ALU.subtract).then_inc(w3_lo[0], 1)

            def gen_odd(fills):
                for n in fills:
                    dve.wait_ge(gen_mm, n + 2)
                    dve.tensor_copy(wbot[:, :, gen_out(n + 1):gen_out(n + 1) + OB].rearrange("p b o -> p o b"),
                                    bank(gen_bank(n + 1)).rearrange("p (o b) -> p o b", o=OB)).then_inc(gen_dve, 1)

            gen_odd(GEN_STEP[-3])
            mix(0)
            for g in range(-2, NG + 2):
                if g + 3 < NG:
                    mix(g + 3)
                if 0 <= g + 2 < NG:
                    n = g + 2
                    dve.wait_ge(l_turn, n + 1)
                    if n >= 3:
                        dve.wait_ge(l_x1l, n - 2)
                        dve.wait_ge(l_x2, n - 2)
                    dve.tensor_tensor(grp(x1[:, n % 3, :]), grp(bank(0)), cols(n), ALU.add).then_inc(l_x1, 1)
                if 0 <= g + 1 < NG:
                    n = g + 1
                    dve.wait_ge(l_a, n + 1)
                    if n >= 1:
                        dve.wait_ge(l_hsl, n)
                    dve.tensor_tensor(by_batch(hs[:, :]), by_batch(bank(1)),
                                      er[:, None, n * G:(n + 1) * G].unsqueeze(3).to_broadcast([P, SC, G, ZC]), ALU.mult).then_inc(l_hs, 1)
                if 0 <= g < NG:
                    dve.wait_ge(l_o, g + 1)
                    dve.scalar_tensor_tensor(out=cols(g), in0=grp(bank(2)), scalar=b1[:, 0:1], in1=grp(x1[:, g % 3, :]),
                                             op0=ALU.add, op1=ALU.add).then_inc(l_x2, 1)
                gen_odd(GEN_STEP.get(g, ()))
                if g > NG:
                    _, slots = nc.values_load_multi_w_load_instructions(
                        slot3[0:1, B - G // 2:B], engines=DVE, min_val=0, max_val=N3 - 1,
                        skip_runtime_bounds_check_because="the table holds slots")
                if g >= 2:
                    x3_part(g - 2)
                if g > NG:
                    dve.wait_ge(q_x3g, NG)
                    for j in range(G // 2, G):
                        last = dve.tensor_copy(x3s[:, bass.ds(slots[j - G // 2], 1), :].rearrange("p a s -> p (a s)"),
                                               x3g[:, (NG - 1) % 3, j, :])
                    last.then_inc(last_placed, 1)
                if 1 <= g <= NG:
                    tok_part(g - 1)
                for e in W3_STEP.get(g, ()):
                    if e >= E - 2:
                        dve.wait_ge(ld_w3[e], 16)
                        dve.tensor_copy(w3[:, e, 0, :], w3_raw(e)).then_inc(w3_hi[1], 1)
                for e in W3_STEP.get(g - (g > NG), ()):
                    if e % 2 == 0 and g != NG:
                        w3_lo_part(e)

            def mul3(t, par):
                dve.wait_ge(e_silu, t + 1)
                dve.wait_ge(e_turn, reusable(t))
                dve.tensor_tensor(h3[:, par, :], st[:, par, :], ps[:, par, I3:2 * I3], ALU.mult).then_inc(e_mul, 1)

            def lo3(t, par):
                dve.wait_ge(e_hi, t + 1)
                dve.tensor_tensor(h3l[:, par, :], bank(2 + par, I3), h3h[:, par, :].bitcast(F32), ALU.subtract).then_inc(e_lo, 1)

            def x3_lo_part(t, k):
                dve.wait_ge(e_xhi, t + 1)
                dve.tensor_tensor(xs3[:, k, 1, :].rearrange("p (q s) -> p q s", s=S), x3s[:, bass.ds(t * TB, TB), :],
                                  xs3[:, k, 0, :].rearrange("p (q s) -> p q s", s=S).bitcast(F32), ALU.subtract).then_inc(e_xlo, 1)

            def result3(t, k):
                dve.wait_ge(e_rest, t + 1)
                dve.tensor_tensor(osb[:, k, :], yres3[:, k % 2, :], bank(4 + k, F), ALU.add).then_inc(e_out, 1)

            for t in range(4):
                x3_lo_part(t, t)
            mul3(0, 0)
            mul3(1, 1)
            lo3(0, 0)
            with dve.Fori(0, (T3 - 2) // 4) as i:
                for k in range(4):
                    mul3(4 * i + k + 2, k % 2)
                    lo3(4 * i + k + 1, (k + 1) % 2)
                    x3_lo_part(4 * i + k + 4, k)
                    dve.wait_ge(out_free, 4 * i + k + 1)
                    result3(4 * i + k, k)
            lo3(T3 - 1, 1)
            for t in (T3 - 2, T3 - 1):
                dve.wait_ge(out_free, t + 1)
                result3(t, t % 4)

        @block.tensor
        def _(pe):
            for s in (sh_down, m_turn, m_down, e_turn, e_down):
                pe.sem_inc(s, CREDIT)

            def split_product(out, w, m, start=True, stop=True):
                for n, (a, b) in enumerate(((0, 0), (0, 1), (1, 0))):
                    last = pe.matmul(out, w[a], m[b], start=start and n == 0, stop=stop and n == 2)
                return last

            def sh_in(g, n, c):
                if c == 0:
                    pe.wait_ge(x_lo, g + 1)
                pe.wait_ge(sh_mul, reusable(n))
                m = [xt[:, bass.ds(g * G, G), k, :] for k in range(2)]
                for what, sem_ in ((0, sh_gate), (1, sh_up)):
                    w = [ws[:, k, what * I0 + c * P:what * I0 + (c + 1) * P] for k in range(2)]
                    out = bank(2 * (c % 2) + what).rearrange("p (b s) -> p b s", s=S)
                    split_product(out, w, m).then_inc(sem_, 1)

            def sh_down_(g, par, n, c):
                if c == 0:
                    pe.wait_ge(sh_out, reusable(g))
                pe.wait_ge(sh_lo, finished(n))
                w = [ws[:, k, 2 * I0 + c * P:2 * I0 + (c + 1) * P] for k in range(2)]
                split_product(bank(4 + par), w, (hh[:, c % 2, :], hl[:, c % 2, :]), start=c == 0, stop=c == 3).then_inc(sh_down, 1)

            def sh_pe(g, par, last):
                for c in range(4):
                    if c < 2:
                        sh_in(g, 4 * g + c + 2, c + 2)
                    elif not last:
                        sh_in(g + 1, 4 * g + c + 2, c - 2)
                    sh_down_(g, par, 4 * g + c, c)

            pe.wait_ge(ws_lo, 1)
            sh_in(0, 0, 0)
            sh_in(0, 1, 1)
            pe.wait_ge(pair_done, 2)
            pe.wait_ge(route, 1)
            pe.matmul(ps[:, 7, 0:2 * E], before, pair[:, :], start=True, stop=True)
            pe.matmul(ps[:, 7, 2 * E:4 * E], ones, pair[:, :], start=True, stop=True).then_inc(rank_done, 1)
            pe.wait_ge(ws_lo, 2)
            with pe.Fori(0, NG // 2 - 1) as i:
                sh_pe(2 * i, 0, False)
                sh_pe(2 * i + 1, 1, False)
            pe.wait_ge(sel_done, 3)
            pe.matmul(ps[0:1, 7, 0:N0], batch[:, 0:1], sel0[:, :], start=True, stop=True)
            pe.matmul(ps[0:1, 7, N0:N0 + B], pos3[:, :], ident_b, start=True, stop=True)
            pe.wait_ge(vals_done, 2)
            pe.matmul(ps[:, 7, N0 + B:N0 + B + 2 * NG * TOPK], kc[:, C_REP:C_REP + P],
                      vals[:, :, :, :].rearrange("p w g k -> p (w g k)"), start=True, stop=True)
            pe.matmul(ps[:, 6, 0:N3], batch, sel3[:, :], start=True, stop=True)
            pe.matmul(ps[:, 6, N3:2 * N3], ones, sel3[:, :], start=True, stop=True)
            pe.matmul(ps[:, 6, 2 * N3:3 * N3], ones, before3[:, :], start=True, stop=True).then_inc(slots_done, 1)
            sh_pe(NG - 2, 0, False)
            sh_pe(NG - 1, 1, True)

            def experts(table, start, count):
                _, e = nc.values_load_multi_w_load_instructions(
                    table[0:1, bass.ds(start, count)], engines=PE, min_val=0, max_val=E - 1,
                    skip_runtime_bounds_check_because="the table holds experts")
                return e

            def both_products(out, x, w, e, inner, start, last_stop):
                halves = out.rearrange("p (k n) -> p k n", k=2)
                for c in range(inner // P):
                    down = w[:, bass.ds(e, 1), :, 2 * inner + c * P:2 * inner + (c + 1) * P].rearrange("p a k n -> p (a k) n")
                    for n, v in enumerate(x):
                        last = pe.matmul(halves, v[:, c * P:(c + 1) * P], down, start=start and c == 0 and n == 0,
                                         stop=last_stop and c == inner // P - 1 and n == 1, skip_group_check=True)
                return last

            def weights(w, e, k, a, b):
                return w[:, bass.ds(e, 1), k, a:b].rearrange("p a n -> p (a n)")

            def gate_up(t, par, e):
                pe.wait_ge(m_xs, t + 1)
                pe.wait_ge(m_mul, reusable(t))
                x = [xs[:, par, k, :, :].rearrange("p q s -> p (q s)") for k in range(2)]
                for what, sem_ in ((0, m_gate), (1, m_up)):
                    w = [weights(wx, e, k, what * I0, (what + 1) * I0) for k in range(2)]
                    split_product(bank(2 * par + what), x, w).then_inc(sem_, 1)

            def turn(t, par):
                pe.wait_ge(m_mul, finished(t))
                pe.wait_ge(m_lo, reusable(t))
                for c in range(4):
                    last = pe.transpose(bank(4 + par)[:, c * P:(c + 1) * P], h[:, par, c * P:(c + 1) * P], ident)
                last.then_inc(m_turn, 1)

            def down(t, par, e):
                pe.wait_ge(m_lo, finished(t))
                pe.wait_ge(m_out, reusable(t))
                both_products(bank(6 + par, 2 * F), (hh[:, par, :], hl[:, par, :]), wx, e, I0, True, True).then_inc(m_down, 1)

            pe.wait_ge(tables, 4)
            pe.wait_ge(wx_lo, E)
            e0, e1 = experts(expert0, 0, 2)
            gate_up(0, 0, e0)
            gate_up(1, 1, e1)
            pe.wait_ge(sh_out, finished(NG - 1))
            turn(0, 0)
            with pe.Fori(0, T0 // 2 - 1) as i:
                e = experts(expert0, 2 * i, 4)
                for par in range(2):
                    gate_up(2 * i + 2 + par, par, e[2 + par])
                    turn(2 * i + 1 + par, 1 - par)
                    down(2 * i + par, par, e[par])
            e0, e1 = experts(expert0, T0 - 2, 2)
            turn(T0 - 1, 1)
            down(T0 - 2, 0, e0)
            down(T0 - 1, 1, e1)

            pe.wait_ge(m_out, finished(T0 - 1))
            pe.wait_ge(w2_stack, 16 * 2 * 3)
            pe.wait_ge(y_stk, 1)
            def gen(fills):
                for n in fills:
                    left = n // 2 - 2 if n < 30 else 14
                    if left > 0:
                        pe.wait_ge(gen_act, left)
                        pe.wait_ge(gen_dve, left)
                    for k in range(OB):
                        for half in range(2):
                            row = 64 * half
                            last = pe.matmul(ps[:, gen_bank(n + half), k * B:(k + 1) * B], wstk[row:row + KY, gen_out(n) + k, :],
                                             ystk[row:row + KY, :], start=True, stop=True)
                    last.then_inc(gen_mm, 2)

            def layer2(n):
                pe.wait_ge(l_x2, n + 1)
                if n >= 2:
                    pe.wait_ge(q_tok, n - 1)
                for j in range(G):
                    b = n * G + j
                    q = j % TB
                    last = pe.matmul(ps[q * S:(q + 1) * S, 4 + n % 2, j // TB * F:(j // TB + 1) * F], res[:, b, :], wbot[:, b, :],
                                     start=True, stop=True)
                last.then_inc(q_mm, 1)

            def turn_layer2(n):
                pe.wait_ge(q_tok, n + 1)
                if n >= 1:
                    pe.wait_ge(q_x3g, n)
                for t in range(4):
                    last = pe.transpose(bank(3)[:, t * P:(t + 1) * P], tok[:, n % 2, t, :], ident)
                last.then_inc(q_turn, 1)

            gen(GEN_STEP[-3])
            pe.wait_ge(w1_lo, 1)
            A_, WB, BB = ([w1[:, k, n * F:(n + 1) * F] for k in range(2)] for n in range(3))
            for g in range(-2, NG + 2):
                if g + 2 < NG:
                    n = g + 2
                    pe.wait_ge(mix2, n + 1)
                    if n >= 1:
                        pe.wait_ge(l_x1, n)
                    for s in range(SC):
                        last = pe.transpose(bank(0)[:, s * P:(s + 1) * P], gath[:, n % 3, 0, s * F:(s + 1) * F], ident)
                    last.then_inc(l_turn, 1)
                if 0 <= g + 1 < NG:
                    n = g + 1
                    pe.wait_ge(l_x1l, n + 1)
                    if n >= 1:
                        pe.wait_ge(l_hs, n)
                    split_product(bank(1), A_, (x1h[:, n % 3, :], x1l[:, n % 3, :])).then_inc(l_a, 1)
                if g == 0:
                    pe.wait_ge(gen_act, 14)
                    pe.wait_ge(gen_dve, 14)
                if 0 <= g < NG:
                    if g >= 1:
                        pe.wait_ge(l_x2, g)
                    split_product(bank(2), WB, (x1h[:, g % 3, :], x1l[:, g % 3, :]), stop=False)
                    pe.wait_ge(l_hsl, g + 1)
                    split_product(bank(2), BB, (hsh[:, g % 2, :], hsl[:, g % 2, :]), start=False).then_inc(l_o, 1)
                gen(GEN_STEP.get(g, ()))
                if g >= 2:
                    turn_layer2(g - 2)
                if g == 1:
                    pe.wait_ge(gen_act, FILLS // 2)
                    pe.wait_ge(gen_dve, FILLS // 2)
                if 1 <= g <= NG:
                    layer2(g - 1)

            def gate_up3(t, k, e):
                pe.wait_ge(e_xlo, t + 1)
                pe.wait_ge(e_mul, reusable(t))
                x = [xs3[:, k, n, :] for n in range(2)]
                for n in range(2):
                    pe.matmul(bank(4 + k, 2 * F), x[n], ident_r[:, n * P:(n + 2) * P], start=n == 0, stop=False,
                              skip_group_check=True)
                w = [weights(w3, e, n, 0, 2 * I3) for n in range(2)]
                split_product(bank(k % 2), x, w, stop=False)
                pe.matmul(bank(k % 2), ones_r[:, :], b3[:, bass.ds(e, 1), :].rearrange("p a n -> p (a n)"),
                          start=False, stop=True).then_inc(e_in, 1)

            def turn3(t, par):
                pe.wait_ge(e_mul, finished(t))
                pe.wait_ge(e_lo, reusable(t))
                for c in range(2):
                    last = pe.transpose(bank(2 + par)[:, c * P:(c + 1) * P], h3[:, par, c * P:(c + 1) * P], ident)
                last.then_inc(e_turn, 1)

            def down3(t, k, e):
                pe.wait_ge(e_lo, finished(t))
                both_products(bank(4 + k, 2 * F), (h3h[:, k % 2, :], h3l[:, k % 2, :]), w3, e, I3, False, False)
                pe.matmul(bank(4 + k, F), ones_r[:, :], b3d[:, bass.ds(e, 1), :].rearrange("p a n -> p (a n)"),
                          start=False, stop=True, skip_group_check=True).then_inc(e_down, 1)

            for lo_done in w3_lo:
                pe.wait_ge(lo_done, E // 2)
            pe.wait_ge(b3_rows, 64)
            pe.wait_ge(consts_done, 4)
            e = experts(expert3, 0, 2)
            gate_up3(0, 0, e[0])
            gate_up3(1, 1, e[1])
            turn3(0, 0)
            with pe.Fori(0, (T3 - 2) // 4) as i:
                e = experts(expert3, 4 * i, 6)
                for k in range(4):
                    pe.wait_ge(e_out, 4 * i + k + 1)
                    gate_up3(4 * i + k + 2, (k + 2) % 4, e[k + 2])
                    turn3(4 * i + k + 1, (k + 1) % 2)
                    down3(4 * i + k, k, e[k])
            e = experts(expert3, T3 - 2, 2)
            turn3(T3 - 1, 1)
            down3(T3 - 2, (T3 - 2) % 4, e[0])
            down3(T3 - 1, (T3 - 1) % 4, e[1])


def kernel(**inputs):
    import numpy as _np
    import concourse.bacc as _bacc
    from concourse import mybir as _mybir
    from concourse.bass_utils import run_bass_kernel_spmd as _run

    v = {k: _np.asarray(a) for k, a in inputs.items()}
    x, cond = v["x"], v["cond_8"]

    def mlp(gate, up, down, inner):
        return _np.concatenate([gate, up, down.reshape(inner // P, P, F).transpose(1, 0, 2).reshape(P, inner)], axis=1)

    w0 = _np.stack([mlp(g, u, d, I0) for g, u, d in zip(v["L0_cond_skill_gate"], v["L0_cond_skill_up"], v["L0_cond_skill_down"])]
                   + [mlp(v["L0_cond_shared_gate"], v["L0_cond_shared_up"], v["L0_cond_shared_down"], I0)])
    w3 = _np.stack([mlp(u.T, g.T, d.T, I3) for u, g, d in zip(v["L3_cond_W_up"], v["L3_cond_W_gate"], v["L3_cond_W_down"])])
    w1 = _np.concatenate([v["L1_cond_As"].reshape(P, F).T, v["L1_cond_W_base"].T,
                          v["L1_cond_Bs"].transpose(0, 2, 1).reshape(P, F)], axis=1)
    rows = _np.zeros((2, 64, B), cond.dtype)
    rows[:, 0:KY] = _np.tile(cond.T, (KY // E, 1))
    arrays = {
        "constants": constants(),
        "cond": cond,
        "x_feature": x.transpose(2, 0, 1),
        "w_layer0": w0,
        "w_layer1": w1,
        "cond_er": _np.repeat(cond.T, R, axis=0),
        "b_layer1": v["L1_cond_b_base"].reshape(F, 1),
        "w_layer2": v["L2_cond_weight"].transpose(1, 0, 2),
        "mask": v["L2_cond_mask"],
        "cond_rows": rows.reshape(P, B),
        "b_layer2": v["L2_cond_bias"].reshape(F, 1),
        "w_layer3": w3,
        "b_layer3": _np.concatenate([_np.concatenate([v["L3_cond_b_up"], v["L3_cond_b_gate"]], axis=1).reshape(-1),
                                    v["L3_cond_b_down"].reshape(-1)]).reshape(P, E * B3 // P),
    }
    nc = _bacc.Bacc("TRN2", target_bir_lowering=False, num_devices=1)
    arrays = {"in_" + k: _np.ascontiguousarray(a) for k, a in arrays.items()}
    args = [nc.dram_tensor(k, a.shape, _mybir.dt.from_np(a.dtype), kind="ExternalInput").ap() for k, a in arrays.items()]
    args.append(nc.dram_tensor("out", (N3, S, F), _mybir.dt.float32, kind="ExternalOutput").ap())
    build(nc, *args)
    r = _run(nc, [arrays], core_ids=[0])
    return r.results[0]["out"][0:B]
```
